# Optimizing a Trainium2 kernel written in Bass

```python
import numpy as np
import jax
import jax.numpy as jnp

def _softmax(x, axis=-1):
    return jax.nn.softmax(x, axis=axis)

def _gelu(x):
    return jax.nn.gelu(x, approximate=True)

def _silu(x):
    return jax.nn.silu(x)

def _sigmoid(x):
    return jax.nn.sigmoid(x)

def _layernorm(x, axis=-1, eps=1e-05):
    m = jnp.mean(x, axis=axis, keepdims=True)
    v = jnp.var(x, axis=axis, keepdims=True)
    return (x - m) / jnp.sqrt(v + eps)

def _scatter_add(tgt, idx, src, axis=0):
    return tgt.at[idx].add(src)

def _segment_sum(src, seg, n):
    return jax.ops.segment_sum(src, seg, n)
kernel_name = 'mk_gnn_resnorm_d4_gnn_r32_1eed57'

def setup_inputs(seed: int=0):
    np.random.seed(seed)
    _w = jnp.asarray

    def _rec_inputs():
        import jax
        import jax.numpy as jnp
        _gk = jax.random.key(seed)
        x = -0.000202 + 1 * jax.random.normal(jax.random.fold_in(_gk, 1), (50000, 128), jnp.float32)
        _s = jax.random.randint(jax.random.fold_in(_gk, 2), (25000,), 0, 50000, jnp.int32)
        _d = jax.random.randint(jax.random.fold_in(_gk, 3), (25000,), 0, 50000, jnp.int32)
        _loop = jnp.arange(50000, dtype=jnp.int32)
        src = jnp.concatenate([_s, _d, _loop])
        dst = jnp.concatenate([_d, _s, _loop])
        _o = jnp.argsort(dst, stable=True)
        src = src[_o]
        dst = dst[_o]
        return (x, src, dst)
    x, src, dst = _rec_inputs()

    def _L0_gnn_setup():
        import jax, jax.numpy as jnp
        import numpy as np
        NUM_NODES = 50000
        IN_DIM = 128
        HIDDEN_DIM = 256
        NUM_EDGES = 25000

        def gcn_layer(x, edge_index, W, b, num_nodes):
            self_idx = jnp.arange(num_nodes, dtype=edge_index.dtype)
            src = jnp.concatenate([edge_index[0], self_idx])
            dst = jnp.concatenate([edge_index[1], self_idx])
            deg = jax.ops.segment_sum(jnp.ones_like(dst, dtype=x.dtype), dst, num_segments=num_nodes)
            dinv = jnp.where(deg > 0, jax.lax.rsqrt(deg), 0.0)
            norm = dinv[src] * dinv[dst]
            h = x @ W
            msg = h[src] * norm[:, None]
            out = jax.ops.segment_sum(msg, dst, num_segments=num_nodes)
            return out + b
        key = jax.random.key(seed)
        kx, ke, k1, k2, k3, k4 = jax.random.split(key, 6)
        x = jax.random.normal(kx, (NUM_NODES, IN_DIM), dtype=jnp.float32)
        edge_index = jax.random.randint(ke, (2, NUM_EDGES), 0, NUM_NODES, dtype=jnp.int64)
        s1 = 1.0 / np.sqrt(IN_DIM)
        s2 = 1.0 / np.sqrt(HIDDEN_DIM)
        W1 = jax.random.uniform(k1, (IN_DIM, HIDDEN_DIM), jnp.float32, -s1, s1)
        b1 = jnp.zeros((HIDDEN_DIM,), jnp.float32)
        W2 = jax.random.uniform(k2, (HIDDEN_DIM, IN_DIM), jnp.float32, -s2, s2)
        b2 = jnp.zeros((IN_DIM,), jnp.float32)
        return {'x': x, 'edge_index': edge_index, 'W1': W1, 'b1': b1, 'W2': W2, 'b2': b2}
    _L0_gnn_all = _L0_gnn_setup()
    _L0_gnn_in = {k: v for k, v in _L0_gnn_all.items() if k in ('W1', 'b1', 'W2', 'b2')}
    del _L0_gnn_all

    def _L1_gnn_setup():
        import jax, jax.numpy as jnp
        import numpy as np
        N_NODES = 50000
        N_EDGES = 25000
        D_IN, D_HID, D_OUT = (128, 256, 128)
        key = jax.random.key(seed)
        ks = jax.random.split(key, 12)
        s = lambda k, fi, fo: jax.random.normal(k, (fi, fo), jnp.float32) * (1.0 / np.sqrt(fi))
        return {'features': jax.random.normal(ks[0], (N_NODES, D_IN), jnp.float32), 'ws0': s(ks[1], D_IN, D_HID), 'wn0': s(ks[2], D_IN, D_HID), 'b0': jnp.zeros((D_HID,), jnp.float32), 'ws1': s(ks[3], D_HID, D_HID), 'wn1': s(ks[4], D_HID, D_HID), 'b1': jnp.zeros((D_HID,), jnp.float32), 'ws2': s(ks[5], D_HID, D_OUT), 'wn2': s(ks[6], D_HID, D_OUT), 'b2': jnp.zeros((D_OUT,), jnp.float32), 'src': jax.random.randint(ks[7], (N_EDGES,), 0, N_NODES, jnp.int32), 'dst': jax.random.randint(ks[8], (N_EDGES,), 0, N_NODES, jnp.int32)}
    _L1_gnn_all = _L1_gnn_setup()
    _L1_gnn_in = {k: v for k, v in _L1_gnn_all.items() if k in ('ws0', 'wn0', 'b0', 'ws1', 'wn1', 'b1', 'ws2', 'wn2', 'b2')}
    del _L1_gnn_all

    def _L2_gnn_setup():
        import jax, jax.numpy as jnp
        import numpy as np
        N_NODES = 50000
        N_EDGES = 25000
        DIM = 128
        BN_EPS = 1e-05
        key = jax.random.key(seed)
        ks = jax.random.split(key, 12)
        d = DIM
        s = 1.0 / np.sqrt(d)
        x = jax.random.normal(ks[0], (N_NODES, d), dtype=jnp.float32)
        edge_index = jax.random.randint(ks[1], (2, N_EDGES), 0, N_NODES, dtype=jnp.int64)
        W_msg = jax.random.uniform(ks[2], (d, d), jnp.float32, -s, s)
        b_msg = jax.random.uniform(ks[3], (d,), jnp.float32, -s, s)
        sa = 1.0 / np.sqrt(2 * d)
        W_att = jax.random.uniform(ks[4], (2 * d, 1), jnp.float32, -sa, sa)
        b_att = jax.random.uniform(ks[5], (1,), jnp.float32, -sa, sa)
        W_ih = jax.random.uniform(ks[6], (3 * d, d), jnp.float32, -s, s)
        b_ih = jax.random.uniform(ks[7], (3 * d,), jnp.float32, -s, s)
        W_hh = jax.random.uniform(ks[8], (3 * d, d), jnp.float32, -s, s)
        b_hh = jax.random.uniform(ks[9], (3 * d,), jnp.float32, -s, s)
        gamma = jnp.ones((d,), jnp.float32)
        beta = jnp.zeros((d,), jnp.float32)
        return {'x': x, 'edge_index': edge_index, 'W_msg': W_msg, 'b_msg': b_msg, 'W_att': W_att, 'b_att': b_att, 'W_ih': W_ih, 'b_ih': b_ih, 'W_hh': W_hh, 'b_hh': b_hh, 'gamma': gamma, 'beta': beta}
    _L2_gnn_all = _L2_gnn_setup()
    _L2_gnn_in = {k: v for k, v in _L2_gnn_all.items() if k in ('W_msg', 'b_msg', 'W_att', 'b_att', 'W_ih', 'b_ih', 'W_hh', 'b_hh', 'gamma', 'beta')}
    del _L2_gnn_all

    def _L3_gnn_setup():
        import jax, jax.numpy as jnp
        import numpy as np
        NUM_NODES = 3125
        NUM_EDGES = 50000
        IN_DIM = 128
        OUT_DIM = 128
        key = jax.random.key(seed)
        k_x, k_e, k_wn, k_bn, k_ws, k_bs = jax.random.split(key, 6)
        x = jax.random.normal(k_x, (NUM_NODES, IN_DIM), dtype=jnp.float32)
        edge_index = jax.random.randint(k_e, (2, NUM_EDGES), 0, NUM_NODES, dtype=jnp.int64)
        s = 1.0 / np.sqrt(IN_DIM)
        W_neigh = jax.random.uniform(k_wn, (OUT_DIM, IN_DIM), dtype=jnp.float32, minval=-s, maxval=s)
        b_neigh = jax.random.uniform(k_bn, (OUT_DIM,), dtype=jnp.float32, minval=-s, maxval=s)
        W_self = jax.random.uniform(k_ws, (OUT_DIM, IN_DIM), dtype=jnp.float32, minval=-s, maxval=s)
        b_self = jax.random.uniform(k_bs, (OUT_DIM,), dtype=jnp.float32, minval=-s, maxval=s)
        return {'x': x, 'edge_index': edge_index, 'W_neigh': W_neigh, 'b_neigh': b_neigh, 'W_self': W_self, 'b_self': b_self}
    _L3_gnn_all = _L3_gnn_setup()
    _L3_gnn_in = {k: v for k, v in _L3_gnn_all.items() if k in ('W_neigh', 'b_neigh', 'W_self', 'b_self')}
    del _L3_gnn_all
    return {'x': x, 'src': src, 'dst': dst, 'L0_gnn_W1': _L0_gnn_in['W1'], 'L0_gnn_b1': _L0_gnn_in['b1'], 'L0_gnn_W2': _L0_gnn_in['W2'], 'L0_gnn_b2': _L0_gnn_in['b2'], 'L1_gnn_ws0': _L1_gnn_in['ws0'], 'L1_gnn_wn0': _L1_gnn_in['wn0'], 'L1_gnn_b0': _L1_gnn_in['b0'], 'L1_gnn_ws1': _L1_gnn_in['ws1'], 'L1_gnn_wn1': _L1_gnn_in['wn1'], 'L1_gnn_b1': _L1_gnn_in['b1'], 'L1_gnn_ws2': _L1_gnn_in['ws2'], 'L1_gnn_wn2': _L1_gnn_in['wn2'], 'L1_gnn_b2': _L1_gnn_in['b2'], 'L2_gnn_W_msg': _L2_gnn_in['W_msg'], 'L2_gnn_b_msg': _L2_gnn_in['b_msg'], 'L2_gnn_W_att': _L2_gnn_in['W_att'], 'L2_gnn_b_att': _L2_gnn_in['b_att'], 'L2_gnn_W_ih': _L2_gnn_in['W_ih'], 'L2_gnn_b_ih': _L2_gnn_in['b_ih'], 'L2_gnn_W_hh': _L2_gnn_in['W_hh'], 'L2_gnn_b_hh': _L2_gnn_in['b_hh'], 'L2_gnn_gamma': _L2_gnn_in['gamma'], 'L2_gnn_beta': _L2_gnn_in['beta'], 'L3_gnn_W_neigh': _L3_gnn_in['W_neigh'], 'L3_gnn_b_neigh': _L3_gnn_in['b_neigh'], 'L3_gnn_W_self': _L3_gnn_in['W_self'], 'L3_gnn_b_self': _L3_gnn_in['b_self']}

def reference(x, src, dst, L0_gnn_W1, L0_gnn_b1, L0_gnn_W2, L0_gnn_b2, L1_gnn_ws0, L1_gnn_wn0, L1_gnn_b0, L1_gnn_ws1, L1_gnn_wn1, L1_gnn_b1, L1_gnn_ws2, L1_gnn_wn2, L1_gnn_b2, L2_gnn_W_msg, L2_gnn_b_msg, L2_gnn_W_att, L2_gnn_b_att, L2_gnn_W_ih, L2_gnn_b_ih, L2_gnn_W_hh, L2_gnn_b_hh, L2_gnn_gamma, L2_gnn_beta, L3_gnn_W_neigh, L3_gnn_b_neigh, L3_gnn_W_self, L3_gnn_b_self):
    import jax
    import jax.numpy as jnp

    def _L0_gnn_ref(x, edge_index, W1, b1, W2, b2):
        import jax, jax.numpy as jnp
        import numpy as np
        NUM_NODES = 50000
        IN_DIM = 128
        HIDDEN_DIM = 256
        NUM_EDGES = 25000

        def gcn_layer(x, edge_index, W, b, num_nodes):
            self_idx = jnp.arange(num_nodes, dtype=edge_index.dtype)
            src = jnp.concatenate([edge_index[0], self_idx])
            dst = jnp.concatenate([edge_index[1], self_idx])
            deg = jax.ops.segment_sum(jnp.ones_like(dst, dtype=x.dtype), dst, num_segments=num_nodes)
            dinv = jnp.where(deg > 0, jax.lax.rsqrt(deg), 0.0)
            norm = dinv[src] * dinv[dst]
            h = x @ W
            msg = h[src] * norm[:, None]
            out = jax.ops.segment_sum(msg, dst, num_segments=num_nodes)
            return out + b
        h = jax.nn.relu(gcn_layer(x, edge_index, W1, b1, NUM_NODES))
        out = gcn_layer(h, edge_index, W2, b2, NUM_NODES)
        return out

    def _L1_gnn_ref(features, ws0, wn0, b0, ws1, wn1, b1, ws2, wn2, b2, src, dst):
        import jax, jax.numpy as jnp
        import numpy as np
        N_NODES = 50000
        N_EDGES = 25000
        D_IN, D_HID, D_OUT = (128, 256, 128)
        n = features.shape[0]
        deg = jax.ops.segment_sum(jnp.ones_like(src, jnp.float32), dst, num_segments=n)
        inv_deg = jnp.where(deg > 0, 1.0 / jnp.maximum(deg, 1.0), 0.0)[:, None]

        def sage(h, w_self, w_neigh, b):
            agg = jax.ops.segment_sum(h[src], dst, num_segments=n) * inv_deg
            return h @ w_self + agg @ w_neigh + b
        h = jax.nn.relu(sage(features, ws0, wn0, b0))
        h = jax.nn.relu(sage(h, ws1, wn1, b1))
        h = sage(h, ws2, wn2, b2)
        return h

    def _L2_gnn_ref(x, edge_index, W_msg, b_msg, W_att, b_att, W_ih, b_ih, W_hh, b_hh, gamma, beta):
        import jax, jax.numpy as jnp
        import numpy as np
        N_NODES = 50000
        N_EDGES = 25000
        DIM = 128
        BN_EPS = 1e-05
        num_nodes, d = x.shape
        src = edge_index[0]
        dst = edge_index[1]
        xs = x[src]
        xd = x[dst]
        att = jax.nn.sigmoid(xs @ W_att[:d] + xd @ W_att[d:] + b_att)
        messages = (xs @ W_msg + b_msg) * att
        aggregated = jax.ops.segment_sum(messages, dst, num_segments=num_nodes)
        gi = aggregated @ W_ih.T + b_ih
        gh = x @ W_hh.T + b_hh
        i_r, i_z, i_n = jnp.split(gi, 3, axis=1)
        h_r, h_z, h_n = jnp.split(gh, 3, axis=1)
        r = jax.nn.sigmoid(i_r + h_r)
        z = jax.nn.sigmoid(i_z + h_z)
        n = jnp.tanh(i_n + r * h_n)
        h_new = (1.0 - z) * n + z * x
        mean = jnp.mean(h_new, axis=0)
        var = jnp.var(h_new, axis=0)
        return gamma * (h_new - mean) * jax.lax.rsqrt(var + BN_EPS) + beta

    def _L3_gnn_ref(x, edge_index, W_neigh, b_neigh, W_self, b_self):
        import jax, jax.numpy as jnp
        import numpy as np
        NUM_NODES = 3125
        NUM_EDGES = 50000
        IN_DIM = 128
        OUT_DIM = 128
        src, dst = (edge_index[0], edge_index[1])
        msgs = x[src]
        neigh = jax.ops.segment_sum(msgs, dst, num_segments=x.shape[0])
        neigh_proj = neigh @ W_neigh.T + b_neigh
        self_proj = x @ W_self.T + b_self
        return neigh_proj + self_proj
    edge_index = jnp.stack([src, dst])
    x = _layernorm(x + _L0_gnn_ref(x, edge_index, L0_gnn_W1, L0_gnn_b1, L0_gnn_W2, L0_gnn_b2), axis=-1)
    x = _layernorm(x + _L1_gnn_ref(x, L1_gnn_ws0, L1_gnn_wn0, L1_gnn_b0, L1_gnn_ws1, L1_gnn_wn1, L1_gnn_b1, L1_gnn_ws2, L1_gnn_wn2, L1_gnn_b2, src, dst), axis=-1)
    x = _layernorm(x + _L2_gnn_ref(x, edge_index, L2_gnn_W_msg, L2_gnn_b_msg, L2_gnn_W_att, L2_gnn_b_att, L2_gnn_W_ih, L2_gnn_b_ih, L2_gnn_W_hh, L2_gnn_b_hh, L2_gnn_gamma, L2_gnn_beta), axis=-1)
    x = _layernorm(x + _L3_gnn_ref(x, edge_index, L3_gnn_W_neigh, L3_gnn_b_neigh, L3_gnn_W_self, L3_gnn_b_self), axis=-1)
    return x

_drawn_inputs = setup_inputs


def setup_inputs(seed=0):
    import zlib

    import numpy as np

    out = dict(_drawn_inputs(seed))
    spreads = {'L0_gnn_b1': (0.0, 0.1),
     'L0_gnn_b2': (0.0, 0.1),
     'L1_gnn_b0': (0.0, 0.1),
     'L1_gnn_b1': (0.0, 0.1),
     'L1_gnn_b2': (0.0, 0.1),
     'L2_gnn_gamma': (1.0, 0.2),
     'L2_gnn_beta': (0.0, 0.1)}
    factors = {'L2_gnn_b_msg': 4.496, 'L2_gnn_b_ih': 4.172, 'L2_gnn_b_hh': 5.234}
    for name, (base, spread) in spreads.items():
        noise = np.random.default_rng([zlib.crc32(name.encode()), seed]).standard_normal(out[name].shape)
        drawn = base * np.exp(spread * noise) if base else spread * noise
        out[name] = jnp.asarray(drawn.astype(out[name].dtype))
    for name, factor in factors.items():
        out[name] = (out[name] * factor).astype(out[name].dtype)
    return out
```

```python
from contextlib import ExitStack

import concourse.bass as bass
from concourse import mybir

F32 = mybir.dt.float32
F32R = mybir.dt.float32r
I32 = mybir.dt.int32
U32 = mybir.dt.uint32
ALU = mybir.AluOpType
ACT = mybir.ActivationFunctionType
AX_X = mybir.AxisListType.X

P = 128
D = 128
HID = 256
NODES = 50000
EDGES = 100000
BLK = 4
GRP = BLK * P
T = -(-NODES // GRP)
NPAD = T * GRP
LAST = NODES - (T - 1) * GRP
LASTP = LAST // BLK
CH = 5
SLOTS = T * CH
EC = -(-EDGES // P)
TAIL = EDGES - (P - 1) * EC
SC = 23
NOWHERE = 1 << 20
PADV = 2000000
MW = D + 4
LN_EPS = 1e-5
BN_EPS = 1e-5
assert LAST % BLK == 0 and EC % (2 * SC) == 0 and P * SLOTS <= NOWHERE


def is_first(t):
    return isinstance(t, int) and t < 2


def wait_for(eng, sem, value):
    eng.wait_ge(sem, value)
    if not isinstance(value, int):
        eng.sem_inc(PASSED[0], 1)


PASSED = []


class Turn:

    def __init__(self, j, unroll, d):
        self.j, self.unroll, self.d = j, unroll, d
        self.t = d if j is None else j * unroll + d
        self.u = d % 2
        self.n = self.use(2)

    def use(self, slots):
        if self.j is None:
            return self.d // slots
        return self.j * (self.unroll // slots) + self.d // slots


def over_groups(eng, stages, unroll=2):
    lim = T - 2

    def step(s):
        for lag, stage in stages:
            if 0 <= s - lag < T:
                stage(Turn(None, unroll, s - lag))

    most = max(lag for lag, _ in stages)
    head = 2 + most
    head += (T - 2 - head) % unroll
    for s in range(head):
        step(s)
    with eng.Fori(0, (lim - head) // unroll) as j:
        for o in range(unroll):
            for lag, stage in stages:
                stage(Turn(j, unroll, head + o - lag))
    for s in range(lim, T + most):
        step(s)


def col(tile, i, n=1):
    return tile[:, bass.ds(i, n)]


def group_of(table, t, b=BLK):
    v = table.rearrange("(t p b) f -> t p (b f)", p=P, b=b)
    return v[bass.ds(t, 1)].rearrange("o p f -> (o p) f")


def slab_of(table, t):
    return table[bass.ds(t, 1)].rearrange("o p f -> (o p) f")


def build_program(nc, x, src, dst, w1, b1, w2, b2, ws0, wn0, sb0, ws1, wn1, sb1, ws2, wn2, sb2,
                  w_msg, b_msg, w_att, b_att, w_ihT, b_ih, w_hhT, b_hh, gamma, beta,
                  w_nT, b_n, w_sT, b_s, out):
    top = ExitStack()

    def sb(name, shape, dt=F32):
        return top.enter_context(nc.sbuf_tensor(name, shape, dt))

    def dram(name, shape, dt=F32):
        return nc.dram_tensor(name, shape, dt, kind="Internal").ap()

    PASSED[:] = [top.enter_context(nc.semaphore("waits_passed"))]

    t_x0 = dram("t_x0", (2 * NPAD, D))
    t_h0 = dram("t_h0", (2 * NPAD, D))
    t_x1 = dram("t_x1", (2 * NPAD, D))
    t_h = dram("t_h", (2 * NPAD, HID))
    t_v = dram("t_v", (2 * NPAD, D))
    t_m = dram("t_m", (2 * NPAD, MW))
    t_x3 = dram("t_x3", (2 * NPAD, D))
    r1 = dram("r1", (NPAD, D))
    r2 = dram("r2", (NPAD, D))
    x2t = dram("x2t", (T, P, GRP))
    hnt = dram("hnt", (T, P, GRP))
    slots_d = dram("slots_d", (P * SLOTS, 2))
    deg_d = dram("deg_d", (T, GRP))
    dinv_d = dram("dinv_d", (T, GRP))
    inv_d = dram("inv_d", (T, GRP))

    idx = sb("idx", [P, SLOTS], U32)
    dcol = sb("dcol", [P, SLOTS])
    dinv_n = sb("dinv_n", [P, T * BLK])
    dinv2_n = sb("dinv2_n", [P, T * BLK])
    inv_n = sb("inv_n", [P, T * BLK])
    selfinv_n = sb("selfinv_n", [P, T * BLK])
    iota = sb("iota", [P, GRP])
    ident = sb("ident", [P, P])
    own = sb("own", [P, 1])
    own1 = sb("own1", [P, 1])
    id_own1 = sb("id_own1", [P, P])
    id_own_r = sb("id_own_r", [P, P], F32R)
    bn_acc = sb("bn_acc", [P, T + BLK - 1, 6])
    bn_mv = sb("bn_mv", [P, 2])
    bn_a = sb("bn_a", [P, 1])
    bn_c = sb("bn_c", [P, 1])

    w1_s = sb("w1_s", [P, HID])
    w2_s = sb("w2_s", [P, 2, D])
    b1_c = sb("b1_c", [P, 2])
    b2_r = sb("b2_r", [P, BLK, D])
    ws0_s = sb("ws0_s", [P, HID])
    wn0_s = sb("wn0_s", [P, HID])
    sb0_r = sb("sb0_r", [P, 2, HID])
    ws1_s = sb("ws1_s", [P, 2, HID])
    wn1_s = sb("wn1_s", [P, 2, HID])
    sb1_c = sb("sb1_c", [P, 2])
    wuv_s = sb("wuv_s", [P, 2, HID])
    sb2_r = sb("sb2_r", [P, BLK, D])
    wm_s = sb("wm_s", [P, MW])
    bm_r = sb("bm_r", [P, 2, MW])
    wad_s = sb("wad_s", [P, P])
    wih_s = sb("wih_s", [P, 3 * D])
    whh_s = sb("whh_s", [P, 3 * D])
    bih_c = sb("bih_c", [P, 3])
    bhh_c = sb("bhh_c", [P, 3])
    brz_c = sb("brz_c", [P, 2])
    gam_c = sb("gam_c", [P, 1])
    bet_c = sb("bet_c", [P, 1])
    wn_s = sb("wn_s", [P, D])
    wsx_s = sb("wsx_s", [P, D])
    b3_r = sb("b3_r", [P, BLK, D])
    b3b_r = sb("b3b_r", [P, BLK, D])

    bank = [top.enter_context(nc.psum_tensor(f"bank{i}", [P, 512], F32)) for i in range(8)]

    class Phase:

        def __init__(self, ctx, name):
            self.ctx, self.name, self.own_sems = ctx, name, []
            ctx.callback(self.clear)

        def clear(self):
            nc.clear_and_free_semaphores(self.own_sems)
            nc.all_engine_barrier()

        def tile(self, name, shape, dt=F32):
            return self.ctx.enter_context(nc.sbuf_tensor(f"{self.name}_{name}", shape, dt))

        def pair(self, name, shape, dt=F32, n=2):
            return [self.tile(f"{name}{u}", shape, dt) for u in range(n)]

        def sem(self, name):
            self.own_sems.append(nc.alloc_semaphore(f"{self.name}_{name}"))
            return self.own_sems[-1]

        def sems(self, name, n=2):
            return [self.sem(f"{name}{u}") for u in range(n)]

    def load_weights():
        with ExitStack() as ctx:
            ph = Phase(ctx, "w")
            got, cleared = ph.sem("loaded"), ph.sem("cleared")
            block = ctx.enter_context(nc.Block())

            def row(a, n):
                return a.rearrange("(o n) -> o n", o=1).broadcast_to([P, n])

            def column(a, k):
                return a.rearrange("(k p) -> p k", p=P)

            loads = [
                (w1_s[:, :], w1), (w2_s[:, :, :], w2.rearrange("(k p) f -> p k f", p=P)),
                (ws0_s[:, :], ws0), (wn0_s[:, :], wn0),
                (ws1_s[:, :, :], ws1.rearrange("(k p) f -> p k f", p=P)),
                (wn1_s[:, :, :], wn1.rearrange("(k p) f -> p k f", p=P)),
                (wuv_s[:, :, 0:D], ws2.rearrange("(k p) f -> p k f", p=P)),
                (wuv_s[:, :, D:HID], wn2.rearrange("(k p) f -> p k f", p=P)),
                (wm_s[:, 0:D], w_msg), (wm_s[:, D:D + 1], w_att[0:D, :]),
                (wm_s[:, D + 1:D + 2], w_att[D:2 * D, :]),
                (wih_s[:, :], w_ihT), (whh_s[:, :], w_hhT), (wn_s[:, :], w_nT), (wsx_s[:, :], w_sT),
                (b1_c[:, :], column(b1, 2)), (sb1_c[:, :], column(sb1, 2)),
                (bih_c[:, :], column(b_ih, 3)), (bhh_c[:, :], column(b_hh, 3)),
                (gam_c[:, :], column(gamma, 1)), (bet_c[:, :], column(beta, 1)),
            ]
            for k in range(BLK):
                loads += [(b2_r[:, k, :], row(b2, D)), (sb2_r[:, k, :], row(sb2, D)),
                          (b3_r[:, k, :], row(b_n, D)), (b3b_r[:, k, :], row(b_s, D))]
            for k in range(2):
                loads += [(sb0_r[:, k, :], row(sb0, HID)), (bm_r[:, k, 0:D], row(b_msg, D)),
                          (bm_r[:, k, D:D + 1], row(b_att, 1))]

            @block.vector
            def _(dve):
                dve.memset(wm_s[:, :], 0.0)
                dve.memset(bm_r[:, :, :], 0.0).then_inc(cleared, 1)

            @block.sync
            def _(sp):
                sp.wait_ge(cleared, 1)
                for to, what in loads:
                    sp.dma_start(to, what, allow_slow_non_contiguous=True).then_inc(got, 16)
                sp.wait_ge(got, 16 * len(loads))

    def sort_edges():
        with ExitStack() as ctx:
            ph = Phase(ctx, "so")
            tmp, sem = ph.tile, ph.sem

            si = tmp("src_i", [P, EC], I32)
            di = tmp("dst_i", [P, EC], I32)
            ni = tmp("next_i", [P, EC], I32)
            ei = tmp("edge_i", [P, EC], I32)
            q1 = tmp("int_1", [P, EC], I32)
            q2 = tmp("int_2", [P, EC], I32)
            ef = tmp("edge_f", [P, EC])
            ends = tmp("ends_f", [P, EC])
            a = tmp("scratch_a", [P, EC])
            b = tmp("scratch_b", [P, EC])
            c = tmp("scratch_c", [P, EC])
            df = tmp("dst_f", [P, EC])
            nf = tmp("next_f", [P, EC])
            base = tmp("base_f", [P, EC + 1])
            pos = tmp("slot_row", [P, EC], U32)
            pair = tmp("slot_pair", [P, EC, 2])
            posb = tmp("slot_row_now", [P, 2, SC], U32)
            pairb = tmp("slot_pair_now", [P, 2, SC, 2])
            rowmax = tmp("rowmax", [P, 1])
            carry = tmp("carry", [P, 1])
            rows = tmp("rows", [1, P + 1])
            empty = tmp("empty_slots", [P, SLOTS, 2])
            back = tmp("slots_back", [P, SLOTS, 2])
            cnt = tmp("counts", [P, 4])
            ones = tmp("ones", [P, P])
            idxi = tmp("iota_i", [P, GRP], I32)

            made = sem("patterns_made")
            padded = sem("edges_padded")
            got = sem("edges_loaded")
            chain = sem("edge_steps")
            turned = sem("carry_turned")
            blank = sem("slots_blanked")
            ready = sem("turn_ready")
            sent = [sem("turn_sent_0"), sem("turn_sent_1")]
            read = sem("slots_read")
            block = ctx.enter_context(nc.Block())

            @block.gpsimd
            def _(pool):
                pool.iota(ei[:, :], pattern=[[1, EC]], base=0, channel_multiplier=EC).then_inc(made, 1)
                pool.iota(idxi[:, :], pattern=[[1, GRP]], base=0, channel_multiplier=0).then_inc(made, 1)
                pool.memset(ident[:, :], 0.0).then_inc(made, 1)
                pool.memset(empty[:, :, 0], float(NOWHERE)).then_inc(made, 1)
                pool.memset(empty[:, :, 1], -1.0).then_inc(made, 1)
                pool.wait_ge(made, 5)
                pool.affine_select(out=ident[:, :], in_=ident[:, :], compare_op=ALU.not_equal, fill=1.0,
                                   base=0, pattern=[[-1, P]], channel_multiplier=1).then_inc(made, 1)
                pool.wait_ge(blank, 16)

                def send(n, u):
                    wait_for(pool, ready, n * 2 + (u + 1))
                    for k in range(SC):
                        pool.indirect_dma_start(
                            out=slots_d, out_offset=bass.IndirectOffsetOnAxis(ap=posb[:, u, k:k + 1], axis=0),
                            in_=pairb[:, u, k, :], in_offset=None,
                            bounds_check=P * SLOTS - 1, oob_is_err=False).then_inc(sent[u], 16)

                with pool.Fori(0, EC // (2 * SC)) as j:
                    send(j, 0)
                    send(j, 1)

            @block.sync
            def _(sp):
                sp.wait_ge(made, 6)
                sp.dma_start(slots_d.rearrange("(p s) f -> p (s f)", p=P),
                             empty[:, :, :].rearrange("p s f -> p (s f)")).then_inc(blank, 16)
                sp.wait_ge(padded, 2)
                full = (P - 1) * EC
                for tile, a, off in ((si, src, 0), (di, dst, 0), (ni, dst, 1)):
                    sp.dma_start(tile[0:P - 1, :], a[off:off + full].rearrange("(p c) -> p c", p=P - 1))\
                      .then_inc(got, 16)
                    sp.dma_start(tile[P - 1:P, 0:TAIL - off],
                                 a[off + full:EDGES].rearrange("(o c) -> o c", o=1)).then_inc(got, 16)
                for u in range(2):
                    sp.wait_ge(sent[u], EC // 2 * 16)
                sp.dma_start(back[:, :, :].rearrange("p s f -> p (s f)"),
                             slots_d.rearrange("(p s) f -> p (s f)", p=P)).then_inc(read, 16)

            @block.tensor
            def _(pe):
                pe.wait_ge(turned, 1)
                pe.transpose(bank[0][0:1, 0:P], rowmax[:, :], ident[:, :]).then_inc(turned, 1)
                pe.wait_ge(turned, 3)
                pe.matmul(bank[1][:, 0:1], rows[0:1, 0:P], ones[0:1, 0:1], start=True, stop=True)\
                  .then_inc(turned, 1)

            @block.vector
            def _(dve):
                steps = [0]

                def then(ins):
                    steps[0] += 1
                    ins.then_inc(chain, 1)
                    dve.wait_ge(chain, steps[0])

                dve.memset(si[:, :], 0).then_inc(padded, 1)
                dve.memset(di[:, :], PADV)
                dve.memset(ni[:, :], PADV).then_inc(padded, 1)
                dve.memset(own[:, :], 1.0)
                then(dve.memset(ones[:, :], 1.0))
                dve.wait_ge(made, 6)
                dve.tensor_copy(iota[:, :], idxi[:, :])
                dve.tensor_copy(ef[:, :], ei[:, :])
                dve.wait_ge(got, 96)
                dve.tensor_copy(df[:, :], di[:, :])
                then(dve.tensor_copy(nf[:, :], ni[:, :]))
                then(dve.tensor_tensor(ends[:, :], df[:, :], nf[:, :], ALU.not_equal))
                dve.tensor_scalar(q1[:, :], di[:, :], 9, None, ALU.logical_shift_right)
                then(dve.tensor_scalar(q2[:, :], ni[:, :], 9, None, ALU.logical_shift_right))
                dve.tensor_copy(a[:, :], q1[:, :])
                then(dve.tensor_copy(b[:, :], q2[:, :]))
                then(dve.tensor_tensor(b[:, :], a[:, :], b[:, :], ALU.not_equal))
                then(dve.scalar_tensor_tensor(out=c[:, :], in0=ef[:, :], scalar=1.0, in1=b[:, :],
                                              op0=ALU.add, op1=ALU.mult))
                dve.tensor_reduce(rowmax[:, :], c[:, :], AX_X, ALU.max).then_inc(turned, 1)
                then(dve.memset(rows[:, :], 0.0))
                dve.wait_ge(turned, 2)
                dve.tensor_tensor_scan(rows[0:1, 1:P + 1], bank[0][0:1, 0:P], rows[0:1, 1:P + 1], 0.0,
                                       ALU.max, ALU.max).then_inc(turned, 1)
                dve.wait_ge(turned, 4)
                then(dve.tensor_copy(carry[:, :], bank[1][:, 0:1]))
                dve.tensor_copy(base[:, 0:1], carry[:, :])
                then(dve.tensor_tensor_scan(base[:, 1:EC + 1], c[:, :], c[:, :], carry[:, 0:1],
                                            ALU.max, ALU.max))
                then(dve.tensor_scalar(q2[:, :], di[:, :], GRP - 1, None, ALU.bitwise_and))
                then(dve.tensor_copy(b[:, :], q2[:, :]))
                dve.tensor_scalar(ni[:, :], q2[:, :], 3, 7, ALU.bitwise_and, ALU.logical_shift_left)
                then(dve.tensor_scalar(q2[:, :], q2[:, :], 2, None, ALU.logical_shift_right))
                then(dve.tensor_tensor(q2[:, :], q2[:, :], ni[:, :], ALU.bitwise_or))
                dve.tensor_copy(pair[:, :, 1], q2[:, :])
                dve.tensor_copy(pair[:, :, 0], si[:, :])
                then(dve.tensor_tensor(c[:, :], ef[:, :], base[:, 0:EC], ALU.subtract))
                then(dve.tensor_tensor(c[:, :], c[:, :], b[:, :], ALU.subtract))
                then(dve.tensor_scalar(c[:, :], c[:, :], 0.0, float(CH * P - 1), ALU.max, ALU.min))
                then(dve.tensor_copy(q1[:, :], c[:, :]))
                dve.tensor_scalar(q2[:, :], q1[:, :], P - 1, None, ALU.bitwise_and)
                then(dve.tensor_scalar(q1[:, :], q1[:, :], 7, None, ALU.logical_shift_right))
                dve.tensor_copy(b[:, :], q2[:, :])
                then(dve.tensor_copy(c[:, :], q1[:, :]))
                then(dve.scalar_tensor_tensor(out=c[:, :], in0=a[:, :], scalar=float(CH), in1=c[:, :],
                                              op0=ALU.mult, op1=ALU.add))
                then(dve.scalar_tensor_tensor(out=c[:, :], in0=b[:, :], scalar=float(SLOTS), in1=c[:, :],
                                              op0=ALU.mult, op1=ALU.add))
                dve.tensor_scalar(b[:, :], df[:, :], float(NODES), None, ALU.is_ge)
                then(dve.tensor_scalar(c[:, :], c[:, :], float(P * SLOTS - 1), None, ALU.min))
                then(dve.tensor_tensor(b[:, :], b[:, :], ends[:, :], ALU.max))
                then(dve.scalar_tensor_tensor(out=c[:, :], in0=b[:, :], scalar=float(NOWHERE), in1=c[:, :],
                                              op0=ALU.mult, op1=ALU.add))
                then(dve.tensor_copy(pos[:, :], c[:, :]))

                def give(n, u, first):
                    if not first:
                        wait_for(dve, sent[u], n * (16 * SC))
                    at = n * (2 * SC) + u * SC
                    dve.tensor_copy(pairb[:, u, :, :], pair[:, bass.ds(at, SC), :])
                    dve.tensor_copy(posb[:, u, :], pos[:, bass.ds(at, SC)]).then_inc(ready, 1)

                give(0, 0, True)
                give(0, 1, True)
                with dve.Fori(1, EC // (2 * SC)) as j:
                    give(j, 0, False)
                    give(j, 1, False)
                dve.wait_ge(read, 16)
                dve.tensor_copy(idx[:, :], back[:, :, 0])
                dve.tensor_copy(dcol[:, :], back[:, :, 1])
                dve.tensor_scalar(own1[:, :], own[:, :], 1.0, None, ALU.add).then_inc(turned, 1)
                dve.wait_ge(turned, 5)
                dve.tensor_scalar(id_own1[:, :], ident[:, :], own1[:, 0:1], None, ALU.mult)
                dve.tensor_scalar(id_own_r[:, :], ident[:, :], own[:, 0:1], None, ALU.mult)


    class EdgeRows:

        def __init__(self, ph, table, width, parts):
            self.table, self.width = table, width
            self.rows = ph.pair("rows", [P, CH, width])
            self.hi = ph.pair("hi", [P, parts, min(width, HID) if width != MW else D], F32R)
            self.lo = ph.pair("lo", [P, parts, min(width, HID) if width != MW else D], F32R)
            self.onehot = ph.pair("onehot", [P, CH, GRP], F32R)
            self.index = ph.pair("index", [P, CH], U32)
            self.cleared = ph.sem("rows_cleared")
            self.indexed = ph.sem("index_copied")
            self.gathered = ph.sems("rows_gathered")
            self.split = ph.sem("rows_hi")
            self.ready = ph.sem("rows_ready")
            self.summed = ph.sem("rows_summed")

        def gather(self, pool, q, used=None):
            if isinstance(q.t, int) and q.t < 2:
                pool.memset(self.rows[q.u][:, :, :], 0.0).then_inc(self.cleared, 1)
            else:
                wait_for(pool, used or self.ready, q.t - 1)
            pool.tensor_copy(self.index[q.u][:, :], col(idx, q.t * CH, CH)).then_inc(self.indexed, 1)
            if isinstance(q.t, int) and q.t < 2:
                pool.wait_ge(self.cleared, q.t + 1)
            wait_for(pool, self.indexed, q.t + 1)
            for k in range(CH):
                pool.indirect_dma_start(
                    out=self.rows[q.u][:, k, :], out_offset=None, in_=self.table[0:NPAD, :],
                    in_offset=bass.IndirectOffsetOnAxis(ap=self.index[q.u][:, k:k + 1], axis=0),
                    bounds_check=NPAD - 1, oob_is_err=False).then_inc(self.gathered[q.u], 16)

        def arrived(self, eng, q):
            eng.wait_ge(self.gathered[q.u], (q.n + 1) * (16 * CH))

        def free(self, eng, q):
            if not is_first(q.t):
                eng.wait_ge(self.summed, q.t - 1)

        def take_hi(self, act, q):
            self.arrived(act, q)
            self.free(act, q)
            act.activation(self.hi[q.u][:, :, :], self.rows[q.u][:, :, :], ACT.Copy).then_inc(self.split, 1)

        def make_onehots(self, dve, q):
            self.free(dve, q)
            for k in range(CH):
                last = dve.tensor_scalar(self.onehot[q.u][:, k, :], iota[:, :],
                                         col(dcol, q.t * CH + k), None, ALU.is_equal)
            return last

        def take_lo(self, dve, q):
            dve.wait_ge(self.split, q.t + 1)
            dve.tensor_tensor(self.lo[q.u][:, :, :], self.rows[q.u][:, :, :],
                              self.hi[q.u][:, :, :].bitcast(F32), ALU.subtract).then_inc(self.ready, 1)

        def prepare(self, dve, q):
            self.make_onehots(dve, q)
            self.take_lo(dve, q)

        def sum_by_feature(self, pe, q, banks, close=True):
            for h, to in enumerate(banks):
                for k in range(CH):
                    for part in (self.hi, self.lo):
                        last = pe.matmul(to[:, :], part[q.u][:, k, h * P:(h + 1) * P],
                                         self.onehot[q.u][:, k, :], start=(k == 0 and part is self.hi),
                                         stop=(close and k == CH - 1 and part is self.lo),
                                         skip_group_check=True)
            return last

        def sum_by_node(self, pe, q, to):
            for b in range(BLK):
                for k in range(CH):
                    for part in (self.hi, self.lo):
                        last = pe.matmul(to[:, b * P:(b + 1) * P],
                                         self.onehot[q.u][:, k, b * P:(b + 1) * P], part[q.u][:, k, :],
                                         start=(k == 0 and part is self.hi),
                                         stop=(k == CH - 1 and part is self.lo), skip_group_check=True)
            return last

    class LayerNorm:

        def __init__(self, ph):
            self.stats = ph.pair("ln_stats", [P, BLK, 6])
            self.mv = ph.pair("ln_mv", [P, BLK, 2])
            self.var = ph.pair("ln_var", [P, BLK])
            self.std = ph.pair("ln_std", [P, BLK])
            self.rstd = ph.pair("ln_rstd", [P, BLK])
            self.shift = ph.pair("ln_shift", [P, BLK])
            self.link = ph.sem("ln_link")
            self.link2 = ph.sem("ln_link2")
            self.varied = ph.sem("ln_varied")
            self.rooted = ph.sem("ln_rooted")
            self.scaled = ph.sem("ln_scaled")
            self.applied = ph.sem("ln_applied")

        def take_stats(self, dve, q, z):
            for b in range(BLK):
                last = dve.bn_stats(self.stats[q.u][:, b, :], z[:, b * D:(b + 1) * D])
            last.then_inc(self.link, 1)
            wait_for(dve, self.link, q.t * 2 + 1)
            for b in range(BLK):
                last = dve.bn_aggr(self.mv[q.u][:, b, :], self.stats[q.u][:, b, :])
            last.then_inc(self.link, 1)
            dve.wait_ge(self.link, q.t * 2 + 2)
            dve.tensor_scalar(self.var[q.u][:, :], self.mv[q.u][:, :, 1], LN_EPS, None, ALU.add)\
               .then_inc(self.varied, 1)

        def root(self, act, q):
            act.wait_ge(self.varied, q.t + 1)
            act.activation(self.std[q.u][:, :], self.var[q.u][:, :], ACT.Sqrt).then_inc(self.rooted, 1)

        def invert(self, dve, q):
            dve.wait_ge(self.rooted, q.t + 1)
            dve.reciprocal(self.rstd[q.u][:, :], self.std[q.u][:, :]).then_inc(self.link2, 1)
            dve.wait_ge(self.link2, q.t + 1)
            dve.scalar_tensor_tensor(out=self.shift[q.u][:, :], in0=self.mv[q.u][:, :, 0], scalar=-1.0,
                                     in1=self.rstd[q.u][:, :], op0=ALU.mult, op1=ALU.mult)\
               .then_inc(self.scaled, 1)

        def normalise(self, act, q, to, z):
            act.wait_ge(self.scaled, q.t + 1)
            for b in range(BLK):
                last = act.activation(to[:, b * D:(b + 1) * D], z[:, b * D:(b + 1) * D], ACT.Identity,
                                      bias=self.shift[q.u][:, b:b + 1], scale=self.rstd[q.u][:, b:b + 1])
            last.then_inc(self.applied, 1)

    def load(sp, q, to, what, loaded, free=None, slots=2):
        if free is not None and not (isinstance(q.t, int) and q.t < slots):
            wait_for(sp, free, q.t - (slots - 1))
        sp.dma_start(to, what).then_inc(loaded, 16)

    def store(sp, q, to, what, made, stored):
        wait_for(sp, made, q.t + 1)
        sp.dma_start(to, what).then_inc(stored[q.u], 16)

    def all_stored(sp, *stored):
        for pair in stored:
            for u, sem in enumerate(pair):
                sp.wait_ge(sem, 16 * ((T + 1 - u) // 2))

    def row_of(a, t):
        return a[bass.ds(t, 1), :].broadcast_to([P, GRP])

    def count_degrees():
        with ExitStack() as ctx:
            ph = Phase(ctx, "deg")
            onehot = ph.pair("onehot", [P, CH, GRP], F32R)
            ones = ph.tile("ones", [P, P], F32R)
            row = ph.pair("row", [1, GRP])
            begun, made, counted = ph.sem("begun"), ph.sem("onehots"), ph.sem("counted")
            copied, stored = ph.sem("copied"), ph.sems("stored")
            block = ctx.enter_context(nc.Block())

            @block.vector
            def _(dve):
                dve.tensor_scalar(ones[:, :], iota[:, 0:P], 0.0, 1.0, ALU.mult, ALU.add).then_inc(begun, 1)

                def onehots(q):
                    if not is_first(q.t):
                        dve.wait_ge(counted, q.t - 1)
                    for k in range(CH):
                        last = dve.tensor_scalar(onehot[q.u][:, k, :], iota[:, :],
                                                 col(dcol, q.t * CH + k), None, ALU.is_equal)
                    last.then_inc(made, 1)

                over_groups(dve, [(0, onehots)])

            @block.tensor
            def _(pe):
                pe.wait_ge(begun, 1)

                def count(q):
                    pe.wait_ge(made, q.t + 1)
                    if not is_first(q.t):
                        pe.wait_ge(copied, q.t - 1)
                    for k in range(CH):
                        last = pe.matmul(bank[q.u][:, :], ones[:, :], onehot[q.u][:, k, :],
                                         start=(k == 0), stop=(k == CH - 1))
                    last.then_inc(counted, 1)

                over_groups(pe, [(0, count)])

            @block.scalar
            def _(act):
                def add_own(q):
                    act.wait_ge(counted, q.t + 1)
                    if not is_first(q.t):
                        act.wait_ge(stored[q.u], q.n * 16)
                    act.activation(row[q.u][0:1, :], bank[q.u][0:1, :], ACT.Identity, bias=own[0:1, 0:1])\
                       .then_inc(copied, 1)

                over_groups(act, [(0, add_own)])

            @block.sync
            def _(sp):
                over_groups(sp, [(0, lambda q: store(sp, q, deg_d[bass.ds(q.t, 1), :], row[q.u][0:1, :],
                                                     copied, stored))])
                all_stored(sp, stored)

    def scale_degrees():
        with ExitStack() as ctx:
            ph = Phase(ctx, "scl")
            deg = ph.tile("deg", [T, GRP])
            a = ph.tile("a", [T, GRP])
            b = ph.tile("b", [T, GRP])
            root = ph.tile("root", [T, GRP])
            got, rooted, made = ph.sem("got"), ph.sem("rooted"), ph.sem("made")
            turned, kept, link = ph.sem("turned"), ph.sem("kept"), ph.sem("link")
            block = ctx.enter_context(nc.Block())

            @block.sync
            def _(sp):
                sp.dma_start(deg[:, :], deg_d).then_inc(got, 16)
                sp.wait_ge(made, 2)
                sp.dma_start(dinv_d, root[:, :]).then_inc(kept, 16)
                sp.dma_start(inv_d, b[:, :]).then_inc(kept, 16)
                sp.wait_ge(kept, 32)

            @block.scalar
            def _(act):
                act.wait_ge(rooted, 1)
                act.activation(root[:, :], a[:, :], ACT.Sqrt).then_inc(rooted, 1)

            @block.tensor
            def _(pe):
                pe.wait_ge(made, 2)
                for i, tile in enumerate((root, b)):
                    for k in range(BLK):
                        last = pe.transpose(bank[i * BLK + k][:, 0:T], tile[:, k * P:(k + 1) * P],
                                            ident[0:T, 0:T])
                last.then_inc(turned, 1)

            @block.vector
            def _(dve):
                steps = [0]

                def then(ins):
                    steps[0] += 1
                    ins.then_inc(link, 1)
                    dve.wait_ge(link, steps[0])

                dve.wait_ge(got, 16)
                dve.tensor_scalar(a[:, :], deg[:, :], 1.0, None, ALU.add).then_inc(rooted, 1)
                then(dve.tensor_scalar(b[:, :], deg[:, :], 1.0, None, ALU.max))
                then(dve.reciprocal(b[:, :], b[:, :]))
                then(dve.scalar_tensor_tensor(out=b[:, :], in0=deg[:, :], scalar=0.0, in1=b[:, :],
                                              op0=ALU.is_gt, op1=ALU.mult))
                dve.wait_ge(rooted, 2)
                then(dve.reciprocal(root[:, :], root[:, :]))
                dve.memset(bn_mv[:, :], 0.0).then_inc(made, 2)
                dve.wait_ge(turned, 1)
                for i, tile in enumerate((dinv_n, inv_n)):
                    for k in range(BLK):
                        dve.tensor_copy(tile[:, :].rearrange("p (t b) -> p t b", b=BLK)[:, :, k],
                                        bank[i * BLK + k][:, 0:T])
                then(dve.memset(bn_mv[:, :], 0.0))
                dve.tensor_scalar(dinv2_n[:, :], dinv_n[:, :], own1[:, 0:1], None, ALU.mult)
                dve.tensor_scalar(selfinv_n[:, :], inv_n[:, :], own[:, 0:1], None, ALU.mult)

    def scale_x():
        with ExitStack() as ctx:
            ph = Phase(ctx, "sx")
            xin, xout = ph.pair("in", [P, GRP]), ph.pair("out", [P, GRP])
            loaded, scaled, stored = ph.sems("loaded"), ph.sem("scaled"), ph.sems("stored")
            block = ctx.enter_context(nc.Block())

            @block.sync
            def _(sp):
                over_groups(sp, [(0, lambda q: load_x(sp, q, xin, loaded, scaled)),
                                 (1, lambda q: store(sp, q, group_of(t_x0[0:NPAD, :], q.t), xout[q.u][:, :],
                                                     scaled, stored))])
                all_stored(sp, stored)

            @block.scalar
            def _(act):
                def scale(q):
                    act.wait_ge(loaded[q.u], q.n * 16 + 16)
                    if not is_first(q.t):
                        act.wait_ge(stored[q.u], q.n * 16)
                    for b in range(BLK):
                        last = act.activation(xout[q.u][:, b * D:(b + 1) * D], xin[q.u][:, b * D:(b + 1) * D],
                                              ACT.Copy, scale=col(dinv_n, q.t * BLK + b))
                    last.then_inc(scaled, 1)

                over_groups(act, [(0, scale)])

    def load_x(sp, q, to, loaded, free):
        if isinstance(q.t, int) and q.t == T - 1:
            load(sp, q, to[q.u][0:LASTP, :],
                 x[(T - 1) * GRP:NODES, :].rearrange("(p b) f -> p (b f)", b=BLK), loaded[q.u], free)
        else:
            load(sp, q, to[q.u][:, :], group_of(x[0:(T - 1) * GRP, :], q.t), loaded[q.u], free)

    def gcn_first():
        with ExitStack() as ctx:
            ph = Phase(ctx, "g1")
            e = EdgeRows(ph, t_x0, D, CH)
            own_rows, xin = ph.pair("own", [P, GRP]), ph.pair("x", [P, GRP])
            scale_row = ph.pair("scale", [P, GRP])
            agg = ph.pair("agg", [P, GRP])
            hid = ph.pair("hid", [P, 2, GRP])
            hout, rout = ph.pair("hout", [P, GRP]), ph.pair("rout", [P, GRP])
            loaded, loaded_x = ph.sems("loaded"), ph.sems("loaded_x")
            agged, relued, scaled, rested = ph.sem("agged"), ph.sem("relued"), ph.sem("scaled"), ph.sem("rested")
            hidden, lowered, link = ph.sem("hidden"), ph.sem("lowered"), ph.sem("link")
            st_h, st_r = ph.sems("stored_h"), ph.sems("stored_r")
            block = ctx.enter_context(nc.Block())

            @block.gpsimd
            def _(pool):
                over_groups(pool, [(0, lambda q: e.gather(pool, q))])

            @block.sync
            def _(sp):
                def loads(q):
                    load(sp, q, own_rows[q.u][:, :], group_of(t_x0[0:NPAD, :], q.t), loaded[q.u], e.summed)
                    load(sp, q, scale_row[q.u][:, :], row_of(dinv_d, q.t), loaded[q.u], agged)

                over_groups(sp, [
                    (0, loads),
                    (2, lambda q: load_x(sp, q, xin, loaded_x, rested)),
                    (3, lambda q: store(sp, q, group_of(t_h0[0:NPAD, :], q.t), hout[q.u][:, :], scaled, st_h)),
                    (3, lambda q: store(sp, q, group_of(r1, q.t), rout[q.u][:, :], rested, st_r))])
                all_stored(sp, st_h, st_r)

            @block.tensor
            def _(pe):
                def sums(q):
                    pe.wait_ge(e.ready, q.t + 1)
                    pe.wait_ge(loaded[q.u], q.n * 32 + 32)
                    if not is_first(q.t):
                        pe.wait_ge(agged, q.t - 1)
                    e.sum_by_feature(pe, q, [bank[q.u]], close=False)
                    for b in range(BLK):
                        last = pe.matmul(bank[q.u][:, b * P:(b + 1) * P], own_rows[q.u][:, b * D:(b + 1) * D],
                                         id_own1[:, :], start=False, stop=(b == BLK - 1),
                                         skip_group_check=True)
                    last.then_inc(e.summed, 1)

                def up(q):
                    pe.wait_ge(agged, q.t + 1)
                    if not (isinstance(q.t, int) and q.t < 1):
                        pe.wait_ge(relued, q.t)
                    for h in range(2):
                        last = pe.matmul(bank[2 + h][:, :], w1_s[:, h * P:(h + 1) * P], agg[q.u][:, :],
                                         start=True, stop=True)
                    last.then_inc(hidden, 1)

                def down(q):
                    pe.wait_ge(relued, q.t + 1)
                    if not is_first(q.t):
                        pe.wait_ge(scaled, q.t - 1)
                    for b in range(BLK):
                        for h in range(2):
                            last = pe.matmul(bank[4 + q.u][:, b * D:(b + 1) * D],
                                             hid[q.u][:, h, b * P:(b + 1) * P], w2_s[:, h, :],
                                             start=(h == 0), stop=(h == 1), skip_group_check=True)
                    last.then_inc(lowered, 1)

                over_groups(pe, [(1, sums), (2, up), (3, down)])

            @block.scalar
            def _(act):
                def relu(q):
                    act.wait_ge(hidden, q.t + 1)
                    if not is_first(q.t):
                        act.wait_ge(lowered, q.t - 1)
                    for h in range(2):
                        last = act.activation(hid[q.u][:, h, :], bank[2 + h][:, :], ACT.Relu,
                                              bias=b1_c[:, h:h + 1])
                    last.then_inc(relued, 1)

                def scale(q):
                    act.wait_ge(lowered, q.t + 1)
                    if not is_first(q.t):
                        act.wait_ge(st_h[q.u], q.n * 16)
                        act.wait_ge(rested, q.t - 1)
                    for b in range(BLK):
                        last = act.activation(hout[q.u][:, b * D:(b + 1) * D],
                                              bank[4 + q.u][:, b * D:(b + 1) * D], ACT.Copy,
                                              scale=col(dinv_n, q.t * BLK + b))
                    last.then_inc(scaled, 1)

                over_groups(act, [(0, lambda q: e.take_hi(act, q)), (2, relu), (3, scale)])

            @block.vector
            def _(dve):
                def scale_sums(q):
                    dve.wait_ge(e.summed, q.t + 1)
                    if not is_first(q.t):
                        dve.wait_ge(hidden, q.t - 1)
                    dve.tensor_tensor(agg[q.u][:, :], bank[q.u][:, :], scale_row[q.u][:, :], ALU.mult)\
                       .then_inc(agged, 1)

                def rest(q):
                    dve.wait_ge(scaled, q.t + 1)
                    dve.wait_ge(loaded_x[q.u], q.n * 16 + 16)
                    if not is_first(q.t):
                        dve.wait_ge(st_r[q.u], q.n * 16)
                    for b in range(BLK):
                        f = slice(b * D, (b + 1) * D)
                        last = dve.scalar_tensor_tensor(out=rout[q.u][:, f], in0=hout[q.u][:, f],
                                                        scalar=col(dinv2_n, q.t * BLK + b),
                                                        in1=xin[q.u][:, f], op0=ALU.mult, op1=ALU.add)
                    last.then_inc(link, 1)
                    dve.wait_ge(link, q.t + 1)
                    dve.tensor_tensor(rout[q.u][:, :], rout[q.u][:, :],
                                      b2_r[:, :, :].rearrange("p b f -> p (b f)"), ALU.add)\
                       .then_inc(rested, 1)

                over_groups(dve, [(0, lambda q: e.prepare(dve, q)), (1, scale_sums), (3, rest)])

    def gcn_second():
        with ExitStack() as ctx:
            ph = Phase(ctx, "g2")
            e = EdgeRows(ph, t_h0, D, CH)
            ln = LayerNorm(ph)
            rest, z, xout = ph.pair("rest", [P, GRP]), ph.pair("z", [P, GRP]), ph.pair("xout", [P, GRP])
            loaded, added, stored = ph.sems("loaded"), ph.sem("added"), ph.sems("stored")
            block = ctx.enter_context(nc.Block())

            @block.gpsimd
            def _(pool):
                over_groups(pool, [(0, lambda q: e.gather(pool, q))])

            @block.sync
            def _(sp):
                over_groups(sp, [
                    (0, lambda q: load(sp, q, rest[q.u][:, :], group_of(r1, q.t), loaded[q.u], added)),
                    (3, lambda q: store(sp, q, group_of(t_x1[0:NPAD, :], q.t), xout[q.u][:, :], ln.applied,
                                        stored))])
                all_stored(sp, stored)

            @block.tensor
            def _(pe):
                def sums(q):
                    pe.wait_ge(e.ready, q.t + 1)
                    if not is_first(q.t):
                        pe.wait_ge(added, q.t - 1)
                    e.sum_by_node(pe, q, bank[q.u]).then_inc(e.summed, 1)

                over_groups(pe, [(1, sums)])

            @block.scalar
            def _(act):
                def apply(q):
                    if not is_first(q.t):
                        act.wait_ge(stored[q.u], q.n * 16)
                    ln.normalise(act, q, xout[q.u], z[q.u])

                over_groups(act, [(0, lambda q: e.take_hi(act, q)), (1, lambda q: ln.root(act, q)),
                                  (2, apply)])

            @block.vector
            def _(dve):
                def add(q):
                    dve.wait_ge(e.summed, q.t + 1)
                    dve.wait_ge(loaded[q.u], q.n * 16 + 16)
                    if not is_first(q.t):
                        dve.wait_ge(ln.applied, q.t - 1)
                    for b in range(BLK):
                        f = slice(b * D, (b + 1) * D)
                        last = dve.scalar_tensor_tensor(out=z[q.u][:, f], in0=bank[q.u][:, f],
                                                        scalar=col(dinv_n, q.t * BLK + b),
                                                        in1=rest[q.u][:, f], op0=ALU.mult, op1=ALU.add)
                    last.then_inc(added, 1)
                    dve.wait_ge(added, q.t + 1)
                    ln.take_stats(dve, q, z[q.u])

                over_groups(dve, [(0, lambda q: e.prepare(dve, q)), (1, add), (2, lambda q: ln.invert(dve, q))])

    def sage_first():
        with ExitStack() as ctx:
            ph = Phase(ctx, "s1")
            e = EdgeRows(ph, t_x1, D, CH)
            own_rows, scale_row = ph.pair("own", [P, GRP]), ph.pair("scale", [P, GRP])
            xt, agg = ph.pair("xt", [P, GRP]), ph.pair("agg", [P, GRP])
            pre, hout = ph.pair("pre", [P, BLK * HID]), ph.pair("hout", [P, BLK * HID])
            loaded, turned, agged, link = ph.sems("loaded"), ph.sem("turned"), ph.sem("agged"), ph.sem("link")
            hidden, biased, relued, stored = ph.sem("hidden"), ph.sem("biased"), ph.sem("relued"), ph.sems("stored")
            block = ctx.enter_context(nc.Block())

            @block.gpsimd
            def _(pool):
                over_groups(pool, [(0, lambda q: e.gather(pool, q))])

            @block.sync
            def _(sp):
                def loads(q):
                    load(sp, q, own_rows[q.u][:, :], group_of(t_x1[0:NPAD, :], q.t), loaded[q.u], e.summed)
                    load(sp, q, scale_row[q.u][:, :], row_of(inv_d, q.t), loaded[q.u], agged)

                over_groups(sp, [
                    (0, loads),
                    (3, lambda q: store(sp, q, group_of(t_h[0:NPAD, :], q.t), hout[q.u][:, :], relued, stored))])
                all_stored(sp, stored)

            @block.tensor
            def _(pe):
                def sums(q):
                    pe.wait_ge(e.ready, q.t + 1)
                    pe.wait_ge(loaded[q.u], q.n * 32 + 32)
                    if not is_first(q.t):
                        pe.wait_ge(agged, q.t - 1)
                    e.sum_by_feature(pe, q, [bank[q.u]])
                    for b in range(BLK):
                        last = pe.transpose(bank[2 + q.u][:, b * P:(b + 1) * P],
                                            own_rows[q.u][:, b * D:(b + 1) * D], ident[:, :])
                    last.then_inc(e.summed, 1)

                def dense(q):
                    pe.wait_ge(agged, q.t + 1)
                    if not (isinstance(q.t, int) and q.t < 1):
                        pe.wait_ge(biased, q.t)
                    for b in range(BLK):
                        to = bank[4 + b // 2][:, (b % 2) * HID:(b % 2 + 1) * HID]
                        pe.matmul(to, xt[q.u][:, b * P:(b + 1) * P], ws0_s[:, :], start=True, stop=False,
                                  skip_group_check=True)
                        last = pe.matmul(to, agg[q.u][:, b * P:(b + 1) * P], wn0_s[:, :], start=False,
                                         stop=True, skip_group_check=True)
                    last.then_inc(hidden, 1)

                over_groups(pe, [(1, sums), (2, dense)])

            @block.scalar
            def _(act):
                def turn(q):
                    act.wait_ge(e.summed, q.t + 1)
                    if not is_first(q.t):
                        act.wait_ge(hidden, q.t - 1)
                    act.activation(xt[q.u][:, :], bank[2 + q.u][:, :], ACT.Copy).then_inc(turned, 1)

                def relu(q):
                    act.wait_ge(biased, q.t + 1)
                    if not is_first(q.t):
                        act.wait_ge(stored[q.u], q.n * 16)
                    act.activation(hout[q.u][:, :], pre[q.u][:, :], ACT.Relu).then_inc(relued, 1)

                over_groups(act, [(0, lambda q: e.take_hi(act, q)), (1, turn), (2, relu)])

            @block.vector
            def _(dve):
                def mean(q):
                    dve.wait_ge(turned, q.t + 1)
                    dve.scalar_tensor_tensor(out=agg[q.u][:, :], in0=xt[q.u][:, :], scalar=own[:, 0:1],
                                             in1=bank[q.u][:, :], op0=ALU.mult, op1=ALU.add)\
                       .then_inc(link, 1)
                    dve.wait_ge(link, q.t + 1)
                    dve.tensor_tensor(agg[q.u][:, :], agg[q.u][:, :], scale_row[q.u][:, :], ALU.mult)\
                       .then_inc(agged, 1)

                def bias(q):
                    dve.wait_ge(hidden, q.t + 1)
                    if not is_first(q.t):
                        dve.wait_ge(relued, q.t - 1)
                    for i in range(2):
                        last = dve.tensor_tensor(pre[q.u][:, i * 512:(i + 1) * 512], bank[4 + i][:, :],
                                                 sb0_r[:, :, :].rearrange("p b f -> p (b f)"), ALU.add)
                    last.then_inc(biased, 1)

                over_groups(dve, [(0, lambda q: e.prepare(dve, q)), (1, mean), (2, bias)])

    def sage_second():
        with ExitStack() as ctx:
            ph = Phase(ctx, "s2")
            e = EdgeRows(ph, t_h, HID, CH)
            own_rows, scale_row = ph.pair("own", [P, BLK * HID]), ph.pair("scale", [P, GRP])
            xin = ph.pair("x", [P, GRP])
            ht, agg = ph.pair("ht", [P, 2, GRP]), ph.pair("agg", [P, 2, GRP])
            hid = ph.pair("hid", [P, 2, GRP])
            vout, rout = ph.pair("vout", [P, GRP]), ph.pair("rout", [P, GRP])
            loaded, loaded_x = ph.sems("loaded"), ph.sems("loaded_x")
            turned, agged, link, link2 = ph.sem("turned"), ph.sem("agged"), ph.sem("link"), ph.sem("link2")
            hidden, relued, lowered = ph.sem("hidden"), ph.sem("relued"), ph.sem("lowered")
            kept, added, rested = ph.sem("kept"), ph.sem("added"), ph.sem("rested")
            st_v, st_r = ph.sems("stored_v"), ph.sems("stored_r")
            block = ctx.enter_context(nc.Block())

            @block.gpsimd
            def _(pool):
                over_groups(pool, [(0, lambda q: e.gather(pool, q))])

            @block.sync
            def _(sp):
                def loads(q):
                    load(sp, q, own_rows[q.u][:, :], group_of(t_h[0:NPAD, :], q.t), loaded[q.u], e.summed)
                    load(sp, q, scale_row[q.u][:, :], row_of(inv_d, q.t), loaded[q.u], agged)

                over_groups(sp, [
                    (0, loads),
                    (2, lambda q: load(sp, q, xin[q.u][:, :], group_of(t_x1[0:NPAD, :], q.t), loaded_x[q.u],
                                       rested)),
                    (3, lambda q: store(sp, q, group_of(t_v[0:NPAD, :], q.t), vout[q.u][:, :], kept, st_v)),
                    (3, lambda q: store(sp, q, group_of(r2, q.t), rout[q.u][:, :], rested, st_r))])
                all_stored(sp, st_v, st_r)

            @block.tensor
            def _(pe):
                def sums(q):
                    pe.wait_ge(e.ready, q.t + 1)
                    pe.wait_ge(loaded[q.u], q.n * 32 + 32)
                    if not (isinstance(q.t, int) and q.t < 1):
                        pe.wait_ge(agged, q.t)
                    e.sum_by_feature(pe, q, [bank[0], bank[1]])
                    for h in range(2):
                        for b in range(BLK):
                            last = pe.transpose(bank[2 + h][:, b * P:(b + 1) * P],
                                                own_rows[q.u][:, b * HID + h * P:b * HID + (h + 1) * P],
                                                ident[:, :])
                    last.then_inc(e.summed, 1)

                def across(q):
                    pe.wait_ge(agged, q.t + 1)
                    if not (isinstance(q.t, int) and q.t < 1):
                        pe.wait_ge(relued, q.t)
                    for o in range(2):
                        for k, (w, r) in enumerate(((ws1_s, ht), (wn1_s, agg))):
                            for h in range(2):
                                last = pe.matmul(bank[4 + o][:, :], w[:, h, o * P:(o + 1) * P], r[q.u][:, h, :],
                                                 start=(k + h == 0), stop=(k + h == 2))
                    last.then_inc(hidden, 1)

                def down(q):
                    pe.wait_ge(relued, q.t + 1)
                    if not (isinstance(q.t, int) and q.t < 1):
                        pe.wait_ge(kept, q.t)
                        pe.wait_ge(added, q.t)
                    for w in range(2):
                        for b in range(BLK):
                            for h in range(2):
                                last = pe.matmul(bank[6 + w][:, b * D:(b + 1) * D],
                                                 hid[q.u][:, h, b * P:(b + 1) * P],
                                                 wuv_s[:, h, w * D:(w + 1) * D],
                                                 start=(h == 0), stop=(h == 1), skip_group_check=True)
                    last.then_inc(lowered, 1)

                over_groups(pe, [(1, sums), (2, across), (3, down)])

            @block.scalar
            def _(act):
                def turn(q):
                    act.wait_ge(e.summed, q.t + 1)
                    if not is_first(q.t):
                        act.wait_ge(hidden, q.t - 1)
                    for h in range(2):
                        last = act.activation(ht[q.u][:, h, :], bank[2 + h][:, :], ACT.Copy)
                    last.then_inc(turned, 1)

                def relu(q):
                    act.wait_ge(hidden, q.t + 1)
                    if not is_first(q.t):
                        act.wait_ge(lowered, q.t - 1)
                    for h in range(2):
                        last = act.activation(hid[q.u][:, h, :], bank[4 + h][:, :], ACT.Relu,
                                              bias=sb1_c[:, h:h + 1])
                    last.then_inc(relued, 1)

                def keep(q):
                    act.wait_ge(lowered, q.t + 1)
                    if not is_first(q.t):
                        act.wait_ge(st_v[q.u], q.n * 16)
                        act.wait_ge(rested, q.t - 1)
                    act.activation(vout[q.u][:, :], bank[7][:, :], ACT.Copy).then_inc(kept, 1)

                over_groups(act, [(0, lambda q: e.take_hi(act, q)), (1, turn), (2, relu), (3, keep)])

            @block.vector
            def _(dve):
                def mean(q):
                    dve.wait_ge(turned, q.t + 1)
                    for h in range(2):
                        last = dve.scalar_tensor_tensor(out=agg[q.u][:, h, :], in0=ht[q.u][:, h, :],
                                                        scalar=own[:, 0:1], in1=bank[h][:, :],
                                                        op0=ALU.mult, op1=ALU.add)
                    last.then_inc(link, 1)
                    dve.wait_ge(link, q.t + 1)
                    for h in range(2):
                        last = dve.tensor_tensor(agg[q.u][:, h, :], agg[q.u][:, h, :], scale_row[q.u][:, :],
                                                 ALU.mult)
                    last.then_inc(agged, 1)

                def rest(q):
                    dve.wait_ge(lowered, q.t + 1)
                    dve.wait_ge(loaded_x[q.u], q.n * 16 + 16)
                    if not is_first(q.t):
                        dve.wait_ge(st_r[q.u], q.n * 16)
                    dve.tensor_tensor(rout[q.u][:, :], bank[6][:, :], xin[q.u][:, :], ALU.add)\
                       .then_inc(added, 1)
                    dve.wait_ge(added, q.t + 1)
                    dve.tensor_tensor(rout[q.u][:, :], rout[q.u][:, :],
                                      sb2_r[:, :, :].rearrange("p b f -> p (b f)"), ALU.add)\
                       .then_inc(link2, 1)
                    dve.wait_ge(link2, q.t + 1)
                    dve.wait_ge(kept, q.t + 1)
                    for b in range(BLK):
                        f = slice(b * D, (b + 1) * D)
                        last = dve.scalar_tensor_tensor(out=rout[q.u][:, f], in0=vout[q.u][:, f],
                                                        scalar=col(selfinv_n, q.t * BLK + b),
                                                        in1=rout[q.u][:, f], op0=ALU.mult, op1=ALU.add)
                    last.then_inc(rested, 1)

                over_groups(dve, [(0, lambda q: e.prepare(dve, q)), (1, mean), (3, rest)])

    def sage_third():
        with ExitStack() as ctx:
            ph = Phase(ctx, "s3")
            e = EdgeRows(ph, t_v, D, CH)
            ln = LayerNorm(ph)
            rest, z, x2 = ph.pair("rest", [P, GRP]), ph.pair("z", [P, GRP]), ph.pair("x2", [P, GRP])
            xt, mout = ph.pair("xt", [P, GRP]), ph.pair("mout", [P, BLK * MW])
            loaded, added, turned = ph.sems("loaded"), ph.sem("added"), ph.sem("turned")
            held, timed, biased = ph.sem("held"), ph.sem("timed"), ph.sem("biased")
            st_x, st_m = ph.sems("stored_x"), ph.sems("stored_m")
            block = ctx.enter_context(nc.Block())

            @block.gpsimd
            def _(pool):
                over_groups(pool, [(0, lambda q: e.gather(pool, q))])

            @block.sync
            def _(sp):
                over_groups(sp, [
                    (0, lambda q: load(sp, q, rest[q.u][:, :], group_of(r2, q.t), loaded[q.u], added)),
                    (4, lambda q: store(sp, q, slab_of(x2t, q.t), xt[q.u][:, :], held, st_x)),
                    (4, lambda q: store(sp, q, group_of(t_m[0:NPAD, :], q.t), mout[q.u][:, :], biased, st_m))])
                all_stored(sp, st_x, st_m)

            @block.tensor
            def _(pe):
                def sums(q):
                    pe.wait_ge(e.ready, q.t + 1)
                    if not is_first(q.t):
                        pe.wait_ge(added, q.t - 1)
                    e.sum_by_node(pe, q, bank[q.u]).then_inc(e.summed, 1)

                def turn(q):
                    pe.wait_ge(ln.applied, q.t + 1)
                    if not is_first(q.t):
                        pe.wait_ge(held, q.t - 1)
                    for b in range(BLK):
                        last = pe.transpose(bank[2 + q.u][:, b * P:(b + 1) * P],
                                            x2[q.u][:, b * D:(b + 1) * D], ident[:, :])
                    last.then_inc(turned, 1)

                def message(q):
                    pe.wait_ge(held, q.t + 1)
                    if not is_first(q.t):
                        pe.wait_ge(biased, q.t - 1)
                    for b in range(BLK):
                        last = pe.matmul(bank[4 + 2 * q.u + b // 2][:, (b % 2) * MW:(b % 2 + 1) * MW],
                                         xt[q.u][:, b * P:(b + 1) * P], wm_s[:, :], start=True, stop=True,
                                         skip_group_check=True)
                    last.then_inc(timed, 1)

                over_groups(pe, [(1, sums), (3, turn), (4, message)])

            @block.scalar
            def _(act):
                def apply(q):
                    if not is_first(q.t):
                        act.wait_ge(turned, q.t - 1)
                    ln.normalise(act, q, x2[q.u], z[q.u])

                def hold(q):
                    act.wait_ge(turned, q.t + 1)
                    if not is_first(q.t):
                        act.wait_ge(st_x[q.u], q.n * 16)
                        act.wait_ge(timed, q.t - 1)
                    act.activation(xt[q.u][:, :], bank[2 + q.u][:, :], ACT.Copy).then_inc(held, 1)

                over_groups(act, [(0, lambda q: e.take_hi(act, q)), (1, lambda q: ln.root(act, q)),
                                  (2, apply), (3, hold)])

            @block.vector
            def _(dve):
                def add(q):
                    dve.wait_ge(e.summed, q.t + 1)
                    dve.wait_ge(loaded[q.u], q.n * 16 + 16)
                    if not is_first(q.t):
                        dve.wait_ge(ln.applied, q.t - 1)
                    for b in range(BLK):
                        f = slice(b * D, (b + 1) * D)
                        last = dve.scalar_tensor_tensor(out=z[q.u][:, f], in0=bank[q.u][:, f],
                                                        scalar=col(inv_n, q.t * BLK + b),
                                                        in1=rest[q.u][:, f], op0=ALU.mult, op1=ALU.add)
                    last.then_inc(added, 1)
                    dve.wait_ge(added, q.t + 1)
                    ln.take_stats(dve, q, z[q.u])

                def bias(q):
                    dve.wait_ge(timed, q.t + 1)
                    if not is_first(q.t):
                        dve.wait_ge(st_m[q.u], q.n * 16)
                    for i in range(2):
                        last = dve.tensor_tensor(mout[q.u][:, i * 2 * MW:(i + 1) * 2 * MW],
                                                 bank[4 + 2 * q.u + i][:, 0:2 * MW],
                                                 bm_r[:, :, :].rearrange("p b f -> p (b f)"), ALU.add)
                    last.then_inc(biased, 1)

                over_groups(dve, [(0, lambda q: e.prepare(dve, q)), (1, add),
                                  (2, lambda q: ln.invert(dve, q)), (4, bias)])

    def attend():
        XS = 4
        with ExitStack() as ctx:
            ph = Phase(ctx, "at")
            e = EdgeRows(ph, t_m, MW, CH + BLK)
            x2 = ph.pair("x2", [P, GRP], n=XS)
            own_rows = ph.pair("own", [P, BLK * MW])
            scrap = ph.tile("scrap", [P, CH, GRP])
            term = ph.pair("term", [P, CH])
            logit, att = ph.pair("logit", [P, CH + BLK]), ph.pair("att", [P, CH + BLK])
            msg = ph.pair("msg", [P, CH + BLK, D])
            agg = ph.pair("agg", [P, GRP])
            r, zg, mix, ng = (ph.pair(n, [P, GRP]) for n in ("r", "z", "mix", "n"))
            hn = ph.pair("hn", [P, GRP])
            loaded_x, loaded_m = ph.sems("loaded_x", XS), ph.sems("loaded_m")
            asked, dotted, linked, weighed = ph.sem("asked"), ph.sem("dotted"), ph.sem("linked"), ph.sem("weighed")
            gated, mailed, agged = ph.sem("gated"), ph.sem("mailed"), ph.sem("agged")
            crossed, opened, mixed, tanhed = ph.sem("crossed"), ph.sem("opened"), ph.sem("mixed"), ph.sem("tanhed")
            link, link3, moved = ph.sem("link"), ph.sem("link3"), ph.sem("moved")
            stored = ph.sems("stored")
            block = ctx.enter_context(nc.Block())

            @block.gpsimd
            def _(pool):
                over_groups(pool, [(0, lambda q: e.gather(pool, q, used=mailed))], XS)

            @block.sync
            def _(sp):
                def loads(q):
                    v = q.use(XS)
                    s = q.d % XS
                    load(sp, q, x2[s][:, :], slab_of(x2t, q.t), loaded_x[s], moved, XS)
                    load(sp, q, own_rows[q.u][:, :], group_of(t_m[0:NPAD, :], q.t), loaded_m[q.u], mailed)

                over_groups(sp, [(0, loads),
                                 (3, lambda q: store(sp, q, slab_of(hnt, q.t), hn[q.u][:, :], moved, stored))],
                            XS)
                all_stored(sp, stored)

            @block.tensor
            def _(pe):
                def ask(q):
                    pe.wait_ge(loaded_x[q.d % XS], q.use(XS) * 16 + 16)
                    if not (isinstance(q.t, int) and q.t < 1):
                        pe.wait_ge(dotted, q.t)
                    pe.matmul(bank[2][:, :], wad_s[:, :], x2[q.d % XS][:, :], start=True, stop=True)\
                      .then_inc(asked, 1)

                def sums(q):
                    pe.wait_ge(e.ready, q.t + 1)
                    if not is_first(q.t):
                        pe.wait_ge(agged, q.t - 1)
                    e.sum_by_feature(pe, q, [bank[q.u]], close=False)
                    for b in range(BLK):
                        for part in (e.hi, e.lo):
                            last = pe.matmul(bank[q.u][:, b * P:(b + 1) * P], part[q.u][:, CH + b, :],
                                             id_own_r[:, :], start=False, skip_group_check=True,
                                             stop=(b == BLK - 1 and part is e.lo))
                    last.then_inc(e.summed, 1)

                def gates(q):
                    pe.wait_ge(agged, q.t + 1)
                    if not (isinstance(q.t, int) and q.t < 1):
                        pe.wait_ge(opened, q.t)
                        pe.wait_ge(mixed, q.t)
                    xq = x2[q.d % XS]
                    for g in range(2):
                        f = slice(g * P, (g + 1) * P)
                        pe.matmul(bank[3 + g][:, :], wih_s[:, f], agg[q.u][:, :], start=True, stop=False)
                        pe.matmul(bank[3 + g][:, :], whh_s[:, f], xq[:, :], start=False, stop=True)
                    f = slice(2 * P, 3 * P)
                    pe.matmul(bank[5][:, :], whh_s[:, f], xq[:, :], start=True, stop=True)
                    pe.matmul(bank[6][:, :], wih_s[:, f], agg[q.u][:, :], start=True, stop=True)\
                      .then_inc(crossed, 1)

                over_groups(pe, [(0, ask), (1, sums), (2, gates)], XS)

            @block.scalar
            def _(act):
                def weigh(q):
                    act.wait_ge(gated, q.t + 1)
                    act.activation(att[q.u][:, :], logit[q.u][:, :], ACT.Sigmoid).then_inc(weighed, 1)
                    act.wait_ge(weighed, q.t + 1)
                    if not is_first(q.t):
                        act.wait_ge(e.ready, q.t - 1)
                    for k in range(CH):
                        act.activation(msg[q.u][:, k, :], e.rows[q.u][:, k, 0:D], ACT.Copy,
                                       scale=att[q.u][:, k:k + 1])
                    for b in range(BLK):
                        last = act.activation(msg[q.u][:, CH + b, :], own_rows[q.u][:, b * MW:b * MW + D],
                                              ACT.Copy, scale=att[q.u][:, CH + b:CH + b + 1])
                    last.then_inc(mailed, 1)
                    act.wait_ge(mailed, q.t + 1)
                    e.free(act, q)
                    act.activation(e.hi[q.u][:, :, :], msg[q.u][:, :, :], ACT.Copy).then_inc(e.split, 1)

                def hold(q):
                    act.wait_ge(e.summed, q.t + 1)
                    if not is_first(q.t):
                        act.wait_ge(crossed, q.t - 1)
                    act.activation(agg[q.u][:, :], bank[q.u][:, :], ACT.Copy).then_inc(agged, 1)

                def gate(q):
                    act.wait_ge(crossed, q.t + 1)
                    if not is_first(q.t):
                        act.wait_ge(moved, q.t - 1)
                    act.activation(r[q.u][:, :], bank[3][:, :], ACT.Sigmoid, bias=brz_c[:, 0:1])
                    act.activation(zg[q.u][:, :], bank[4][:, :], ACT.Sigmoid, bias=brz_c[:, 1:2])\
                       .then_inc(opened, 1)

                def candidate(q):
                    act.wait_ge(mixed, q.t + 1)
                    act.activation(ng[q.u][:, :], mix[q.u][:, :], ACT.Tanh, bias=bih_c[:, 2:3])\
                       .then_inc(tanhed, 1)

                over_groups(act, [(0, weigh), (1, hold), (2, gate), (2, candidate)], XS)

            @block.vector
            def _(dve):
                def low(q):
                    dve.wait_ge(e.split, q.t + 1)
                    dve.tensor_tensor(e.lo[q.u][:, :, :], msg[q.u][:, :, :],
                                      e.hi[q.u][:, :, :].bitcast(F32), ALU.subtract).then_inc(e.ready, 1)

                def look(q):
                    e.make_onehots(dve, q).then_inc(linked, 1)
                    dve.wait_ge(linked, q.t + 1)
                    dve.wait_ge(asked, q.t + 1)
                    for k in range(CH):
                        last = dve.tensor_tensor_reduce(scrap[:, k, :], e.onehot[q.u][:, k, :].bitcast(F32),
                                                        bank[2][:, :], 1.0, 0.0, ALU.mult, ALU.add,
                                                        term[q.u][:, k:k + 1])
                    last.then_inc(dotted, 1)
                    dve.wait_ge(dotted, q.t + 1)
                    e.arrived(dve, q)
                    dve.wait_ge(loaded_m[q.u], q.n * 16 + 16)
                    if not is_first(q.t):
                        dve.wait_ge(weighed, q.t - 1)
                    dve.tensor_tensor(logit[q.u][:, 0:CH], term[q.u][:, :], e.rows[q.u][:, :, D], ALU.add)
                    mine = own_rows[q.u][:, :].rearrange("p (b f) -> p b f", b=BLK)
                    dve.tensor_tensor(logit[q.u][:, CH:CH + BLK], mine[:, :, D], mine[:, :, D + 1], ALU.add)\
                       .then_inc(gated, 1)

                def blend(q):
                    dve.wait_ge(opened, q.t + 1)
                    dve.scalar_tensor_tensor(out=mix[q.u][:, :], in0=bank[5][:, :], scalar=bhh_c[:, 2:3],
                                             in1=r[q.u][:, :], op0=ALU.add, op1=ALU.mult).then_inc(link, 1)
                    dve.wait_ge(link, q.t + 1)
                    dve.tensor_tensor(mix[q.u][:, :], mix[q.u][:, :], bank[6][:, :], ALU.add)\
                       .then_inc(mixed, 1)

                def move(q):
                    dve.wait_ge(tanhed, q.t + 1)
                    if not is_first(q.t):
                        dve.wait_ge(stored[q.u], q.n * 16)
                    dve.tensor_tensor(hn[q.u][:, :], x2[q.d % XS][:, :], ng[q.u][:, :], ALU.subtract)\
                       .then_inc(link3, 1)
                    dve.wait_ge(link3, q.t * 2 + 1)
                    dve.tensor_tensor(hn[q.u][:, :], hn[q.u][:, :], zg[q.u][:, :], ALU.mult)\
                       .then_inc(link3, 1)
                    dve.wait_ge(link3, q.t * 2 + 2)
                    dve.tensor_tensor(hn[q.u][:, :], hn[q.u][:, :], ng[q.u][:, :], ALU.add)\
                       .then_inc(moved, 1)
                    dve.wait_ge(moved, q.t + 1)
                    if isinstance(q.t, int) and q.t == T - 1:
                        for b in range(BLK):
                            dve.bn_stats(bn_acc[:, T - 1 + b, :], hn[q.u][:, b * P:b * P + LASTP])
                    else:
                        dve.bn_stats(bn_acc[:, bass.ds(q.t, 1), :].rearrange("p o s -> p (o s)"),
                                     hn[q.u][:, :])

                over_groups(dve, [(1, low), (0, look), (2, blend), (3, move)], XS)

    def batch_constants():
        with ExitStack() as ctx:
            ph = Phase(ctx, "bc")
            link, rooted = ph.sem("link"), ph.sem("rooted")
            block = ctx.enter_context(nc.Block())

            @block.scalar
            def _(act):
                act.wait_ge(link, 2)
                act.activation(bn_c[:, :], bn_mv[:, 1:2], ACT.Sqrt).then_inc(rooted, 1)

            @block.vector
            def _(dve):
                dve.bn_aggr(bn_mv[:, :], bn_acc[:, :, :].rearrange("p t s -> p (t s)")).then_inc(link, 1)
                dve.wait_ge(link, 1)
                dve.tensor_scalar(bn_mv[:, 1:2], bn_mv[:, 1:2], BN_EPS, None, ALU.add).then_inc(link, 1)
                dve.wait_ge(rooted, 1)
                dve.reciprocal(bn_a[:, :], bn_c[:, :]).then_inc(link, 1)
                dve.wait_ge(link, 3)
                dve.tensor_tensor(bn_a[:, :], bn_a[:, :], gam_c[:, :], ALU.mult).then_inc(link, 1)
                dve.wait_ge(link, 4)
                dve.tensor_tensor(bn_c[:, :], bn_mv[:, 0:1], bn_a[:, :], ALU.mult).then_inc(link, 1)
                dve.wait_ge(link, 5)
                dve.tensor_tensor(bn_c[:, :], bet_c[:, :], bn_c[:, :], ALU.subtract)

    def batch_normed():
        with ExitStack() as ctx:
            ph = Phase(ctx, "bn")
            ln = LayerNorm(ph)
            hin, xin = ph.pair("h", [P, GRP]), ph.pair("x", [P, GRP])
            y, z, xout = ph.pair("y", [P, GRP]), ph.pair("z", [P, GRP]), ph.pair("xout", [P, GRP])
            loaded, scaled, summed = ph.sems("loaded"), ph.sem("scaled"), ph.sem("summed")
            turned, stored = ph.sem("turned"), ph.sems("stored")
            block = ctx.enter_context(nc.Block())

            @block.sync
            def _(sp):
                def loads(q):
                    load(sp, q, hin[q.u][:, :], slab_of(hnt, q.t), loaded[q.u], scaled)
                    load(sp, q, xin[q.u][:, :], slab_of(x2t, q.t), loaded[q.u], summed)

                over_groups(sp, [
                    (0, loads),
                    (3, lambda q: store(sp, q, group_of(t_x3[0:NPAD, :], q.t), xout[q.u][:, :], ln.applied,
                                        stored))])
                all_stored(sp, stored)

            @block.scalar
            def _(act):
                def scale(q):
                    act.wait_ge(loaded[q.u], q.n * 32 + 32)
                    if not is_first(q.t):
                        act.wait_ge(summed, q.t - 1)
                    act.activation(y[q.u][:, :], hin[q.u][:, :], ACT.Identity, bias=bn_c[:, 0:1],
                                   scale=bn_a[:, 0:1]).then_inc(scaled, 1)

                def apply(q):
                    if not is_first(q.t):
                        act.wait_ge(stored[q.u], q.n * 16)
                    ln.normalise(act, q, xout[q.u], bank[q.u])

                over_groups(act, [(0, scale), (1, lambda q: ln.root(act, q)), (2, apply)])

            @block.tensor
            def _(pe):
                def turn(q):
                    pe.wait_ge(summed, q.t + 1)
                    if not is_first(q.t):
                        pe.wait_ge(ln.applied, q.t - 1)
                    for b in range(BLK):
                        last = pe.transpose(bank[q.u][:, b * P:(b + 1) * P], z[q.u][:, b * P:(b + 1) * P],
                                            ident[:, :])
                    last.then_inc(turned, 1)

                over_groups(pe, [(1, turn)])

            @block.vector
            def _(dve):
                def add(q):
                    dve.wait_ge(scaled, q.t + 1)
                    if not is_first(q.t):
                        dve.wait_ge(turned, q.t - 1)
                    dve.tensor_tensor(z[q.u][:, :], y[q.u][:, :], xin[q.u][:, :], ALU.add)\
                       .then_inc(summed, 1)

                def gauge(q):
                    dve.wait_ge(turned, q.t + 1)
                    ln.take_stats(dve, q, bank[q.u])

                over_groups(dve, [(0, add), (1, gauge), (2, lambda q: ln.invert(dve, q))])

    def combine():
        with ExitStack() as ctx:
            ph = Phase(ctx, "cb")
            e = EdgeRows(ph, t_x3, D, CH)
            ln = LayerNorm(ph)
            own_rows, xt, agg = ph.pair("own", [P, GRP]), ph.pair("xt", [P, GRP]), ph.pair("agg", [P, GRP])
            z, xout = ph.pair("z", [P, GRP]), ph.pair("xout", [P, GRP])
            loaded, held, dense_done, added = ph.sems("loaded"), ph.sem("held"), ph.sem("dense"), ph.sem("added")
            stored = ph.sems("stored")
            block = ctx.enter_context(nc.Block())

            @block.gpsimd
            def _(pool):
                over_groups(pool, [(0, lambda q: e.gather(pool, q))])

            @block.sync
            def _(sp):
                def leave(q):
                    if isinstance(q.t, int) and q.t == T - 1:
                        store(sp, q, out[(T - 1) * GRP:NODES, :].rearrange("(p b) f -> p (b f)", b=BLK),
                              xout[q.u][0:LASTP, :], ln.applied, stored)
                    else:
                        store(sp, q, group_of(out[0:(T - 1) * GRP, :], q.t), xout[q.u][:, :], ln.applied,
                              stored)

                over_groups(sp, [
                    (0, lambda q: load(sp, q, own_rows[q.u][:, :], group_of(t_x3[0:NPAD, :], q.t),
                                       loaded[q.u], e.summed)),
                    (4, leave)])
                all_stored(sp, stored)

            @block.tensor
            def _(pe):
                def sums(q):
                    pe.wait_ge(e.ready, q.t + 1)
                    pe.wait_ge(loaded[q.u], q.n * 16 + 16)
                    if not is_first(q.t):
                        pe.wait_ge(held, q.t - 1)
                    e.sum_by_feature(pe, q, [bank[q.u]])
                    for b in range(BLK):
                        last = pe.transpose(bank[2 + q.u][:, b * P:(b + 1) * P],
                                            own_rows[q.u][:, b * D:(b + 1) * D], ident[:, :])
                    last.then_inc(e.summed, 1)

                def dense(q):
                    pe.wait_ge(held, q.t + 1)
                    if not is_first(q.t):
                        pe.wait_ge(added, q.t - 1)
                    for b in range(BLK):
                        to = bank[4 + q.u][:, b * D:(b + 1) * D]
                        pe.matmul(to, agg[q.u][:, b * P:(b + 1) * P], wn_s[:, :], start=True, stop=False,
                                  skip_group_check=True)
                        last = pe.matmul(to, xt[q.u][:, b * P:(b + 1) * P], wsx_s[:, :], start=False,
                                         stop=True, skip_group_check=True)
                    last.then_inc(dense_done, 1)

                over_groups(pe, [(1, sums), (2, dense)])

            @block.scalar
            def _(act):
                def hold(q):
                    act.wait_ge(e.summed, q.t + 1)
                    if not is_first(q.t):
                        act.wait_ge(dense_done, q.t - 1)
                    act.activation(agg[q.u][:, :], bank[q.u][:, :], ACT.Copy)
                    act.activation(xt[q.u][:, :], bank[2 + q.u][:, :], ACT.Copy).then_inc(held, 1)

                def apply(q):
                    if not is_first(q.t):
                        act.wait_ge(stored[q.u], q.n * 16)
                    ln.normalise(act, q, xout[q.u], z[q.u])

                over_groups(act, [(0, lambda q: e.take_hi(act, q)), (1, hold),
                                  (2, lambda q: ln.root(act, q)), (3, apply)])

            @block.vector
            def _(dve):
                def add(q):
                    dve.wait_ge(dense_done, q.t + 1)
                    if not is_first(q.t):
                        dve.wait_ge(ln.applied, q.t - 1)
                    dve.tensor_tensor(z[q.u][:, :], bank[4 + q.u][:, :],
                                      b3_r[:, :, :].rearrange("p b f -> p (b f)"), ALU.add)\
                       .then_inc(added, 1)
                    dve.wait_ge(added, q.t + 1)
                    ln.take_stats(dve, q, z[q.u])

                over_groups(dve, [(0, lambda q: e.prepare(dve, q)), (2, add),
                                  (3, lambda q: ln.invert(dve, q))])

    def fold_weights():
        with ExitStack() as ctx:
            ph = Phase(ctx, "fw")
            link = ph.sem("link")
            block = ctx.enter_context(nc.Block())

            @block.vector
            def _(dve):
                dve.tensor_tensor(brz_c[:, :], bih_c[:, 0:2], bhh_c[:, 0:2], ALU.add)
                dve.tensor_tensor(b3_r[:, :, :], b3_r[:, :, :], b3b_r[:, :, :], ALU.add)
                dve.tensor_scalar(wad_s[:, :], iota[:, 0:P], 0.0, wm_s[:, D + 1:D + 2], ALU.mult, ALU.add)
                dve.scalar_tensor_tensor(out=wsx_s[:, :], in0=wn_s[:, :], scalar=own[:, 0:1],
                                         in1=wsx_s[:, :], op0=ALU.mult, op1=ALU.add).then_inc(link, 1)
                dve.wait_ge(link, 1)
                dve.tensor_tensor(wsx_s[:, :], wsx_s[:, :], ident[:, :], ALU.add)

    with top:
        load_weights()
        sort_edges()
        fold_weights()
        count_degrees()
        scale_degrees()
        scale_x()
        gcn_first()
        gcn_second()
        sage_first()
        sage_second()
        sage_third()
        attend()
        batch_constants()
        batch_normed()
        combine()


_INS = ["x", "src", "dst", "L0_gnn_W1", "L0_gnn_b1", "L0_gnn_W2", "L0_gnn_b2", "L1_gnn_ws0",
        "L1_gnn_wn0", "L1_gnn_b0", "L1_gnn_ws1", "L1_gnn_wn1", "L1_gnn_b1", "L1_gnn_ws2", "L1_gnn_wn2",
        "L1_gnn_b2", "L2_gnn_W_msg", "L2_gnn_b_msg", "L2_gnn_W_att", "L2_gnn_b_att", "L2_gnn_W_ih",
        "L2_gnn_b_ih", "L2_gnn_W_hh", "L2_gnn_b_hh", "L2_gnn_gamma", "L2_gnn_beta", "L3_gnn_W_neigh",
        "L3_gnn_b_neigh", "L3_gnn_W_self", "L3_gnn_b_self"]
_TURNED = {"L2_gnn_W_ih", "L2_gnn_W_hh", "L3_gnn_W_neigh", "L3_gnn_W_self"}


def kernel(**inputs):
    import numpy as _np
    import concourse.bacc as _bacc
    from concourse import mybir as _mybir
    from concourse.bass_utils import run_bass_kernel_spmd as _run

    nc = _bacc.Bacc("TRN2", target_bir_lowering=False, num_devices=1)
    arrays, args = {}, []
    for name in _INS:
        a = _np.asarray(inputs[name])
        a = _np.ascontiguousarray(a.T if name in _TURNED else a)
        arrays[f"in_{name}_dram"] = a
        args.append(nc.dram_tensor(f"in_{name}_dram", a.shape, _mybir.dt.from_np(a.dtype),
                                   kind="ExternalInput").ap())
    out = nc.dram_tensor("out_0_dram", (NODES, D), F32, kind="ExternalOutput").ap()
    build_program(nc, *args, out)
    r = _run(nc, [arrays], core_ids=[0])
    return r.results[0]["out_0_dram"]
```

```python
from contextlib import ExitStack

import concourse.bass as bass
from concourse import mybir

F32 = mybir.dt.float32
F32R = mybir.dt.float32r
I32 = mybir.dt.int32
U32 = mybir.dt.uint32
ALU = mybir.AluOpType
ACT = mybir.ActivationFunctionType
AX_X = mybir.AxisListType.X

P = 128
D = 128
HID = 256
NODES = 50000
EDGES = 100000
BLK = 4
GRP = BLK * P
T = -(-NODES // GRP)
NPAD = T * GRP
LAST = NODES - (T - 1) * GRP
LASTP = LAST // BLK
CH = 5
SLOTS = T * CH
EC = -(-EDGES // P)
TAIL = EDGES - (P - 1) * EC
SC = 23
NOWHERE = 1 << 20
PADV = 2000000
MW = D + 4
LN_EPS = 1e-5
BN_EPS = 1e-5
assert LAST % BLK == 0 and EC % (2 * SC) == 0 and P * SLOTS <= NOWHERE


def is_first(t, slots=2):
    return isinstance(t, int) and t < slots


def wait_for(eng, sem, value):
    eng.wait_ge(sem, value)
    if not isinstance(value, int):
        eng.sem_inc(PASSED[0], 1)


PASSED = []


class Turn:

    def __init__(self, j, unroll, d):
        self.j, self.unroll, self.d = j, unroll, d
        self.t = d if j is None else j * unroll + d
        self.u = d % 2
        self.n = self.use(2)
        self.r = d % 4
        self.m = self.use(4)

    def use(self, slots):
        if self.j is None:
            return self.d // slots
        return self.j * (self.unroll // slots) + self.d // slots


def over_groups(eng, stages, unroll=4):
    lim = T - 2

    def step(s):
        for lag, stage in stages:
            if 0 <= s - lag < T:
                stage(Turn(None, unroll, s - lag))

    most = max(lag for lag, _ in stages)
    head = max(2 + most, unroll)
    head += (T - 2 - head) % unroll
    for s in range(head):
        step(s)
    with eng.Fori(0, (lim - head) // unroll) as j:
        for o in range(unroll):
            for lag, stage in stages:
                stage(Turn(j, unroll, head + o - lag))
    for s in range(lim, T + most):
        step(s)


def col(tile, i, n=1):
    return tile[:, bass.ds(i, n)]


def group_of(table, t, b=BLK):
    v = table.rearrange("(t p b) f -> t p (b f)", p=P, b=b)
    return v[bass.ds(t, 1)].rearrange("o p f -> (o p) f")


def slab_of(table, t):
    return table[bass.ds(t, 1)].rearrange("o p f -> (o p) f")


def build_program(nc, x, src, dst, w1, b1, w2, b2, ws0, wn0, sb0, ws1, wn1, sb1, ws2, wn2, sb2,
                  w_msg, b_msg, w_att, b_att, w_ihT, b_ih, w_hhT, b_hh, gamma, beta,
                  w_nT, b_n, w_sT, b_s, out):
    top = ExitStack()

    def sb(name, shape, dt=F32):
        return top.enter_context(nc.sbuf_tensor(name, shape, dt))

    def dram(name, shape, dt=F32):
        return nc.dram_tensor(name, shape, dt, kind="Internal").ap()

    PASSED[:] = [top.enter_context(nc.semaphore("waits_passed"))]

    t_x0 = dram("t_x0", (2 * NPAD, D))
    t_h0 = dram("t_h0", (2 * NPAD, D))
    t_x1 = dram("t_x1", (2 * NPAD, D))
    t_h = dram("t_h", (2 * NPAD, HID))
    t_v = dram("t_v", (2 * NPAD, D))
    t_m = dram("t_m", (2 * NPAD, MW))
    t_x3 = dram("t_x3", (2 * NPAD, D))
    r1 = dram("r1", (NPAD, D))
    r2 = dram("r2", (NPAD, D))
    x2t = dram("x2t", (T, P, GRP))
    hnt = dram("hnt", (T, P, GRP))
    sums_by_width = {w: dram(f"sums_{w}", (NPAD + 2 * P, w)) for w in (D, MW, HID)}
    slots_d = dram("slots_d", (P * SLOTS, 2))
    deg_d = dram("deg_d", (T, GRP))
    dinv_d = dram("dinv_d", (T, GRP))
    inv_d = dram("inv_d", (T, GRP))

    idx = sb("idx", [P, SLOTS], U32)
    dcol = sb("dcol", [P, SLOTS])
    dinv_n = sb("dinv_n", [P, T * BLK])
    dinv2_n = sb("dinv2_n", [P, T * BLK])
    inv_n = sb("inv_n", [P, T * BLK])
    selfinv_n = sb("selfinv_n", [P, T * BLK])
    iota = sb("iota", [P, GRP])
    ident = sb("ident", [P, P])
    own = sb("own", [P, 1])
    general = sb("general", [P, 1], I32)
    own1 = sb("own1", [P, 1])
    id_own1 = sb("id_own1", [P, P])
    id_own_r = sb("id_own_r", [P, P], F32R)
    bn_acc = sb("bn_acc", [P, T + BLK - 1, 6])
    bn_mv = sb("bn_mv", [P, 2])
    bn_a = sb("bn_a", [P, 1])
    bn_c = sb("bn_c", [P, 1])

    w1_s = sb("w1_s", [P, HID])
    w2_s = sb("w2_s", [P, 2, D])
    b1_c = sb("b1_c", [P, 2])
    b2_r = sb("b2_r", [P, BLK, D])
    ws0_s = sb("ws0_s", [P, HID])
    wn0_s = sb("wn0_s", [P, HID])
    sb0_r = sb("sb0_r", [P, 2, HID])
    ws1_s = sb("ws1_s", [P, 2, HID])
    wn1_s = sb("wn1_s", [P, 2, HID])
    sb1_c = sb("sb1_c", [P, 2])
    wuv_s = sb("wuv_s", [P, 2, HID])
    sb2_r = sb("sb2_r", [P, BLK, D])
    wm_s = sb("wm_s", [P, MW])
    bm_r = sb("bm_r", [P, 2, MW])
    wad_s = sb("wad_s", [P, P])
    wih_s = sb("wih_s", [P, 3 * D])
    whh_s = sb("whh_s", [P, 3 * D])
    bih_c = sb("bih_c", [P, 3])
    bhh_c = sb("bhh_c", [P, 3])
    brz_c = sb("brz_c", [P, 2])
    gam_c = sb("gam_c", [P, 1])
    bet_c = sb("bet_c", [P, 1])
    wn_s = sb("wn_s", [P, D])
    wsx_s = sb("wsx_s", [P, D])
    b3_r = sb("b3_r", [P, BLK, D])
    b3b_r = sb("b3b_r", [P, BLK, D])

    bank = [top.enter_context(nc.psum_tensor(f"bank{i}", [P, 512], F32)) for i in range(8)]

    class Phase:

        def __init__(self, ctx, name):
            self.ctx, self.name, self.own_sems = ctx, name, []
            ctx.callback(self.clear)

        def clear(self):
            nc.clear_and_free_semaphores(self.own_sems)
            nc.all_engine_barrier()

        def tile(self, name, shape, dt=F32):
            return self.ctx.enter_context(nc.sbuf_tensor(f"{self.name}_{name}", shape, dt))

        def pair(self, name, shape, dt=F32, n=2):
            return [self.tile(f"{name}{u}", shape, dt) for u in range(n)]

        def sem(self, name):
            self.own_sems.append(nc.alloc_semaphore(f"{self.name}_{name}"))
            return self.own_sems[-1]

        def sems(self, name, n=2):
            return [self.sem(f"{name}{u}") for u in range(n)]

    def load_weights():
        with ExitStack() as ctx:
            ph = Phase(ctx, "w")
            got, cleared = ph.sem("loaded"), ph.sem("cleared")
            block = ctx.enter_context(nc.Block())

            def row(a, n):
                return a.rearrange("(o n) -> o n", o=1).broadcast_to([P, n])

            def column(a, k):
                return a.rearrange("(k p) -> p k", p=P)

            loads = [
                (w1_s[:, :], w1), (w2_s[:, :, :], w2.rearrange("(k p) f -> p k f", p=P)),
                (ws0_s[:, :], ws0), (wn0_s[:, :], wn0),
                (ws1_s[:, :, :], ws1.rearrange("(k p) f -> p k f", p=P)),
                (wn1_s[:, :, :], wn1.rearrange("(k p) f -> p k f", p=P)),
                (wuv_s[:, :, 0:D], ws2.rearrange("(k p) f -> p k f", p=P)),
                (wuv_s[:, :, D:HID], wn2.rearrange("(k p) f -> p k f", p=P)),
                (wm_s[:, 0:D], w_msg), (wm_s[:, D:D + 1], w_att[0:D, :]),
                (wm_s[:, D + 1:D + 2], w_att[D:2 * D, :]),
                (wih_s[:, :], w_ihT), (whh_s[:, :], w_hhT), (wn_s[:, :], w_nT), (wsx_s[:, :], w_sT),
                (b1_c[:, :], column(b1, 2)), (sb1_c[:, :], column(sb1, 2)),
                (bih_c[:, :], column(b_ih, 3)), (bhh_c[:, :], column(b_hh, 3)),
                (gam_c[:, :], column(gamma, 1)), (bet_c[:, :], column(beta, 1)),
            ]
            for k in range(BLK):
                loads += [(b2_r[:, k, :], row(b2, D)), (sb2_r[:, k, :], row(sb2, D)),
                          (b3_r[:, k, :], row(b_n, D)), (b3b_r[:, k, :], row(b_s, D))]
            for k in range(2):
                loads += [(sb0_r[:, k, :], row(sb0, HID)), (bm_r[:, k, 0:D], row(b_msg, D)),
                          (bm_r[:, k, D:D + 1], row(b_att, 1))]

            @block.vector
            def _(dve):
                dve.memset(wm_s[:, :], 0.0)
                dve.memset(bm_r[:, :, :], 0.0).then_inc(cleared, 1)

            @block.sync
            def _(sp):
                sp.wait_ge(cleared, 1)
                for to, what in loads:
                    sp.dma_start(to, what, allow_slow_non_contiguous=True).then_inc(got, 16)
                sp.wait_ge(got, 16 * len(loads))

    def sort_edges():
        with ExitStack() as ctx:
            ph = Phase(ctx, "so")
            tmp, sem = ph.tile, ph.sem

            si = tmp("src_i", [P, EC], I32)
            di = tmp("dst_i", [P, EC], I32)
            ni = tmp("next_i", [P, EC], I32)
            ei = tmp("edge_i", [P, EC], I32)
            q1 = tmp("int_1", [P, EC], I32)
            q2 = tmp("int_2", [P, EC], I32)
            ef = tmp("edge_f", [P, EC])
            ends = tmp("ends_f", [P, EC])
            a = tmp("scratch_a", [P, EC])
            b = tmp("scratch_b", [P, EC])
            c = tmp("scratch_c", [P, EC])
            df = tmp("dst_f", [P, EC])
            nf = tmp("next_f", [P, EC])
            base = tmp("base_f", [P, EC + 1])
            pos = tmp("slot_row", [P, EC], U32)
            pair = tmp("slot_pair", [P, EC, 2])
            posb = tmp("slot_row_now", [P, 2, SC], U32)
            pairb = tmp("slot_pair_now", [P, 2, SC, 2])
            rowmax = tmp("rowmax", [P, 1])
            carry = tmp("carry", [P, 1])
            rows = tmp("rows", [1, P + 1])
            empty = tmp("empty_slots", [P, SLOTS, 2])
            back = tmp("slots_back", [P, SLOTS, 2])
            seen = tmp("seen", [P, 4])
            total = tmp("total", [P, 4])
            ones = tmp("ones", [P, P])
            idxi = tmp("iota_i", [P, GRP], I32)

            made = sem("patterns_made")
            padded = sem("edges_padded")
            got = sem("edges_loaded")
            chain = sem("edge_steps")
            turned = sem("carry_turned")
            blank = sem("slots_blanked")
            ready = sem("turn_ready")
            sent = [sem("turn_sent_0"), sem("turn_sent_1")]
            read = sem("slots_read")
            block = ctx.enter_context(nc.Block())

            @block.gpsimd
            def _(pool):
                pool.iota(ei[:, :], pattern=[[1, EC]], base=0, channel_multiplier=EC).then_inc(made, 1)
                pool.iota(idxi[:, :], pattern=[[1, GRP]], base=0, channel_multiplier=0).then_inc(made, 1)
                pool.memset(ident[:, :], 0.0).then_inc(made, 1)
                pool.memset(empty[:, :, 0], float(NOWHERE)).then_inc(made, 1)
                pool.memset(empty[:, :, 1], -1.0).then_inc(made, 1)
                pool.wait_ge(made, 5)
                pool.affine_select(out=ident[:, :], in_=ident[:, :], compare_op=ALU.not_equal, fill=1.0,
                                   base=0, pattern=[[-1, P]], channel_multiplier=1).then_inc(made, 1)
                pool.wait_ge(blank, 16)

                def send(n, u):
                    wait_for(pool, ready, n * 2 + (u + 1))
                    for k in range(SC):
                        pool.indirect_dma_start(
                            out=slots_d, out_offset=bass.IndirectOffsetOnAxis(ap=posb[:, u, k:k + 1], axis=0),
                            in_=pairb[:, u, k, :], in_offset=None,
                            bounds_check=P * SLOTS - 1, oob_is_err=False).then_inc(sent[u], 16)

                with pool.Fori(0, EC // (2 * SC)) as j:
                    send(j, 0)
                    send(j, 1)

            @block.sync
            def _(sp):
                sp.wait_ge(made, 6)
                sp.dma_start(slots_d.rearrange("(p s) f -> p (s f)", p=P),
                             empty[:, :, :].rearrange("p s f -> p (s f)")).then_inc(blank, 16)
                sp.wait_ge(padded, 2)
                full = (P - 1) * EC
                for tile, a, off in ((si, src, 0), (di, dst, 0), (ni, dst, 1)):
                    sp.dma_start(tile[0:P - 1, :], a[off:off + full].rearrange("(p c) -> p c", p=P - 1))\
                      .then_inc(got, 16)
                    sp.dma_start(tile[P - 1:P, 0:TAIL - off],
                                 a[off + full:EDGES].rearrange("(o c) -> o c", o=1)).then_inc(got, 16)
                for u in range(2):
                    sp.wait_ge(sent[u], EC // 2 * 16)
                sp.dma_start(back[:, :, :].rearrange("p s f -> p (s f)"),
                             slots_d.rearrange("(p s) f -> p (s f)", p=P)).then_inc(read, 16)

            @block.tensor
            def _(pe):
                pe.wait_ge(turned, 1)
                pe.transpose(bank[0][0:1, 0:P], rowmax[:, :], ident[:, :]).then_inc(turned, 1)
                pe.wait_ge(turned, 3)
                pe.matmul(bank[1][:, 0:1], rows[0:1, 0:P], ones[0:1, 0:1], start=True, stop=True)\
                  .then_inc(turned, 1)
                pe.wait_ge(turned, 5)
                pe.matmul(bank[2][:, 0:4], ones[:, :], seen[:, :], start=True, stop=True)\
                  .then_inc(turned, 1)

            @block.vector
            def _(dve):
                steps = [0]

                def then(ins):
                    steps[0] += 1
                    ins.then_inc(chain, 1)
                    dve.wait_ge(chain, steps[0])

                dve.memset(si[:, :], 0).then_inc(padded, 1)
                dve.memset(di[:, :], PADV)
                dve.memset(ni[:, :], PADV).then_inc(padded, 1)
                dve.memset(seen[:, :], 0.0)
                then(dve.memset(ones[:, :], 1.0))
                dve.wait_ge(made, 6)
                dve.tensor_copy(iota[:, :], idxi[:, :])
                dve.tensor_copy(ef[:, :], ei[:, :])
                dve.wait_ge(got, 96)
                dve.tensor_copy(df[:, :], di[:, :])
                then(dve.tensor_copy(nf[:, :], ni[:, :]))
                then(dve.tensor_tensor(ends[:, :], df[:, :], nf[:, :], ALU.not_equal))
                dve.tensor_reduce(seen[:, 2:3], ends[:, :], AX_X, ALU.add)
                then(dve.tensor_copy(b[:, :], si[:, :]))
                then(dve.tensor_tensor(b[:, :], b[:, :], df[:, :], ALU.not_equal))
                then(dve.tensor_tensor(b[:, :], b[:, :], ends[:, :], ALU.mult))
                dve.tensor_reduce(seen[:, 1:2], b[:, :], AX_X, ALU.add)
                then(dve.tensor_tensor(c[:, :], nf[:, :], df[:, :], ALU.is_lt))
                then(dve.tensor_reduce(seen[:, 0:1], c[:, :], AX_X, ALU.add))
                dve.tensor_scalar(q1[:, :], di[:, :], 9, None, ALU.logical_shift_right)
                then(dve.tensor_scalar(q2[:, :], ni[:, :], 9, None, ALU.logical_shift_right))
                dve.tensor_copy(a[:, :], q1[:, :])
                then(dve.tensor_copy(b[:, :], q2[:, :]))
                then(dve.tensor_tensor(b[:, :], a[:, :], b[:, :], ALU.not_equal))
                then(dve.scalar_tensor_tensor(out=c[:, :], in0=ef[:, :], scalar=1.0, in1=b[:, :],
                                              op0=ALU.add, op1=ALU.mult))
                dve.tensor_reduce(rowmax[:, :], c[:, :], AX_X, ALU.max).then_inc(turned, 1)
                then(dve.memset(rows[:, :], 0.0))
                dve.wait_ge(turned, 2)
                dve.tensor_tensor_scan(rows[0:1, 1:P + 1], bank[0][0:1, 0:P], rows[0:1, 1:P + 1], 0.0,
                                       ALU.max, ALU.max).then_inc(turned, 1)
                dve.wait_ge(turned, 4)
                then(dve.tensor_copy(carry[:, :], bank[1][:, 0:1]))
                dve.tensor_copy(base[:, 0:1], carry[:, :])
                then(dve.tensor_tensor_scan(base[:, 1:EC + 1], c[:, :], c[:, :], carry[:, 0:1],
                                            ALU.max, ALU.max))
                then(dve.tensor_scalar(q2[:, :], di[:, :], GRP - 1, None, ALU.bitwise_and))
                then(dve.tensor_copy(b[:, :], q2[:, :]))
                dve.tensor_scalar(ni[:, :], q2[:, :], 3, 7, ALU.bitwise_and, ALU.logical_shift_left)
                then(dve.tensor_scalar(q2[:, :], q2[:, :], 2, None, ALU.logical_shift_right))
                then(dve.tensor_tensor(q2[:, :], q2[:, :], ni[:, :], ALU.bitwise_or))
                dve.tensor_copy(pair[:, :, 1], q2[:, :])
                dve.tensor_copy(pair[:, :, 0], si[:, :])
                then(dve.tensor_tensor(c[:, :], ef[:, :], base[:, 0:EC], ALU.subtract))
                then(dve.tensor_tensor(c[:, :], c[:, :], b[:, :], ALU.subtract))
                dve.tensor_scalar(b[:, :], df[:, :], float(NODES), None, ALU.is_ge)
                then(dve.tensor_scalar(nf[:, :], c[:, :], float(CH * P), None, ALU.is_ge))
                then(dve.tensor_tensor(b[:, :], b[:, :], ends[:, :], ALU.max))
                then(dve.tensor_tensor(b[:, :], nf[:, :], b[:, :], ALU.is_gt))
                dve.tensor_reduce(seen[:, 3:4], b[:, :], AX_X, ALU.add).then_inc(turned, 1)
                then(dve.tensor_scalar(c[:, :], c[:, :], 0.0, float(CH * P - 1), ALU.max, ALU.min))
                then(dve.tensor_copy(q1[:, :], c[:, :]))
                dve.tensor_scalar(q2[:, :], q1[:, :], P - 1, None, ALU.bitwise_and)
                then(dve.tensor_scalar(q1[:, :], q1[:, :], 7, None, ALU.logical_shift_right))
                dve.tensor_copy(b[:, :], q2[:, :])
                then(dve.tensor_copy(c[:, :], q1[:, :]))
                then(dve.scalar_tensor_tensor(out=c[:, :], in0=a[:, :], scalar=float(CH), in1=c[:, :],
                                              op0=ALU.mult, op1=ALU.add))
                then(dve.scalar_tensor_tensor(out=c[:, :], in0=b[:, :], scalar=float(SLOTS), in1=c[:, :],
                                              op0=ALU.mult, op1=ALU.add))
                dve.tensor_scalar(b[:, :], df[:, :], float(NODES), None, ALU.is_ge)
                then(dve.tensor_scalar(c[:, :], c[:, :], float(P * SLOTS - 1), None, ALU.min))
                then(dve.tensor_tensor(b[:, :], b[:, :], ends[:, :], ALU.max))
                then(dve.scalar_tensor_tensor(out=c[:, :], in0=b[:, :], scalar=float(NOWHERE), in1=c[:, :],
                                              op0=ALU.mult, op1=ALU.add))
                dve.wait_ge(turned, 6)
                then(dve.tensor_copy(total[:, :], bank[2][:, 0:4]))
                dve.tensor_tensor(total[:, 0:1], total[:, 0:1], total[:, 1:2], ALU.add)
                then(dve.tensor_scalar(total[:, 2:3], total[:, 2:3], float(NODES), None, ALU.not_equal))
                then(dve.tensor_tensor(total[:, 2:3], total[:, 2:3], total[:, 3:4], ALU.add))
                then(dve.tensor_tensor(total[:, 0:1], total[:, 0:1], total[:, 2:3], ALU.add))
                then(dve.tensor_scalar(total[:, 0:1], total[:, 0:1], 0.0, None, ALU.is_gt))
                dve.tensor_copy(general[:, :], total[:, 0:1])
                then(dve.tensor_scalar(own[:, :], total[:, 0:1], -1.0, 1.0, ALU.mult, ALU.add))
                then(dve.tensor_scalar(total[:, 1:2], total[:, 0:1], float(NOWHERE), None, ALU.mult))
                then(dve.tensor_scalar(c[:, :], c[:, :], total[:, 1:2], None, ALU.add))
                then(dve.tensor_copy(pos[:, :], c[:, :]))

                def give(n, u, first):
                    if not first:
                        wait_for(dve, sent[u], n * (16 * SC))
                    at = n * (2 * SC) + u * SC
                    dve.tensor_copy(pairb[:, u, :, :], pair[:, bass.ds(at, SC), :])
                    dve.tensor_copy(posb[:, u, :], pos[:, bass.ds(at, SC)]).then_inc(ready, 1)

                give(0, 0, True)
                give(0, 1, True)
                with dve.Fori(1, EC // (2 * SC)) as j:
                    give(j, 0, False)
                    give(j, 1, False)
                dve.wait_ge(read, 16)
                dve.tensor_copy(idx[:, :], back[:, :, 0])
                dve.tensor_copy(dcol[:, :], back[:, :, 1])
                dve.tensor_scalar(own1[:, :], own[:, :], 1.0, None, ALU.add).then_inc(turned, 1)
                dve.wait_ge(turned, 7)
                dve.tensor_scalar(id_own1[:, :], ident[:, :], own1[:, 0:1], None, ALU.mult)
                dve.tensor_scalar(id_own_r[:, :], ident[:, :], own[:, 0:1], None, ALU.mult)


    class EdgeRows:

        def __init__(self, ph, table, width, parts, hots=2):
            self.table, self.width = table, width
            self.rows = ph.pair("rows", [P, CH, width], n=4)
            self.hi = ph.pair("hi", [P, parts, min(width, HID) if width != MW else D], F32R)
            self.lo = ph.pair("lo", [P, parts, min(width, HID) if width != MW else D], F32R)
            self.hots = hots
            self.onehot = ph.pair("onehot", [P, CH, GRP], F32R, n=hots)
            self.index = ph.pair("index", [P, CH], U32, n=4)
            self.cleared = ph.sem("rows_cleared")
            self.indexed = ph.sem("index_copied")
            self.gathered = ph.sems("rows_gathered", 4)
            self.split = ph.sem("rows_hi")
            self.ready = ph.sem("rows_ready")
            self.summed = ph.sem("rows_summed")

        def gather(self, pool, q, used=None):
            if isinstance(q.t, int) and q.t < 4:
                pool.memset(self.rows[q.r][:, :, :], 0.0).then_inc(self.cleared, 1)
            else:
                wait_for(pool, used or self.ready, q.t - 3)
            pool.tensor_copy(self.index[q.r][:, :], col(idx, q.t * CH, CH)).then_inc(self.indexed, 1)
            if isinstance(q.t, int) and q.t < 4:
                pool.wait_ge(self.cleared, q.t + 1)
            wait_for(pool, self.indexed, q.t + 1)
            for k in range(CH):
                pool.indirect_dma_start(
                    out=self.rows[q.r][:, k, :], out_offset=None, in_=self.table[0:NPAD, :],
                    in_offset=bass.IndirectOffsetOnAxis(ap=self.index[q.r][:, k:k + 1], axis=0),
                    bounds_check=NPAD - 1, oob_is_err=False).then_inc(self.gathered[q.r], 16)

        def arrived(self, eng, q):
            eng.wait_ge(self.gathered[q.r], (q.m + 1) * (16 * CH))

        def free(self, eng, q):
            if not is_first(q.t):
                eng.wait_ge(self.summed, q.t - 1)

        def take_hi(self, act, q):
            self.arrived(act, q)
            self.free(act, q)
            act.activation(self.hi[q.u][:, :, :], self.rows[q.r][:, :, :], ACT.Copy).then_inc(self.split, 1)

        def make_onehots(self, dve, q):
            if not is_first(q.t, self.hots):
                dve.wait_ge(self.summed, q.t - (self.hots - 1))
            for k in range(CH):
                last = dve.tensor_scalar(self.onehot[q.d % self.hots][:, k, :], iota[:, :],
                                         col(dcol, q.t * CH + k), None, ALU.is_equal)
            return last

        def take_lo(self, dve, q):
            dve.wait_ge(self.split, q.t + 1)
            dve.tensor_tensor(self.lo[q.u][:, :, :], self.rows[q.r][:, :, :],
                              self.hi[q.u][:, :, :].bitcast(F32), ALU.subtract).then_inc(self.ready, 1)

        def prepare(self, dve, q):
            self.make_onehots(dve, q)
            self.take_lo(dve, q)

        def sum_by_feature(self, pe, q, banks, close=True):
            for h, to in enumerate(banks):
                for k in range(CH):
                    for part in (self.hi, self.lo):
                        last = pe.matmul(to[:, :], part[q.u][:, k, h * P:(h + 1) * P],
                                         self.onehot[q.d % self.hots][:, k, :], start=(k == 0 and part is self.hi),
                                         stop=(close and k == CH - 1 and part is self.lo),
                                         skip_group_check=True)
            return last

        def sum_by_node(self, pe, q, to):
            for b in range(BLK):
                for k in range(CH):
                    for part in (self.hi, self.lo):
                        last = pe.matmul(to[:, b * P:(b + 1) * P],
                                         self.onehot[q.d % self.hots][:, k, b * P:(b + 1) * P], part[q.u][:, k, :],
                                         start=(k == 0 and part is self.hi),
                                         stop=(k == CH - 1 and part is self.lo), skip_group_check=True)
            return last

    class LayerNorm:

        def __init__(self, ph):
            self.stats = ph.pair("ln_stats", [P, BLK, 6])
            self.mv = ph.pair("ln_mv", [P, BLK, 2])
            self.var = ph.pair("ln_var", [P, BLK])
            self.std = ph.pair("ln_std", [P, BLK])
            self.rstd = ph.pair("ln_rstd", [P, BLK])
            self.shift = ph.pair("ln_shift", [P, BLK])
            self.link = ph.sem("ln_link")
            self.link2 = ph.sem("ln_link2")
            self.varied = ph.sem("ln_varied")
            self.rooted = ph.sem("ln_rooted")
            self.scaled = ph.sem("ln_scaled")
            self.applied = ph.sem("ln_applied")

        def take_stats(self, dve, q, z):
            for b in range(BLK):
                last = dve.bn_stats(self.stats[q.u][:, b, :], z[:, b * D:(b + 1) * D])
            last.then_inc(self.link, 1)
            wait_for(dve, self.link, q.t * 2 + 1)
            for b in range(BLK):
                last = dve.bn_aggr(self.mv[q.u][:, b, :], self.stats[q.u][:, b, :])
            last.then_inc(self.link, 1)
            dve.wait_ge(self.link, q.t * 2 + 2)
            dve.tensor_scalar(self.var[q.u][:, :], self.mv[q.u][:, :, 1], LN_EPS, None, ALU.add)\
               .then_inc(self.varied, 1)

        def root(self, act, q):
            act.wait_ge(self.varied, q.t + 1)
            act.activation(self.std[q.u][:, :], self.var[q.u][:, :], ACT.Sqrt).then_inc(self.rooted, 1)

        def invert(self, dve, q):
            dve.wait_ge(self.rooted, q.t + 1)
            dve.reciprocal(self.rstd[q.u][:, :], self.std[q.u][:, :]).then_inc(self.link2, 1)
            dve.wait_ge(self.link2, q.t + 1)
            dve.scalar_tensor_tensor(out=self.shift[q.u][:, :], in0=self.mv[q.u][:, :, 0], scalar=-1.0,
                                     in1=self.rstd[q.u][:, :], op0=ALU.mult, op1=ALU.mult)\
               .then_inc(self.scaled, 1)

        def normalise(self, act, q, to, z):
            act.wait_ge(self.scaled, q.t + 1)
            for b in range(BLK):
                last = act.activation(to[:, b * D:(b + 1) * D], z[:, b * D:(b + 1) * D], ACT.Identity,
                                      bias=self.shift[q.u][:, b:b + 1], scale=self.rstd[q.u][:, b:b + 1])
            last.then_inc(self.applied, 1)

    def load(sp, q, to, what, loaded, free=None, slots=2):
        if free is not None and not (isinstance(q.t, int) and q.t < slots):
            wait_for(sp, free, q.t - (slots - 1))
        sp.dma_start(to, what).then_inc(loaded, 16)

    def store(sp, q, to, what, made, stored):
        wait_for(sp, made, q.t + 1)
        sp.dma_start(to, what).then_inc(stored[q.d % len(stored)], 16)

    def all_stored(sp, *stored):
        for sems in stored:
            for u, sem in enumerate(sems):
                sp.wait_ge(sem, 16 * ((T + len(sems) - 1 - u) // len(sems)))

    def own_group(table, t):
        return group_of(table, t + way["rows"])

    def row_of(a, t):
        return a[bass.ds(t, 1), :].broadcast_to([P, GRP])

    def general_slots():
        with ExitStack() as ctx:
            ph = Phase(ctx, "gs")
            row = ph.tile("row", [P, T, BLK], I32)
            place = ph.tile("place", [P, BLK], I32)
            made, link = ph.sem("made"), ph.sem("link")
            block = ctx.enter_context(nc.Block())

            @block.gpsimd
            def _(pool):
                pool.iota(row[:, :, :], pattern=[[GRP, T], [1, BLK]], base=0, channel_multiplier=BLK)\
                    .then_inc(made, 1)
                pool.iota(place[:, :], pattern=[[P, BLK]], base=0, channel_multiplier=1).then_inc(made, 1)

            @block.vector
            def _(dve):
                dve.memset(idx[:, :], NOWHERE)
                dve.memset(dcol[:, :], -1.0).then_inc(link, 1)
                dve.wait_ge(link, 1)
                dve.wait_ge(made, 2)
                dve.tensor_copy(idx[:, :].rearrange("p (t k) -> p t k", k=CH)[:, :, 0:BLK], row[:, :, :])
                for k in range(BLK):
                    dve.tensor_scalar(dcol[:, :].rearrange("p (t k) -> p t k", k=CH)[:, :, k], row[:, :, 0],
                                      0.0, 0.0, ALU.mult, ALU.add).then_inc(link, 1)
                dve.tensor_copy(id_own1[:, 0:BLK], place[:, :]).then_inc(link, 1)
                dve.wait_ge(link, 2 + BLK)
                for k in range(BLK):
                    v = dcol[:, :].rearrange("p (t k) -> p t k", k=CH)[:, :, k]
                    dve.tensor_scalar(v, v, id_own1[:, k:k + 1], None, ALU.add).then_inc(link, 1)
                dve.wait_ge(link, 2 + 2 * BLK)
                dve.tensor_scalar(id_own1[:, :], ident[:, :], own1[:, 0:1], None, ALU.mult)

    summed_for = []

    def general_sums(table, width, kind="rows"):
        JUNK = NPAD + P
        sums = sums_by_width[width]
        with ExitStack() as ctx:
            ph = Phase(ctx, f"sums{len(summed_for)}")
            summed_for.append(table)
            si, di = ph.tile("src", [P, EC], I32), ph.tile("dst", [P, EC], I32)
            nowhere = ph.tile("nowhere", [P, EC], I32)
            jrow = ph.tile("jrow", [P, 1], I32)
            junk, before = ph.tile("junk", [P, 1]), ph.tile("before", [P, P])
            zero, ones = ph.tile("zero", [P, BLK * width]), ph.tile("ones", [P, P])
            s_now, d_now, to_now = (ph.tile(n, [P, 1], U32) for n in ("s_now", "d_now", "to_now"))
            d_f, d_all = ph.tile("d_f", [P, 1]), ph.tile("d_all", [P, P])
            same, scrap = ph.tile("same", [P, P]), ph.tile("scrap", [P, P])
            ahead, move = ph.tile("ahead", [P, 1]), ph.tile("move", [P, 1])
            rows, theirs = ph.tile("rows", [P, width]), ph.tile("theirs", [P, width])
            att = ph.tile("att", [P, 1])
            part = ph.tile("part", [P, width])
            degs = ph.tile("degs", [P, T, BLK])
            made, filled, got, link = ph.sem("made"), ph.sem("filled"), ph.sem("got"), ph.sem("link")
            spread, matched, gathered = ph.sem("spread"), ph.sem("matched"), ph.sem("gathered")
            aimed, weighed, summed = ph.sem("aimed"), ph.sem("weighed"), ph.sem("summed")
            parted, added, copied = ph.sem("parted"), ph.sem("added"), ph.sem("copied")
            asked = ph.sem("asked")
            gathers = 0 if kind == "ones" else 2 if kind == "messages" else 1
            block = ctx.enter_context(nc.Block())

            @block.sync
            def _(sp):
                sp.wait_ge(filled, 1)
                full = (P - 1) * EC
                for tile, a in ((si, src), (di, dst)):
                    sp.dma_start(tile[0:P - 1, :], a[0:full].rearrange("(p c) -> p c", p=P - 1)).then_inc(got, 16)
                    sp.dma_start(tile[P - 1:P, 0:TAIL], a[full:EDGES].rearrange("(o c) -> o c", o=1))\
                      .then_inc(got, 16)
                view = sums[0:NPAD, :].rearrange("(t p b) f -> t p (b f)", p=P, b=BLK)
                for t in range(T):
                    sp.dma_start(view[t], zero[:, :])\
                      .then_inc(copied, 16)
                sp.dma_start(sums[NPAD:NPAD + P, 0:width], zero[:, 0:width]).then_inc(copied, 16)
                sp.dma_start(sums[JUNK:JUNK + P, 0:width], zero[:, 0:width]).then_inc(copied, 16)
                moves = T + 2
                if kind != "ones":
                    sp.dma_start(table[NPAD:2 * NPAD, :], table[0:NPAD, :]).then_inc(copied, 16)
                    moves += 1
                sp.wait_ge(added, 16 * EC)
                if kind == "ones":
                    for k in range(BLK):
                        sp.dma_start(degs[:, :, k], sums[0:NPAD, :].rearrange("(t p b) f -> p t b f", p=P, b=BLK)
                                     [:, :, k, 0], allow_slow_non_contiguous=True).then_inc(got, 16)
                    sp.wait_ge(got, 16 * (4 + BLK))
                    for k in range(BLK):
                        sp.dma_start(deg_d[:, k * P:(k + 1) * P].rearrange("t p -> p t"), degs[:, :, k],
                                     allow_slow_non_contiguous=True).then_inc(copied, 16)
                    sp.wait_ge(copied, 16 * (moves + BLK))
                else:
                    sp.wait_ge(copied, 16 * moves)
                    sp.dma_start(table[0:NPAD, :], sums[0:NPAD, 0:width]).then_inc(copied, 16)
                    sp.wait_ge(copied, 16 * (moves + 1))

            @block.gpsimd
            def _(pool):
                pool.iota(jrow[:, :], pattern=[[0, 1]], base=JUNK, channel_multiplier=1).then_inc(made, 1)
                pool.iota(nowhere[:, :], pattern=[[0, EC]], base=NPAD, channel_multiplier=1).then_inc(made, 1)
                pool.memset(before[:, :], 0.0).then_inc(made, 1)
                pool.memset(ones[:, :], 1.0).then_inc(made, 1)
                pool.memset(rows[:, :], 1.0 if kind == "ones" else 0.0).then_inc(made, 1)
                pool.memset(theirs[:, :], 0.0).then_inc(made, 1)
                pool.wait_ge(made, 6)
                pool.affine_select(out=before[:, :], in_=before[:, :], compare_op=ALU.is_ge, fill=1.0,
                                   base=0, pattern=[[1, P]], channel_multiplier=-1).then_inc(made, 1)
                pool.wait_ge(copied, 16 * (T + (3 if kind != "ones" else 2)))
                with pool.Fori(0, EC) as c:
                    wait_for(pool, aimed, c + 1)
                    if gathers:
                        pool.indirect_dma_start(
                            out=rows[:, :], out_offset=None, in_=table[0:NPAD, :],
                            in_offset=bass.IndirectOffsetOnAxis(ap=s_now[:, :], axis=0),
                            bounds_check=NPAD - 1, oob_is_err=False).then_inc(gathered, 16)
                    if gathers == 2:
                        pool.indirect_dma_start(
                            out=theirs[:, :], out_offset=None, in_=table[0:NPAD, :],
                            in_offset=bass.IndirectOffsetOnAxis(ap=d_now[:, :], axis=0),
                            bounds_check=NPAD - 1, oob_is_err=False).then_inc(gathered, 16)
                    wait_for(pool, parted, c + 1)
                    pool.indirect_dma_start(
                        out=sums, out_offset=bass.IndirectOffsetOnAxis(ap=to_now[:, :], axis=0),
                        in_=part[:, :], in_offset=None, compute_op=ALU.add).then_inc(added, 16)

            @block.tensor
            def _(pe):
                pe.wait_ge(made, 7)
                with pe.Fori(0, EC) as c:
                    pe.wait_ge(spread, c + 1)
                    pe.matmul(bank[0][:, 0:P], d_all[:, :], ident[:, :], start=True, stop=True)\
                      .then_inc(matched, 1)
                    pe.wait_ge(weighed, c + 1)
                    pe.matmul(bank[1][:, 0:width], same[:, :], rows[:, :], start=True, stop=True)\
                      .then_inc(summed, 1)

            @block.scalar
            def _(act):
                if gathers == 2:
                    with act.Fori(0, EC) as c:
                        act.wait_ge(asked, c * 2 + 1)
                        act.activation(att[:, :], att[:, :], ACT.Sigmoid).then_inc(asked, 1)

            @block.vector
            def _(dve):
                dve.memset(zero[:, :], 0.0).then_inc(link, 1)
                dve.memset(si[:, :], NOWHERE)
                dve.wait_ge(made, 7)
                dve.tensor_copy(di[:, :], nowhere[:, :]).then_inc(link, 1)
                dve.tensor_copy(junk[:, :], jrow[:, :]).then_inc(link, 1)
                dve.wait_ge(link, 3)
                dve.memset(ahead[:, :], 0.0).then_inc(filled, 1)
                dve.wait_ge(got, 64)
                links = 7 + (3 if gathers == 2 else 0)
                with dve.Fori(0, EC) as c:
                    at = [0]

                    def then(ins):
                        at[0] += 1
                        ins.then_inc(link, 1)
                        dve.wait_ge(link, c * links + (3 + at[0]))

                    dve.wait_ge(added, c * 16)
                    dve.tensor_copy(s_now[:, :], col(si, c))
                    dve.tensor_copy(d_now[:, :], col(di, c))
                    then(dve.tensor_copy(d_f[:, :], col(di, c)))
                    dve.tensor_scalar(d_all[:, :], ones[:, :], d_f[:, 0:1], None, ALU.mult).then_inc(spread, 1)
                    dve.wait_ge(matched, c + 1)
                    then(dve.tensor_scalar(same[:, :], bank[0][:, 0:P], d_f[:, 0:1], None, ALU.is_equal))
                    then(dve.tensor_tensor(scrap[:, :], same[:, :], before[:, :], ALU.mult))
                    then(dve.tensor_reduce(ahead[:, :], scrap[:, :], AX_X, ALU.add))
                    dve.tensor_scalar(ahead[:, :], ahead[:, :], 0.0, None, ALU.is_gt)
                    then(dve.tensor_tensor(move[:, :], junk[:, :], d_f[:, :], ALU.subtract))
                    then(dve.tensor_tensor(move[:, :], move[:, :], ahead[:, :], ALU.mult))
                    then(dve.tensor_tensor(move[:, :], move[:, :], d_f[:, :], ALU.add))
                    dve.tensor_copy(to_now[:, :], move[:, :]).then_inc(aimed, 1)
                    if gathers:
                        dve.wait_ge(gathered, c * (16 * gathers) + 16 * gathers)
                    if gathers == 2:
                        dve.tensor_tensor(att[:, :], rows[:, D:D + 1], theirs[:, D + 1:D + 2], ALU.add)\
                           .then_inc(asked, 1)
                        dve.wait_ge(asked, c * 2 + 2)
                        then(dve.tensor_scalar(rows[:, :], rows[:, :], att[:, 0:1], None, ALU.mult))
                        then(dve.memset(rows[:, D:MW], 0.0))
                        then(dve.memset(rows[:, D:D + 1], 1e30))
                    dve.memset(scrap[:, 0:1], 0.0).then_inc(weighed, 1)
                    dve.wait_ge(summed, c + 1)
                    dve.tensor_copy(part[:, :], bank[1][:, 0:width]).then_inc(parted, 1)

    def count_degrees():
        with ExitStack() as ctx:
            ph = Phase(ctx, "deg")
            onehot = ph.pair("onehot", [P, CH, GRP], F32R)
            ones = ph.tile("ones", [P, P], F32R)
            row = ph.pair("row", [1, GRP])
            begun, made, counted = ph.sem("begun"), ph.sem("onehots"), ph.sem("counted")
            copied, stored = ph.sem("copied"), ph.sems("stored")
            block = ctx.enter_context(nc.Block())

            @block.vector
            def _(dve):
                dve.tensor_scalar(ones[:, :], iota[:, 0:P], 0.0, 1.0, ALU.mult, ALU.add).then_inc(begun, 1)

                def onehots(q):
                    if not is_first(q.t):
                        dve.wait_ge(counted, q.t - 1)
                    for k in range(CH):
                        last = dve.tensor_scalar(onehot[q.u][:, k, :], iota[:, :],
                                                 col(dcol, q.t * CH + k), None, ALU.is_equal)
                    last.then_inc(made, 1)

                over_groups(dve, [(0, onehots)])

            @block.tensor
            def _(pe):
                pe.wait_ge(begun, 1)

                def count(q):
                    pe.wait_ge(made, q.t + 1)
                    if not is_first(q.t):
                        pe.wait_ge(copied, q.t - 1)
                    for k in range(CH):
                        last = pe.matmul(bank[q.u][:, :], ones[:, :], onehot[q.u][:, k, :],
                                         start=(k == 0), stop=(k == CH - 1))
                    last.then_inc(counted, 1)

                over_groups(pe, [(0, count)])

            @block.scalar
            def _(act):
                def add_own(q):
                    act.wait_ge(counted, q.t + 1)
                    if not is_first(q.t):
                        act.wait_ge(stored[q.u], q.n * 16)
                    act.activation(row[q.u][0:1, :], bank[q.u][0:1, :], ACT.Identity, bias=own[0:1, 0:1])\
                       .then_inc(copied, 1)

                over_groups(act, [(0, add_own)])

            @block.sync
            def _(sp):
                over_groups(sp, [(0, lambda q: store(sp, q, deg_d[bass.ds(q.t, 1), :], row[q.u][0:1, :],
                                                     copied, stored))])
                all_stored(sp, stored)

    def scale_degrees():
        with ExitStack() as ctx:
            ph = Phase(ctx, "scl")
            deg = ph.tile("deg", [T, GRP])
            a = ph.tile("a", [T, GRP])
            b = ph.tile("b", [T, GRP])
            root = ph.tile("root", [T, GRP])
            got, rooted, made = ph.sem("got"), ph.sem("rooted"), ph.sem("made")
            turned, kept, link = ph.sem("turned"), ph.sem("kept"), ph.sem("link")
            block = ctx.enter_context(nc.Block())

            @block.sync
            def _(sp):
                sp.dma_start(deg[:, :], deg_d).then_inc(got, 16)
                sp.wait_ge(made, 2)
                sp.dma_start(dinv_d, root[:, :]).then_inc(kept, 16)
                sp.dma_start(inv_d, b[:, :]).then_inc(kept, 16)
                sp.wait_ge(kept, 32)

            @block.scalar
            def _(act):
                act.wait_ge(rooted, 1)
                act.activation(root[:, :], a[:, :], ACT.Sqrt).then_inc(rooted, 1)

            @block.tensor
            def _(pe):
                pe.wait_ge(made, 2)
                for i, tile in enumerate((root, b)):
                    for k in range(BLK):
                        last = pe.transpose(bank[i * BLK + k][:, 0:T], tile[:, k * P:(k + 1) * P],
                                            ident[0:T, 0:T])
                last.then_inc(turned, 1)

            @block.vector
            def _(dve):
                steps = [0]

                def then(ins):
                    steps[0] += 1
                    ins.then_inc(link, 1)
                    dve.wait_ge(link, steps[0])

                dve.wait_ge(got, 16)
                dve.tensor_scalar(a[:, :], deg[:, :], 1.0, None, ALU.add).then_inc(rooted, 1)
                then(dve.tensor_scalar(b[:, :], deg[:, :], 1.0, None, ALU.max))
                then(dve.reciprocal(b[:, :], b[:, :]))
                then(dve.scalar_tensor_tensor(out=b[:, :], in0=deg[:, :], scalar=0.0, in1=b[:, :],
                                              op0=ALU.is_gt, op1=ALU.mult))
                dve.wait_ge(rooted, 2)
                then(dve.reciprocal(root[:, :], root[:, :]))
                dve.memset(bn_mv[:, :], 0.0).then_inc(made, 2)
                dve.wait_ge(turned, 1)
                for i, tile in enumerate((dinv_n, inv_n)):
                    for k in range(BLK):
                        dve.tensor_copy(tile[:, :].rearrange("p (t b) -> p t b", b=BLK)[:, :, k],
                                        bank[i * BLK + k][:, 0:T])
                then(dve.memset(bn_mv[:, :], 0.0))
                dve.tensor_scalar(dinv2_n[:, :], dinv_n[:, :], own1[:, 0:1], None, ALU.mult)
                dve.tensor_scalar(selfinv_n[:, :], inv_n[:, :], own[:, 0:1], None, ALU.mult)

    def scale_x():
        with ExitStack() as ctx:
            ph = Phase(ctx, "sx")
            xin, xout = ph.pair("in", [P, GRP], n=4), ph.pair("out", [P, GRP], n=4)
            loaded, scaled, stored = ph.sems("loaded", 4), ph.sem("scaled"), ph.sems("stored", 4)
            block = ctx.enter_context(nc.Block())

            @block.sync
            def _(sp):
                over_groups(sp, [(0, lambda q: load_x(sp, q, xin, loaded, scaled)),
                                 (3, lambda q: store(sp, q, group_of(t_x0[0:NPAD, :], q.t), xout[q.r][:, :],
                                                     scaled, stored))])
                all_stored(sp, stored)

            @block.scalar
            def _(act):
                def scale(q):
                    act.wait_ge(loaded[q.r], q.m * 16 + 16)
                    if not is_first(q.t, 4):
                        act.wait_ge(stored[q.r], q.m * 16)
                    for b in range(BLK):
                        last = act.activation(xout[q.r][:, b * D:(b + 1) * D], xin[q.r][:, b * D:(b + 1) * D],
                                              ACT.Copy, scale=col(dinv_n, q.t * BLK + b))
                    last.then_inc(scaled, 1)

                over_groups(act, [(0, scale)])

    def load_x(sp, q, to, loaded, free):
        if isinstance(q.t, int) and q.t == T - 1:
            load(sp, q, to[q.d % len(to)][0:LASTP, :],
                 x[(T - 1) * GRP:NODES, :].rearrange("(p b) f -> p (b f)", b=BLK),
                 loaded[q.d % len(to)], free, len(to))
        else:
            load(sp, q, to[q.d % len(to)][:, :], group_of(x[0:(T - 1) * GRP, :], q.t),
                 loaded[q.d % len(to)], free, len(to))

    def gcn_first():
        with ExitStack() as ctx:
            ph = Phase(ctx, "g1")
            e = EdgeRows(ph, t_x0, D, CH)
            own_rows, xin = ph.pair("own", [P, GRP]), ph.pair("x", [P, GRP])
            scale_row = ph.pair("scale", [P, GRP])
            agg = ph.pair("agg", [P, GRP])
            hid = ph.pair("hid", [P, 2, GRP])
            hout, rout = ph.pair("hout", [P, GRP]), ph.pair("rout", [P, GRP])
            loaded, loaded_x = ph.sems("loaded"), ph.sems("loaded_x")
            agged, relued, scaled, rested = ph.sem("agged"), ph.sem("relued"), ph.sem("scaled"), ph.sem("rested")
            hidden, lowered, link = ph.sem("hidden"), ph.sem("lowered"), ph.sem("link")
            st_h, st_r = ph.sems("stored_h"), ph.sems("stored_r")
            block = ctx.enter_context(nc.Block())

            @block.gpsimd
            def _(pool):
                over_groups(pool, [(0, lambda q: e.gather(pool, q))])

            @block.sync
            def _(sp):
                def loads(q):
                    load(sp, q, own_rows[q.u][:, :], own_group(t_x0, q.t), loaded[q.u], e.summed)
                    load(sp, q, scale_row[q.u][:, :], row_of(dinv_d, q.t), loaded[q.u], agged)

                over_groups(sp, [
                    (0, loads),
                    (3, lambda q: load_x(sp, q, xin, loaded_x, rested)),
                    (4, lambda q: store(sp, q, group_of(t_h0[0:NPAD, :], q.t), hout[q.u][:, :], scaled, st_h)),
                    (5, lambda q: store(sp, q, group_of(r1, q.t), rout[q.u][:, :], rested, st_r))])
                all_stored(sp, st_h, st_r)

            @block.tensor
            def _(pe):
                def sums(q):
                    pe.wait_ge(e.ready, q.t + 1)
                    pe.wait_ge(loaded[q.u], q.n * 32 + 32)
                    if not is_first(q.t):
                        pe.wait_ge(agged, q.t - 1)
                    e.sum_by_feature(pe, q, [bank[q.u]], close=False)
                    for b in range(BLK):
                        last = pe.matmul(bank[q.u][:, b * P:(b + 1) * P], own_rows[q.u][:, b * D:(b + 1) * D],
                                         id_own1[:, :], start=False, stop=(b == BLK - 1),
                                         skip_group_check=True)
                    last.then_inc(e.summed, 1)

                def up(q):
                    pe.wait_ge(agged, q.t + 1)
                    if not (isinstance(q.t, int) and q.t < 1):
                        pe.wait_ge(relued, q.t)
                    for h in range(2):
                        last = pe.matmul(bank[2 + h][:, :], w1_s[:, h * P:(h + 1) * P], agg[q.u][:, :],
                                         start=True, stop=True)
                    last.then_inc(hidden, 1)

                def down(q):
                    pe.wait_ge(relued, q.t + 1)
                    if not is_first(q.t):
                        pe.wait_ge(scaled, q.t - 1)
                    for b in range(BLK):
                        for h in range(2):
                            last = pe.matmul(bank[4 + q.u][:, b * D:(b + 1) * D],
                                             hid[q.u][:, h, b * P:(b + 1) * P], w2_s[:, h, :],
                                             start=(h == 0), stop=(h == 1), skip_group_check=True)
                    last.then_inc(lowered, 1)

                over_groups(pe, [(1, sums), (2, up), (3, down)])

            @block.scalar
            def _(act):
                def relu(q):
                    act.wait_ge(hidden, q.t + 1)
                    if not is_first(q.t):
                        act.wait_ge(lowered, q.t - 1)
                    for h in range(2):
                        last = act.activation(hid[q.u][:, h, :], bank[2 + h][:, :], ACT.Relu,
                                              bias=b1_c[:, h:h + 1])
                    last.then_inc(relued, 1)

                def scale(q):
                    act.wait_ge(lowered, q.t + 1)
                    if not is_first(q.t):
                        act.wait_ge(st_h[q.u], q.n * 16)
                        act.wait_ge(rested, q.t - 1)
                    for b in range(BLK):
                        last = act.activation(hout[q.u][:, b * D:(b + 1) * D],
                                              bank[4 + q.u][:, b * D:(b + 1) * D], ACT.Copy,
                                              scale=col(dinv_n, q.t * BLK + b))
                    last.then_inc(scaled, 1)

                over_groups(act, [(0, lambda q: e.take_hi(act, q)), (2, relu), (3, scale)])

            @block.vector
            def _(dve):
                def scale_sums(q):
                    dve.wait_ge(e.summed, q.t + 1)
                    if not is_first(q.t):
                        dve.wait_ge(hidden, q.t - 1)
                    dve.tensor_tensor(agg[q.u][:, :], bank[q.u][:, :], scale_row[q.u][:, :], ALU.mult)\
                       .then_inc(agged, 1)

                def rest(q):
                    dve.wait_ge(scaled, q.t + 1)
                    dve.wait_ge(loaded_x[q.u], q.n * 16 + 16)
                    if not is_first(q.t):
                        dve.wait_ge(st_r[q.u], q.n * 16)
                    for b in range(BLK):
                        f = slice(b * D, (b + 1) * D)
                        last = dve.scalar_tensor_tensor(out=rout[q.u][:, f], in0=hout[q.u][:, f],
                                                        scalar=col(dinv2_n, q.t * BLK + b),
                                                        in1=xin[q.u][:, f], op0=ALU.mult, op1=ALU.add)
                    last.then_inc(link, 1)
                    dve.wait_ge(link, q.t + 1)
                    dve.tensor_tensor(rout[q.u][:, :], rout[q.u][:, :],
                                      b2_r[:, :, :].rearrange("p b f -> p (b f)"), ALU.add)\
                       .then_inc(rested, 1)

                over_groups(dve, [(0, lambda q: e.prepare(dve, q)), (1, scale_sums), (4, rest)])

    def gcn_second():
        with ExitStack() as ctx:
            ph = Phase(ctx, "g2")
            e = EdgeRows(ph, t_h0, D, CH)
            ln = LayerNorm(ph)
            rest, z, xout = ph.pair("rest", [P, GRP]), ph.pair("z", [P, GRP], n=4), ph.pair("xout", [P, GRP])
            loaded, added, stored = ph.sems("loaded"), ph.sem("added"), ph.sems("stored")
            block = ctx.enter_context(nc.Block())

            @block.gpsimd
            def _(pool):
                over_groups(pool, [(0, lambda q: e.gather(pool, q))])

            @block.sync
            def _(sp):
                over_groups(sp, [
                    (0, lambda q: load(sp, q, rest[q.u][:, :], group_of(r1, q.t), loaded[q.u], added)),
                    (5, lambda q: store(sp, q, group_of(t_x1[0:NPAD, :], q.t), xout[q.u][:, :], ln.applied,
                                        stored))])
                all_stored(sp, stored)

            @block.tensor
            def _(pe):
                def sums(q):
                    pe.wait_ge(e.ready, q.t + 1)
                    if not is_first(q.t):
                        pe.wait_ge(added, q.t - 1)
                    e.sum_by_node(pe, q, bank[q.u]).then_inc(e.summed, 1)

                over_groups(pe, [(1, sums)])

            @block.scalar
            def _(act):
                def apply(q):
                    if not is_first(q.t):
                        act.wait_ge(stored[q.u], q.n * 16)
                    ln.normalise(act, q, xout[q.u], z[q.r])

                over_groups(act, [(0, lambda q: e.take_hi(act, q)), (3, lambda q: ln.root(act, q)),
                                  (4, apply)])

            @block.vector
            def _(dve):
                def add(q):
                    dve.wait_ge(e.summed, q.t + 1)
                    dve.wait_ge(loaded[q.u], q.n * 16 + 16)
                    if not is_first(q.t, 4):
                        dve.wait_ge(ln.applied, q.t - 3)
                    for b in range(BLK):
                        f = slice(b * D, (b + 1) * D)
                        last = dve.scalar_tensor_tensor(out=z[q.r][:, f], in0=bank[q.u][:, f],
                                                        scalar=col(dinv_n, q.t * BLK + b),
                                                        in1=rest[q.u][:, f], op0=ALU.mult, op1=ALU.add)
                    last.then_inc(added, 1)
                    dve.wait_ge(added, q.t + 1)
                    ln.take_stats(dve, q, z[q.r])

                over_groups(dve, [(0, lambda q: e.prepare(dve, q)), (2, add), (3, lambda q: ln.invert(dve, q))])

    def sage_first():
        with ExitStack() as ctx:
            ph = Phase(ctx, "s1")
            e = EdgeRows(ph, t_x1, D, CH)
            own_rows, scale_row = ph.pair("own", [P, GRP]), ph.pair("scale", [P, GRP])
            xt, agg = ph.pair("xt", [P, GRP]), ph.pair("agg", [P, GRP])
            pre, hout = ph.pair("pre", [P, BLK * HID]), ph.pair("hout", [P, BLK * HID])
            loaded, turned, agged, link = ph.sems("loaded"), ph.sem("turned"), ph.sem("agged"), ph.sem("link")
            hidden, biased, relued, stored = ph.sem("hidden"), ph.sem("biased"), ph.sem("relued"), ph.sems("stored")
            block = ctx.enter_context(nc.Block())

            @block.gpsimd
            def _(pool):
                over_groups(pool, [(0, lambda q: e.gather(pool, q))])

            @block.sync
            def _(sp):
                def loads(q):
                    load(sp, q, own_rows[q.u][:, :], own_group(t_x1, q.t), loaded[q.u], e.summed)
                    load(sp, q, scale_row[q.u][:, :], row_of(inv_d, q.t), loaded[q.u], agged)

                over_groups(sp, [
                    (0, loads),
                    (3, lambda q: store(sp, q, group_of(t_h[0:NPAD, :], q.t), hout[q.u][:, :], relued, stored))])
                all_stored(sp, stored)

            @block.tensor
            def _(pe):
                def sums(q):
                    pe.wait_ge(e.ready, q.t + 1)
                    pe.wait_ge(loaded[q.u], q.n * 32 + 32)
                    if not is_first(q.t):
                        pe.wait_ge(agged, q.t - 1)
                    e.sum_by_feature(pe, q, [bank[q.u]])
                    for b in range(BLK):
                        last = pe.transpose(bank[2 + q.u][:, b * P:(b + 1) * P],
                                            own_rows[q.u][:, b * D:(b + 1) * D], ident[:, :])
                    last.then_inc(e.summed, 1)

                def dense(q):
                    pe.wait_ge(agged, q.t + 1)
                    if not (isinstance(q.t, int) and q.t < 1):
                        pe.wait_ge(biased, q.t)
                    for b in range(BLK):
                        to = bank[4 + b // 2][:, (b % 2) * HID:(b % 2 + 1) * HID]
                        pe.matmul(to, xt[q.u][:, b * P:(b + 1) * P], ws0_s[:, :], start=True, stop=False,
                                  skip_group_check=True)
                        last = pe.matmul(to, agg[q.u][:, b * P:(b + 1) * P], wn0_s[:, :], start=False,
                                         stop=True, skip_group_check=True)
                    last.then_inc(hidden, 1)

                over_groups(pe, [(1, sums), (2, dense)])

            @block.scalar
            def _(act):
                def turn(q):
                    act.wait_ge(e.summed, q.t + 1)
                    if not is_first(q.t):
                        act.wait_ge(hidden, q.t - 1)
                    act.activation(xt[q.u][:, :], bank[2 + q.u][:, :], ACT.Copy).then_inc(turned, 1)

                def relu(q):
                    act.wait_ge(biased, q.t + 1)
                    if not is_first(q.t):
                        act.wait_ge(stored[q.u], q.n * 16)
                    act.activation(hout[q.u][:, :], pre[q.u][:, :], ACT.Relu).then_inc(relued, 1)

                over_groups(act, [(0, lambda q: e.take_hi(act, q)), (1, turn), (2, relu)])

            @block.vector
            def _(dve):
                def mean(q):
                    dve.wait_ge(turned, q.t + 1)
                    dve.scalar_tensor_tensor(out=agg[q.u][:, :], in0=xt[q.u][:, :], scalar=own[:, 0:1],
                                             in1=bank[q.u][:, :], op0=ALU.mult, op1=ALU.add)\
                       .then_inc(link, 1)
                    dve.wait_ge(link, q.t + 1)
                    dve.tensor_tensor(agg[q.u][:, :], agg[q.u][:, :], scale_row[q.u][:, :], ALU.mult)\
                       .then_inc(agged, 1)

                def bias(q):
                    dve.wait_ge(hidden, q.t + 1)
                    if not is_first(q.t):
                        dve.wait_ge(relued, q.t - 1)
                    for i in range(2):
                        last = dve.tensor_tensor(pre[q.u][:, i * 512:(i + 1) * 512], bank[4 + i][:, :],
                                                 sb0_r[:, :, :].rearrange("p b f -> p (b f)"), ALU.add)
                    last.then_inc(biased, 1)

                over_groups(dve, [(0, lambda q: e.prepare(dve, q)), (1, mean), (2, bias)])

    def sage_second():
        with ExitStack() as ctx:
            ph = Phase(ctx, "s2")
            e = EdgeRows(ph, t_h, HID, CH)
            own_rows, scale_row = ph.pair("own", [P, BLK * HID]), ph.pair("scale", [P, GRP])
            xin = ph.pair("x", [P, GRP])
            ht, agg = ph.pair("ht", [P, 2, GRP]), ph.pair("agg", [P, 2, GRP])
            hid = ph.pair("hid", [P, 2, GRP])
            vout, rout = ph.pair("vout", [P, GRP]), ph.pair("rout", [P, GRP])
            loaded, loaded_x = ph.sems("loaded"), ph.sems("loaded_x")
            turned, agged, link, link2 = ph.sem("turned"), ph.sem("agged"), ph.sem("link"), ph.sem("link2")
            hidden, relued, lowered = ph.sem("hidden"), ph.sem("relued"), ph.sem("lowered")
            kept, added, rested = ph.sem("kept"), ph.sem("added"), ph.sem("rested")
            st_v, st_r = ph.sems("stored_v"), ph.sems("stored_r")
            block = ctx.enter_context(nc.Block())

            @block.gpsimd
            def _(pool):
                over_groups(pool, [(0, lambda q: e.gather(pool, q))])

            @block.sync
            def _(sp):
                def loads(q):
                    load(sp, q, own_rows[q.u][:, :], own_group(t_h, q.t), loaded[q.u], e.summed)
                    load(sp, q, scale_row[q.u][:, :], row_of(inv_d, q.t), loaded[q.u], agged)

                over_groups(sp, [
                    (0, loads),
                    (2, lambda q: load(sp, q, xin[q.u][:, :], own_group(t_x1, q.t), loaded_x[q.u],
                                       rested)),
                    (3, lambda q: store(sp, q, group_of(t_v[0:NPAD, :], q.t), vout[q.u][:, :], kept, st_v)),
                    (3, lambda q: store(sp, q, group_of(r2, q.t), rout[q.u][:, :], rested, st_r))])
                all_stored(sp, st_v, st_r)

            @block.tensor
            def _(pe):
                def sums(q):
                    pe.wait_ge(e.ready, q.t + 1)
                    pe.wait_ge(loaded[q.u], q.n * 32 + 32)
                    if not (isinstance(q.t, int) and q.t < 1):
                        pe.wait_ge(agged, q.t)
                    e.sum_by_feature(pe, q, [bank[0], bank[1]])
                    for h in range(2):
                        for b in range(BLK):
                            last = pe.transpose(bank[2 + h][:, b * P:(b + 1) * P],
                                                own_rows[q.u][:, b * HID + h * P:b * HID + (h + 1) * P],
                                                ident[:, :])
                    last.then_inc(e.summed, 1)

                def across(q):
                    pe.wait_ge(agged, q.t + 1)
                    if not (isinstance(q.t, int) and q.t < 1):
                        pe.wait_ge(relued, q.t)
                    for o in range(2):
                        for k, (w, r) in enumerate(((ws1_s, ht), (wn1_s, agg))):
                            for h in range(2):
                                last = pe.matmul(bank[4 + o][:, :], w[:, h, o * P:(o + 1) * P], r[q.u][:, h, :],
                                                 start=(k + h == 0), stop=(k + h == 2))
                    last.then_inc(hidden, 1)

                def down(q):
                    pe.wait_ge(relued, q.t + 1)
                    if not (isinstance(q.t, int) and q.t < 1):
                        pe.wait_ge(kept, q.t)
                        pe.wait_ge(added, q.t)
                    for w in range(2):
                        for b in range(BLK):
                            for h in range(2):
                                last = pe.matmul(bank[6 + w][:, b * D:(b + 1) * D],
                                                 hid[q.u][:, h, b * P:(b + 1) * P],
                                                 wuv_s[:, h, w * D:(w + 1) * D],
                                                 start=(h == 0), stop=(h == 1), skip_group_check=True)
                    last.then_inc(lowered, 1)

                over_groups(pe, [(1, sums), (2, across), (3, down)])

            @block.scalar
            def _(act):
                def turn(q):
                    act.wait_ge(e.summed, q.t + 1)
                    if not is_first(q.t):
                        act.wait_ge(hidden, q.t - 1)
                    for h in range(2):
                        last = act.activation(ht[q.u][:, h, :], bank[2 + h][:, :], ACT.Copy)
                    last.then_inc(turned, 1)

                def relu(q):
                    act.wait_ge(hidden, q.t + 1)
                    if not is_first(q.t):
                        act.wait_ge(lowered, q.t - 1)
                    for h in range(2):
                        last = act.activation(hid[q.u][:, h, :], bank[4 + h][:, :], ACT.Relu,
                                              bias=sb1_c[:, h:h + 1])
                    last.then_inc(relued, 1)

                def keep(q):
                    act.wait_ge(lowered, q.t + 1)
                    if not is_first(q.t):
                        act.wait_ge(st_v[q.u], q.n * 16)
                        act.wait_ge(rested, q.t - 1)
                    act.activation(vout[q.u][:, :], bank[7][:, :], ACT.Copy).then_inc(kept, 1)

                over_groups(act, [(0, lambda q: e.take_hi(act, q)), (1, turn), (2, relu), (3, keep)])

            @block.vector
            def _(dve):
                def mean(q):
                    dve.wait_ge(turned, q.t + 1)
                    for h in range(2):
                        last = dve.scalar_tensor_tensor(out=agg[q.u][:, h, :], in0=ht[q.u][:, h, :],
                                                        scalar=own[:, 0:1], in1=bank[h][:, :],
                                                        op0=ALU.mult, op1=ALU.add)
                    last.then_inc(link, 1)
                    dve.wait_ge(link, q.t + 1)
                    for h in range(2):
                        last = dve.tensor_tensor(agg[q.u][:, h, :], agg[q.u][:, h, :], scale_row[q.u][:, :],
                                                 ALU.mult)
                    last.then_inc(agged, 1)

                def rest(q):
                    dve.wait_ge(lowered, q.t + 1)
                    dve.wait_ge(loaded_x[q.u], q.n * 16 + 16)
                    if not is_first(q.t):
                        dve.wait_ge(st_r[q.u], q.n * 16)
                    dve.tensor_tensor(rout[q.u][:, :], bank[6][:, :], xin[q.u][:, :], ALU.add)\
                       .then_inc(added, 1)
                    dve.wait_ge(added, q.t + 1)
                    dve.tensor_tensor(rout[q.u][:, :], rout[q.u][:, :],
                                      sb2_r[:, :, :].rearrange("p b f -> p (b f)"), ALU.add)\
                       .then_inc(link2, 1)
                    dve.wait_ge(link2, q.t + 1)
                    dve.wait_ge(kept, q.t + 1)
                    for b in range(BLK):
                        f = slice(b * D, (b + 1) * D)
                        last = dve.scalar_tensor_tensor(out=rout[q.u][:, f], in0=vout[q.u][:, f],
                                                        scalar=col(selfinv_n, q.t * BLK + b),
                                                        in1=rout[q.u][:, f], op0=ALU.mult, op1=ALU.add)
                    last.then_inc(rested, 1)

                over_groups(dve, [(0, lambda q: e.prepare(dve, q)), (1, mean), (3, rest)])

    def sage_third():
        with ExitStack() as ctx:
            ph = Phase(ctx, "s3")
            e = EdgeRows(ph, t_v, D, CH)
            ln = LayerNorm(ph)
            rest, z, x2 = ph.pair("rest", [P, GRP]), ph.pair("z", [P, GRP], n=4), ph.pair("x2", [P, GRP])
            xt, mout = ph.pair("xt", [P, GRP]), ph.pair("mout", [P, BLK * MW])
            loaded, added, turned = ph.sems("loaded"), ph.sem("added"), ph.sem("turned")
            held, timed, biased = ph.sem("held"), ph.sem("timed"), ph.sem("biased")
            st_x, st_m = ph.sems("stored_x"), ph.sems("stored_m")
            block = ctx.enter_context(nc.Block())

            @block.gpsimd
            def _(pool):
                over_groups(pool, [(0, lambda q: e.gather(pool, q))])

            @block.sync
            def _(sp):
                over_groups(sp, [
                    (0, lambda q: load(sp, q, rest[q.u][:, :], group_of(r2, q.t), loaded[q.u], added)),
                    (6, lambda q: store(sp, q, slab_of(x2t, q.t), xt[q.u][:, :], held, st_x)),
                    (8, lambda q: store(sp, q, group_of(t_m[0:NPAD, :], q.t), mout[q.u][:, :], biased, st_m))])
                all_stored(sp, st_x, st_m)

            @block.tensor
            def _(pe):
                def sums(q):
                    pe.wait_ge(e.ready, q.t + 1)
                    if not is_first(q.t):
                        pe.wait_ge(added, q.t - 1)
                    e.sum_by_node(pe, q, bank[q.u]).then_inc(e.summed, 1)

                def turn(q):
                    pe.wait_ge(ln.applied, q.t + 1)
                    if not is_first(q.t):
                        pe.wait_ge(held, q.t - 1)
                    for b in range(BLK):
                        last = pe.transpose(bank[2 + q.u][:, b * P:(b + 1) * P],
                                            x2[q.u][:, b * D:(b + 1) * D], ident[:, :])
                    last.then_inc(turned, 1)

                def message(q):
                    pe.wait_ge(held, q.t + 1)
                    if not is_first(q.t):
                        pe.wait_ge(biased, q.t - 1)
                    for b in range(BLK):
                        last = pe.matmul(bank[4 + 2 * q.u + b // 2][:, (b % 2) * MW:(b % 2 + 1) * MW],
                                         xt[q.u][:, b * P:(b + 1) * P], wm_s[:, :], start=True, stop=True,
                                         skip_group_check=True)
                    last.then_inc(timed, 1)

                over_groups(pe, [(5, turn), (1, sums), (6, message)])

            @block.scalar
            def _(act):
                def apply(q):
                    if not is_first(q.t):
                        act.wait_ge(turned, q.t - 1)
                    ln.normalise(act, q, x2[q.u], z[q.r])

                def hold(q):
                    act.wait_ge(turned, q.t + 1)
                    if not is_first(q.t):
                        act.wait_ge(st_x[q.u], q.n * 16)
                        act.wait_ge(timed, q.t - 1)
                    act.activation(xt[q.u][:, :], bank[2 + q.u][:, :], ACT.Copy).then_inc(held, 1)

                over_groups(act, [(0, lambda q: e.take_hi(act, q)), (3, lambda q: ln.root(act, q)),
                                  (4, apply), (5, hold)])

            @block.vector
            def _(dve):
                def add(q):
                    dve.wait_ge(e.summed, q.t + 1)
                    dve.wait_ge(loaded[q.u], q.n * 16 + 16)
                    if not is_first(q.t, 4):
                        dve.wait_ge(ln.applied, q.t - 3)
                    for b in range(BLK):
                        f = slice(b * D, (b + 1) * D)
                        last = dve.scalar_tensor_tensor(out=z[q.r][:, f], in0=bank[q.u][:, f],
                                                        scalar=col(inv_n, q.t * BLK + b),
                                                        in1=rest[q.u][:, f], op0=ALU.mult, op1=ALU.add)
                    last.then_inc(added, 1)
                    dve.wait_ge(added, q.t + 1)
                    ln.take_stats(dve, q, z[q.r])

                def bias(q):
                    dve.wait_ge(timed, q.t + 1)
                    if not is_first(q.t):
                        dve.wait_ge(st_m[q.u], q.n * 16)
                    for i in range(2):
                        last = dve.tensor_tensor(mout[q.u][:, i * 2 * MW:(i + 1) * 2 * MW],
                                                 bank[4 + 2 * q.u + i][:, 0:2 * MW],
                                                 bm_r[:, :, :].rearrange("p b f -> p (b f)"), ALU.add)
                    last.then_inc(biased, 1)

                over_groups(dve, [(0, lambda q: e.prepare(dve, q)), (2, add),
                                  (3, lambda q: ln.invert(dve, q)), (7, bias)])

    def attend():
        XS = 8
        with ExitStack() as ctx:
            ph = Phase(ctx, "at")
            e = EdgeRows(ph, t_m, MW, CH + BLK, hots=4)
            x2 = ph.pair("x2", [P, GRP], n=XS)
            own_rows = ph.pair("own", [P, BLK * MW])
            scrap = ph.tile("scrap", [P, CH, GRP])
            term = ph.pair("term", [P, CH])
            logit, att = ph.pair("logit", [P, CH + BLK]), ph.pair("att", [P, CH + BLK])
            msg = ph.pair("msg", [P, CH + BLK, D])
            agg = ph.pair("agg", [P, GRP])
            r, zg, mix, ng = (ph.pair(n, [P, GRP]) for n in ("r", "z", "mix", "n"))
            hn = ph.pair("hn", [P, GRP])
            loaded_x, loaded_m = ph.sems("loaded_x", XS), ph.sems("loaded_m")
            asked, dotted, linked, weighed = ph.sem("asked"), ph.sem("dotted"), ph.sem("linked"), ph.sem("weighed")
            gated, mailed, agged = ph.sem("gated"), ph.sem("mailed"), ph.sem("agged")
            crossed, opened, mixed, tanhed = ph.sem("crossed"), ph.sem("opened"), ph.sem("mixed"), ph.sem("tanhed")
            link, link3, moved = ph.sem("link"), ph.sem("link3"), ph.sem("moved")
            stored = ph.sems("stored")
            block = ctx.enter_context(nc.Block())

            @block.gpsimd
            def _(pool):
                over_groups(pool, [(0, lambda q: e.gather(pool, q, used=mailed))])

            @block.sync
            def _(sp):
                def loads(q):
                    v = q.use(XS)
                    s = q.d % XS
                    load(sp, q, x2[s][:, :], slab_of(x2t, q.t), loaded_x[s], moved, XS)
                    load(sp, q, own_rows[q.u][:, :], own_group(t_m, q.t), loaded_m[q.u], mailed)

                over_groups(sp, [(0, loads),
                                 (5, lambda q: store(sp, q, slab_of(hnt, q.t), hn[q.u][:, :], moved, stored))],
                            XS)
                all_stored(sp, stored)

            @block.tensor
            def _(pe):
                def ask(q):
                    pe.wait_ge(loaded_x[q.d % XS], q.use(XS) * 16 + 16)
                    if not is_first(q.t):
                        pe.wait_ge(dotted, q.t - 1)
                    pe.matmul(bank[2 + 5 * q.u][:, :], wad_s[:, :], x2[q.d % XS][:, :], start=True, stop=True)\
                      .then_inc(asked, 1)

                def sums(q):
                    pe.wait_ge(e.ready, q.t + 1)
                    if not is_first(q.t):
                        pe.wait_ge(agged, q.t - 1)
                    e.sum_by_feature(pe, q, [bank[q.u]], close=False)
                    for b in range(BLK):
                        for part in (e.hi, e.lo):
                            last = pe.matmul(bank[q.u][:, b * P:(b + 1) * P], part[q.u][:, CH + b, :],
                                             id_own_r[:, :], start=False, skip_group_check=True,
                                             stop=(b == BLK - 1 and part is e.lo))
                    last.then_inc(e.summed, 1)

                def gates(q):
                    pe.wait_ge(agged, q.t + 1)
                    if not (isinstance(q.t, int) and q.t < 1):
                        pe.wait_ge(opened, q.t)
                        pe.wait_ge(mixed, q.t)
                    xq = x2[q.d % XS]
                    for g in range(2):
                        f = slice(g * P, (g + 1) * P)
                        pe.matmul(bank[3 + g][:, :], wih_s[:, f], agg[q.u][:, :], start=True, stop=False)
                        pe.matmul(bank[3 + g][:, :], whh_s[:, f], xq[:, :], start=False, stop=True)
                    f = slice(2 * P, 3 * P)
                    pe.matmul(bank[5][:, :], whh_s[:, f], xq[:, :], start=True, stop=True)
                    pe.matmul(bank[6][:, :], wih_s[:, f], agg[q.u][:, :], start=True, stop=True)\
                      .then_inc(crossed, 1)

                over_groups(pe, [(4, gates), (3, sums), (0, ask)], XS)

            @block.scalar
            def _(act):
                def weigh(q):
                    act.wait_ge(gated, q.t + 1)
                    act.activation(att[q.u][:, :], logit[q.u][:, :], ACT.Sigmoid).then_inc(weighed, 1)
                    act.wait_ge(weighed, q.t + 1)
                    if not is_first(q.t):
                        act.wait_ge(e.ready, q.t - 1)
                    for k in range(CH):
                        act.activation(msg[q.u][:, k, :], e.rows[q.r][:, k, 0:D], ACT.Copy,
                                       scale=att[q.u][:, k:k + 1])
                    for b in range(BLK):
                        last = act.activation(msg[q.u][:, CH + b, :], own_rows[q.u][:, b * MW:b * MW + D],
                                              ACT.Copy, scale=att[q.u][:, CH + b:CH + b + 1])
                    last.then_inc(mailed, 1)
                    act.wait_ge(mailed, q.t + 1)
                    e.free(act, q)
                    act.activation(e.hi[q.u][:, :, :], msg[q.u][:, :, :], ACT.Copy).then_inc(e.split, 1)

                def hold(q):
                    act.wait_ge(e.summed, q.t + 1)
                    if not is_first(q.t):
                        act.wait_ge(crossed, q.t - 1)
                    act.activation(agg[q.u][:, :], bank[q.u][:, :], ACT.Copy).then_inc(agged, 1)

                def gate(q):
                    act.wait_ge(crossed, q.t + 1)
                    if not is_first(q.t):
                        act.wait_ge(moved, q.t - 1)
                    act.activation(r[q.u][:, :], bank[3][:, :], ACT.Sigmoid, bias=brz_c[:, 0:1])
                    act.activation(zg[q.u][:, :], bank[4][:, :], ACT.Sigmoid, bias=brz_c[:, 1:2])\
                       .then_inc(opened, 1)

                def candidate(q):
                    act.wait_ge(mixed, q.t + 1)
                    act.activation(ng[q.u][:, :], mix[q.u][:, :], ACT.Tanh, bias=bih_c[:, 2:3])\
                       .then_inc(tanhed, 1)

                over_groups(act, [(2, weigh), (4, gate), (4, candidate), (3, hold)], XS)

            @block.vector
            def _(dve):
                def low(q):
                    dve.wait_ge(e.split, q.t + 1)
                    dve.tensor_tensor(e.lo[q.u][:, :, :], msg[q.u][:, :, :],
                                      e.hi[q.u][:, :, :].bitcast(F32), ALU.subtract).then_inc(e.ready, 1)

                def look(q):
                    e.make_onehots(dve, q).then_inc(linked, 1)
                    dve.wait_ge(linked, q.t + 1)
                    dve.wait_ge(asked, q.t + 1)
                    for k in range(CH):
                        last = dve.tensor_tensor_reduce(scrap[:, k, :], e.onehot[q.r][:, k, :].bitcast(F32),
                                                        bank[2 + 5 * q.u][:, :], 1.0, 0.0, ALU.mult, ALU.add,
                                                        term[q.u][:, k:k + 1])
                    last.then_inc(dotted, 1)
                    dve.wait_ge(dotted, q.t + 1)
                    e.arrived(dve, q)
                    dve.wait_ge(loaded_m[q.u], q.n * 16 + 16)
                    if not is_first(q.t):
                        dve.wait_ge(weighed, q.t - 1)
                    dve.tensor_tensor(logit[q.u][:, 0:CH], term[q.u][:, :], e.rows[q.r][:, :, D], ALU.add)
                    mine = own_rows[q.u][:, :].rearrange("p (b f) -> p b f", b=BLK)
                    dve.tensor_tensor(logit[q.u][:, CH:CH + BLK], mine[:, :, D], mine[:, :, D + 1], ALU.add)\
                       .then_inc(gated, 1)

                def blend(q):
                    dve.wait_ge(opened, q.t + 1)
                    dve.scalar_tensor_tensor(out=mix[q.u][:, :], in0=bank[5][:, :], scalar=bhh_c[:, 2:3],
                                             in1=r[q.u][:, :], op0=ALU.add, op1=ALU.mult).then_inc(link, 1)
                    dve.wait_ge(link, q.t + 1)
                    dve.tensor_tensor(mix[q.u][:, :], mix[q.u][:, :], bank[6][:, :], ALU.add)\
                       .then_inc(mixed, 1)

                def move(q):
                    dve.wait_ge(tanhed, q.t + 1)
                    if not is_first(q.t):
                        dve.wait_ge(stored[q.u], q.n * 16)
                    dve.tensor_tensor(hn[q.u][:, :], x2[q.d % XS][:, :], ng[q.u][:, :], ALU.subtract)\
                       .then_inc(link3, 1)
                    dve.wait_ge(link3, q.t * 2 + 1)
                    dve.tensor_tensor(hn[q.u][:, :], hn[q.u][:, :], zg[q.u][:, :], ALU.mult)\
                       .then_inc(link3, 1)
                    dve.wait_ge(link3, q.t * 2 + 2)
                    dve.tensor_tensor(hn[q.u][:, :], hn[q.u][:, :], ng[q.u][:, :], ALU.add)\
                       .then_inc(moved, 1)
                    dve.wait_ge(moved, q.t + 1)
                    if isinstance(q.t, int) and q.t == T - 1:
                        for b in range(BLK):
                            dve.bn_stats(bn_acc[:, T - 1 + b, :], hn[q.u][:, b * P:b * P + LASTP])
                    else:
                        dve.bn_stats(bn_acc[:, bass.ds(q.t, 1), :].rearrange("p o s -> p (o s)"),
                                     hn[q.u][:, :])

                over_groups(dve, [(1, look), (4, blend), (2, low), (4, move)], XS)

    def batch_constants():
        with ExitStack() as ctx:
            ph = Phase(ctx, "bc")
            link, rooted = ph.sem("link"), ph.sem("rooted")
            block = ctx.enter_context(nc.Block())

            @block.scalar
            def _(act):
                act.wait_ge(link, 2)
                act.activation(bn_c[:, :], bn_mv[:, 1:2], ACT.Sqrt).then_inc(rooted, 1)

            @block.vector
            def _(dve):
                dve.bn_aggr(bn_mv[:, :], bn_acc[:, :, :].rearrange("p t s -> p (t s)")).then_inc(link, 1)
                dve.wait_ge(link, 1)
                dve.tensor_scalar(bn_mv[:, 1:2], bn_mv[:, 1:2], BN_EPS, None, ALU.add).then_inc(link, 1)
                dve.wait_ge(rooted, 1)
                dve.reciprocal(bn_a[:, :], bn_c[:, :]).then_inc(link, 1)
                dve.wait_ge(link, 3)
                dve.tensor_tensor(bn_a[:, :], bn_a[:, :], gam_c[:, :], ALU.mult).then_inc(link, 1)
                dve.wait_ge(link, 4)
                dve.tensor_tensor(bn_c[:, :], bn_mv[:, 0:1], bn_a[:, :], ALU.mult).then_inc(link, 1)
                dve.wait_ge(link, 5)
                dve.tensor_tensor(bn_c[:, :], bet_c[:, :], bn_c[:, :], ALU.subtract)

    def batch_normed():
        with ExitStack() as ctx:
            ph = Phase(ctx, "bn")
            ln = LayerNorm(ph)
            hin, xin = ph.pair("h", [P, GRP], n=4), ph.pair("x", [P, GRP], n=4)
            y, z, xout = ph.pair("y", [P, GRP]), ph.pair("z", [P, GRP]), ph.pair("xout", [P, GRP], n=4)
            loaded, scaled, summed = ph.sems("loaded", 4), ph.sem("scaled"), ph.sem("summed")
            turned, stored = ph.sem("turned"), ph.sems("stored", 4)
            block = ctx.enter_context(nc.Block())

            @block.sync
            def _(sp):
                def loads(q):
                    load(sp, q, hin[q.r][:, :], slab_of(hnt, q.t), loaded[q.r], scaled, 4)
                    load(sp, q, xin[q.r][:, :], slab_of(x2t, q.t), loaded[q.r], summed, 4)

                over_groups(sp, [
                    (0, loads),
                    (4, lambda q: store(sp, q, group_of(t_x3[0:NPAD, :], q.t), xout[q.r][:, :], ln.applied,
                                        stored))])
                all_stored(sp, stored)

            @block.scalar
            def _(act):
                def scale(q):
                    act.wait_ge(loaded[q.r], q.m * 32 + 32)
                    if not is_first(q.t):
                        act.wait_ge(summed, q.t - 1)
                    act.activation(y[q.u][:, :], hin[q.r][:, :], ACT.Identity, bias=bn_c[:, 0:1],
                                   scale=bn_a[:, 0:1]).then_inc(scaled, 1)

                def apply(q):
                    if not is_first(q.t, 4):
                        act.wait_ge(stored[q.r], q.m * 16)
                    ln.normalise(act, q, xout[q.r], bank[q.r])

                over_groups(act, [(0, scale), (2, lambda q: ln.root(act, q)), (3, apply)])

            @block.tensor
            def _(pe):
                def turn(q):
                    pe.wait_ge(summed, q.t + 1)
                    if not is_first(q.t, 4):
                        pe.wait_ge(ln.applied, q.t - 3)
                    for b in range(BLK):
                        last = pe.transpose(bank[q.r][:, b * P:(b + 1) * P], z[q.u][:, b * P:(b + 1) * P],
                                            ident[:, :])
                    last.then_inc(turned, 1)

                over_groups(pe, [(1, turn)])

            @block.vector
            def _(dve):
                def add(q):
                    dve.wait_ge(scaled, q.t + 1)
                    if not is_first(q.t):
                        dve.wait_ge(turned, q.t - 1)
                    dve.tensor_tensor(z[q.u][:, :], y[q.u][:, :], xin[q.r][:, :], ALU.add)\
                       .then_inc(summed, 1)

                def gauge(q):
                    dve.wait_ge(turned, q.t + 1)
                    ln.take_stats(dve, q, bank[q.r])

                over_groups(dve, [(0, add), (1, gauge), (2, lambda q: ln.invert(dve, q))])

    def combine():
        with ExitStack() as ctx:
            ph = Phase(ctx, "cb")
            e = EdgeRows(ph, t_x3, D, CH)
            ln = LayerNorm(ph)
            own_rows, xt, agg = ph.pair("own", [P, GRP]), ph.pair("xt", [P, GRP]), ph.pair("agg", [P, GRP])
            z, xout = ph.pair("z", [P, GRP], n=4), ph.pair("xout", [P, GRP])
            loaded, held, dense_done, added = ph.sems("loaded"), ph.sem("held"), ph.sem("dense"), ph.sem("added")
            stored = ph.sems("stored")
            block = ctx.enter_context(nc.Block())

            @block.gpsimd
            def _(pool):
                over_groups(pool, [(0, lambda q: e.gather(pool, q))])

            @block.sync
            def _(sp):
                def leave(q):
                    if isinstance(q.t, int) and q.t == T - 1:
                        store(sp, q, out[(T - 1) * GRP:NODES, :].rearrange("(p b) f -> p (b f)", b=BLK),
                              xout[q.u][0:LASTP, :], ln.applied, stored)
                    else:
                        store(sp, q, group_of(out[0:(T - 1) * GRP, :], q.t), xout[q.u][:, :], ln.applied,
                              stored)

                over_groups(sp, [
                    (0, lambda q: load(sp, q, own_rows[q.u][:, :], own_group(t_x3, q.t),
                                       loaded[q.u], e.summed)),
                    (6, leave)])
                all_stored(sp, stored)

            @block.tensor
            def _(pe):
                def sums(q):
                    pe.wait_ge(e.ready, q.t + 1)
                    pe.wait_ge(loaded[q.u], q.n * 16 + 16)
                    if not is_first(q.t):
                        pe.wait_ge(held, q.t - 1)
                    e.sum_by_feature(pe, q, [bank[q.u]])
                    for b in range(BLK):
                        last = pe.transpose(bank[2 + q.u][:, b * P:(b + 1) * P],
                                            own_rows[q.u][:, b * D:(b + 1) * D], ident[:, :])
                    last.then_inc(e.summed, 1)

                def dense(q):
                    pe.wait_ge(held, q.t + 1)
                    if not is_first(q.t):
                        pe.wait_ge(added, q.t - 1)
                    for b in range(BLK):
                        to = bank[4 + q.u][:, b * D:(b + 1) * D]
                        pe.matmul(to, agg[q.u][:, b * P:(b + 1) * P], wn_s[:, :], start=True, stop=False,
                                  skip_group_check=True)
                        last = pe.matmul(to, xt[q.u][:, b * P:(b + 1) * P], wsx_s[:, :], start=False,
                                         stop=True, skip_group_check=True)
                    last.then_inc(dense_done, 1)

                over_groups(pe, [(1, sums), (2, dense)])

            @block.scalar
            def _(act):
                def hold(q):
                    act.wait_ge(e.summed, q.t + 1)
                    if not is_first(q.t):
                        act.wait_ge(dense_done, q.t - 1)
                    act.activation(agg[q.u][:, :], bank[q.u][:, :], ACT.Copy)
                    act.activation(xt[q.u][:, :], bank[2 + q.u][:, :], ACT.Copy).then_inc(held, 1)

                def apply(q):
                    if not is_first(q.t):
                        act.wait_ge(stored[q.u], q.n * 16)
                    ln.normalise(act, q, xout[q.u], z[q.r])

                over_groups(act, [(0, lambda q: e.take_hi(act, q)), (1, hold),
                                  (4, lambda q: ln.root(act, q)), (5, apply)])

            @block.vector
            def _(dve):
                def add(q):
                    dve.wait_ge(dense_done, q.t + 1)
                    if not is_first(q.t, 4):
                        dve.wait_ge(ln.applied, q.t - 3)
                    dve.tensor_tensor(z[q.r][:, :], bank[4 + q.u][:, :],
                                      b3_r[:, :, :].rearrange("p b f -> p (b f)"), ALU.add)\
                       .then_inc(added, 1)
                    dve.wait_ge(added, q.t + 1)
                    ln.take_stats(dve, q, z[q.r])

                over_groups(dve, [(0, lambda q: e.prepare(dve, q)), (3, add),
                                  (4, lambda q: ln.invert(dve, q))])

    def fold_weights():
        with ExitStack() as ctx:
            ph = Phase(ctx, "fw")
            link = ph.sem("link")
            block = ctx.enter_context(nc.Block())

            @block.vector
            def _(dve):
                dve.tensor_tensor(brz_c[:, :], bih_c[:, 0:2], bhh_c[:, 0:2], ALU.add)
                dve.tensor_tensor(b3_r[:, :, :], b3_r[:, :, :], b3b_r[:, :, :], ALU.add)
                dve.tensor_scalar(wad_s[:, :], iota[:, 0:P], 0.0, wm_s[:, D + 1:D + 2], ALU.mult, ALU.add)
                dve.scalar_tensor_tensor(out=wsx_s[:, :], in0=wn_s[:, :], scalar=own[:, 0:1],
                                         in1=wsx_s[:, :], op0=ALU.mult, op1=ALU.add).then_inc(link, 1)
                dve.wait_ge(link, 1)
                dve.tensor_tensor(wsx_s[:, :], wsx_s[:, :], ident[:, :], ALU.add)

    def if_general(*parts):
        with nc.If(way["general"] == 1):
            for part, *args in parts:
                part(*args)

    way = {}
    with top:
        load_weights()
        sort_edges()
        way["general"] = nc.values_load(general[0:1, 0:1], min_val=0, max_val=1)
        way["rows"] = way["general"] * T
        fold_weights()
        count_degrees()
        if_general((general_sums, None, D, "ones"), (general_slots,))
        scale_degrees()
        scale_x()
        if_general((general_sums, t_x0, D))
        gcn_first()
        if_general((general_sums, t_h0, D))
        gcn_second()
        if_general((general_sums, t_x1, D))
        sage_first()
        if_general((general_sums, t_h, HID))
        sage_second()
        if_general((general_sums, t_v, D))
        sage_third()
        if_general((general_sums, t_m, MW, "messages"))
        attend()
        batch_constants()
        batch_normed()
        if_general((general_sums, t_x3, D))
        combine()


_INS = ["x", "src", "dst", "L0_gnn_W1", "L0_gnn_b1", "L0_gnn_W2", "L0_gnn_b2", "L1_gnn_ws0",
        "L1_gnn_wn0", "L1_gnn_b0", "L1_gnn_ws1", "L1_gnn_wn1", "L1_gnn_b1", "L1_gnn_ws2", "L1_gnn_wn2",
        "L1_gnn_b2", "L2_gnn_W_msg", "L2_gnn_b_msg", "L2_gnn_W_att", "L2_gnn_b_att", "L2_gnn_W_ih",
        "L2_gnn_b_ih", "L2_gnn_W_hh", "L2_gnn_b_hh", "L2_gnn_gamma", "L2_gnn_beta", "L3_gnn_W_neigh",
        "L3_gnn_b_neigh", "L3_gnn_W_self", "L3_gnn_b_self"]
_TURNED = {"L2_gnn_W_ih", "L2_gnn_W_hh", "L3_gnn_W_neigh", "L3_gnn_W_self"}


def kernel(**inputs):
    import numpy as _np
    import concourse.bacc as _bacc
    from concourse import mybir as _mybir
    from concourse.bass_utils import run_bass_kernel_spmd as _run

    nc = _bacc.Bacc("TRN2", target_bir_lowering=False, num_devices=1)
    arrays, args = {}, []
    for name in _INS:
        a = _np.asarray(inputs[name])
        a = _np.ascontiguousarray(a.T if name in _TURNED else a)
        arrays[f"in_{name}_dram"] = a
        args.append(nc.dram_tensor(f"in_{name}_dram", a.shape, _mybir.dt.from_np(a.dtype),
                                   kind="ExternalInput").ap())
    out = nc.dram_tensor("out_0_dram", (NODES, D), F32, kind="ExternalOutput").ap()
    build_program(nc, *args, out)
    r = _run(nc, [arrays], core_ids=[0])
    return r.results[0]["out_0_dram"]
```

```python
from contextlib import ExitStack

import concourse.bass as bass
from concourse import mybir

F32 = mybir.dt.float32
F32R = mybir.dt.float32r
BF16 = mybir.dt.bfloat16
I32 = mybir.dt.int32
U32 = mybir.dt.uint32
ALU = mybir.AluOpType
ACT = mybir.ActivationFunctionType
AX_X = mybir.AxisListType.X

P = 128
D = 128
HID = 256
NODES = 50000
EDGES = 100000
BLK = 4
GRP = BLK * P
T = -(-NODES // GRP)
NPAD = T * GRP
LAST = NODES - (T - 1) * GRP
LASTP = LAST // BLK
CH = 5
SLOTS = T * CH
EC = -(-EDGES // P)
TAIL = EDGES - (P - 1) * EC
WIN = 9
EROWS = -(-(P * EC + WIN * P) // WIN) + 2
EROWS += (EROWS * WIN - P * EC) % 2
PADS = EROWS * WIN - P * EC
SEVEN = 7
NOWHERE = 1 << 20
PADV = 2000000
MW = D + 4
LN_EPS = 1e-5
BN_EPS = 1e-5
assert LAST % BLK == 0 and T % (2 * SEVEN) == 0 and PADS % 2 == 0 and T * CH <= 512


def is_first(t, slots=2):
    return isinstance(t, int) and t < slots


def wait_for(eng, sem, value):
    eng.wait_ge(sem, value)
    if not isinstance(value, int):
        eng.sem_inc(PASSED[0], 1)


PASSED = []


class Turn:

    def __init__(self, j, unroll, d):
        self.j, self.unroll, self.d = j, unroll, d
        self.t = d if j is None else j * unroll + d
        self.u = d % 2
        self.n = self.use(2)
        self.r = d % 4
        self.m = self.use(4)

    def use(self, slots):
        if self.j is None:
            return self.d // slots
        return self.j * (self.unroll // slots) + self.d // slots


def over_groups(eng, stages, unroll=4):
    lim = T - 2

    def step(s):
        for lag, stage in stages:
            if 0 <= s - lag < T:
                stage(Turn(None, unroll, s - lag))

    most = max(lag for lag, _ in stages)
    head = max(2 + most, unroll)
    head += (T - 2 - head) % unroll
    for s in range(head):
        step(s)
    with eng.Fori(0, (lim - head) // unroll) as j:
        for o in range(unroll):
            for lag, stage in stages:
                stage(Turn(j, unroll, head + o - lag))
    for s in range(lim, T + most):
        step(s)


def col(tile, i, n=1):
    return tile[:, bass.ds(i, n)]


def group_of(table, t, b=BLK):
    v = table.rearrange("(t p b) f -> t p (b f)", p=P, b=b)
    return v[bass.ds(t, 1)].rearrange("o p f -> (o p) f")


def slab_of(table, t):
    return table[bass.ds(t, 1)].rearrange("o p f -> (o p) f")


def build_program(nc, x, src, dst, w1, b1, w2, b2, ws0, wn0, sb0, ws1, wn1, sb1, ws2, wn2, sb2,
                  w_msg, b_msg, w_att, b_att, w_ihT, b_ih, w_hhT, b_hh, gamma, beta,
                  w_nT, b_n, w_sT, b_s, out):
    top = ExitStack()

    def sb(name, shape, dt=F32):
        return top.enter_context(nc.sbuf_tensor(name, shape, dt))

    def dram(name, shape, dt=F32):
        return nc.dram_tensor(name, shape, dt, kind="Internal").ap()

    PASSED[:] = [top.enter_context(nc.semaphore("waits_passed"))]

    t_x0 = dram("t_x0", (2 * NPAD, D))
    t_h0 = dram("t_h0", (2 * NPAD, D))
    t_x1 = dram("t_x1", (2 * NPAD, D))
    t_h = dram("t_h", (2 * NPAD, HID))
    t_v = dram("t_v", (2 * NPAD, D))
    t_m = dram("t_m", (2 * NPAD, MW))
    t_x3 = dram("t_x3", (2 * NPAD, D))
    r1 = dram("r1", (NPAD, D))
    r2 = dram("r2", (NPAD, D))
    x2t = dram("x2t", (T, P, GRP))
    hnt = dram("hnt", (T, P, GRP))
    sums_by_width = {w: dram(f"sums_{w}", (NPAD + 2 * P, w)) for w in (D, MW, HID)}
    edges_d = dram("edges_d", (EROWS, 2 * WIN))
    deg_d = dram("deg_d", (T, GRP))
    dinv_d = dram("dinv_d", (T, GRP))
    inv_d = dram("inv_d", (T, GRP))

    idx = sb("idx", [P, SLOTS], U32)
    dcol = sb("dcol", [P, SLOTS])
    dinv_n = sb("dinv_n", [P, T * BLK])
    dinv2_n = sb("dinv2_n", [P, T * BLK])
    inv_n = sb("inv_n", [P, T * BLK])
    selfinv_n = sb("selfinv_n", [P, T * BLK])
    iota = sb("iota", [P, GRP])
    ident = sb("ident", [P, P])
    own = sb("own", [P, 1])
    general = sb("general", [P, 1], I32)
    own1 = sb("own1", [P, 1])
    id_own1 = sb("id_own1", [P, P])
    id_own = sb("id_own", [P, P])
    bn_acc = sb("bn_acc", [P, T + BLK - 1, 6])
    bn_mv = sb("bn_mv", [P, 2])
    bn_a = sb("bn_a", [P, 1])
    bn_c = sb("bn_c", [P, 1])

    w1_s = sb("w1_s", [P, HID])
    w2_s = sb("w2_s", [P, 2, D])
    b1_c = sb("b1_c", [P, 2])
    b2_r = sb("b2_r", [P, BLK, D])
    ws0_s = sb("ws0_s", [P, HID])
    wn0_s = sb("wn0_s", [P, HID])
    sb0_r = sb("sb0_r", [P, 2, HID])
    ws1_s = sb("ws1_s", [P, 2, HID])
    wn1_s = sb("wn1_s", [P, 2, HID])
    sb1_c = sb("sb1_c", [P, 2])
    wuv_s = sb("wuv_s", [P, 2, HID])
    sb2_r = sb("sb2_r", [P, BLK, D])
    wm_s = sb("wm_s", [P, MW])
    bm_r = sb("bm_r", [P, 2, MW])
    wad_s = sb("wad_s", [P, P])
    wih_s = sb("wih_s", [P, 3 * D])
    whh_s = sb("whh_s", [P, 3 * D])
    bih_c = sb("bih_c", [P, 3])
    bhh_c = sb("bhh_c", [P, 3])
    brz_c = sb("brz_c", [P, 2])
    gam_c = sb("gam_c", [P, 1])
    bet_c = sb("bet_c", [P, 1])
    wn_s = sb("wn_s", [P, D])
    wsx_s = sb("wsx_s", [P, D])
    b3_r = sb("b3_r", [P, BLK, D])
    b3b_r = sb("b3b_r", [P, BLK, D])

    bank = [top.enter_context(nc.psum_tensor(f"bank{i}", [P, 512], F32)) for i in range(8)]

    class Phase:

        def __init__(self, ctx, name):
            self.ctx, self.name, self.own_sems = ctx, name, []
            ctx.callback(self.clear)

        def clear(self):
            nc.clear_and_free_semaphores(self.own_sems)
            nc.all_engine_barrier()

        def tile(self, name, shape, dt=F32):
            return self.ctx.enter_context(nc.sbuf_tensor(f"{self.name}_{name}", shape, dt))

        def pair(self, name, shape, dt=F32, n=2):
            return [self.tile(f"{name}{u}", shape, dt) for u in range(n)]

        def sem(self, name):
            self.own_sems.append(nc.alloc_semaphore(f"{self.name}_{name}"))
            return self.own_sems[-1]

        def sems(self, name, n=2):
            return [self.sem(f"{name}{u}") for u in range(n)]

    def load_weights():
        with ExitStack() as ctx:
            ph = Phase(ctx, "w")
            got, cleared = ph.sem("loaded"), ph.sem("cleared")
            block = ctx.enter_context(nc.Block())

            def row(a, n):
                return a.rearrange("(o n) -> o n", o=1).broadcast_to([P, n])

            def column(a, k):
                return a.rearrange("(k p) -> p k", p=P)

            loads = [
                (w1_s[:, :], w1), (w2_s[:, :, :], w2.rearrange("(k p) f -> p k f", p=P)),
                (ws0_s[:, :], ws0), (wn0_s[:, :], wn0),
                (ws1_s[:, :, :], ws1.rearrange("(k p) f -> p k f", p=P)),
                (wn1_s[:, :, :], wn1.rearrange("(k p) f -> p k f", p=P)),
                (wuv_s[:, :, 0:D], ws2.rearrange("(k p) f -> p k f", p=P)),
                (wuv_s[:, :, D:HID], wn2.rearrange("(k p) f -> p k f", p=P)),
                (wm_s[:, 0:D], w_msg), (wm_s[:, D:D + 1], w_att[0:D, :]),
                (wm_s[:, D + 1:D + 2], w_att[D:2 * D, :]),
                (wih_s[:, :], w_ihT), (whh_s[:, :], w_hhT), (wn_s[:, :], w_nT), (wsx_s[:, :], w_sT),
                (b1_c[:, :], column(b1, 2)), (sb1_c[:, :], column(sb1, 2)),
                (bih_c[:, :], column(b_ih, 3)), (bhh_c[:, :], column(b_hh, 3)),
                (gam_c[:, :], column(gamma, 1)), (bet_c[:, :], column(beta, 1)),
            ]
            for k in range(BLK):
                loads += [(b2_r[:, k, :], row(b2, D)), (sb2_r[:, k, :], row(sb2, D)),
                          (b3_r[:, k, :], row(b_n, D)), (b3b_r[:, k, :], row(b_s, D))]
            for k in range(2):
                loads += [(sb0_r[:, k, :], row(sb0, HID)), (bm_r[:, k, 0:D], row(b_msg, D)),
                          (bm_r[:, k, D:D + 1], row(b_att, 1))]

            @block.vector
            def _(dve):
                dve.memset(wm_s[:, :], 0.0)
                dve.memset(bm_r[:, :, :], 0.0).then_inc(cleared, 1)

            @block.sync
            def _(sp):
                sp.wait_ge(cleared, 1)
                for to, what in loads:
                    sp.dma_start(to, what, allow_slow_non_contiguous=True).then_inc(got, 16)
                sp.wait_ge(got, 16 * len(loads))

    def sort_edges():
        with ExitStack() as ctx:
            ph = Phase(ctx, "so")
            tmp, sem = ph.tile, ph.sem

            si = tmp("src_i", [P, EC], I32)
            di = tmp("dst_i", [P, EC], I32)
            ni = tmp("next_i", [P, EC], I32)
            q1 = tmp("int_1", [P, EC], I32)
            q2 = tmp("int_2", [P, EC], I32)
            ends = tmp("ends_f", [P, EC])
            a = tmp("scratch_a", [P, EC])
            b = tmp("scratch_b", [P, EC])
            c = tmp("scratch_c", [P, EC])
            df = tmp("dst_f", [P, EC])
            nf = tmp("next_f", [P, EC])
            pair = tmp("pair", [P, EC, 2])
            pads = tmp("pads", [2, PADS // 2, 2])
            first = tmp("first_group", [P, 4])
            held = tmp("edges_held", [P, 4])
            spread = tmp("spread", [P, 4, P])
            start = tmp("start", [P, T + 1])
            place = tmp("place_i", [P, 1], I32)
            place_f = tmp("place_f", [P, 1])
            row_f = tmp("row_f", [P, T])
            row = tmp("row", [P, T], U32)
            base_i, base_f = tmp("base_i", [P, T], I32), tmp("base_f", [P, T])
            win = tmp("window", [P, T, WIN, 2])
            w = tmp("column", [P, T, WIN])
            ok = tmp("valid", [P, T, WIN])
            before = tmp("before", [P, T, WIN])
            below = tmp("below", [P, P])
            rank = tmp("rank", [P, T, WIN], I32)
            rank_k, rank_p = tmp("rank_k", [P, T, WIN], I32), tmp("rank_p", [P, T, WIN], I32)
            of_k, of_p = tmp("of_k", [P, T * WIN]), tmp("of_p", [P, T * WIN])
            digit = [tmp(f"digit{f}", [P, T * WIN]) for f in range(4)]
            value = tmp("value", [P, T * WIN, 4, CH], BF16)
            parts = [tmp(f"parts{u}", [P, WIN, P], BF16) for u in range(SEVEN)]
            sums = tmp("sums", [P, 4, T // 2, 2, CH])
            filled = tmp("filled", [P, SLOTS])
            seen = tmp("seen", [P, 4])
            total = tmp("total", [P, 4])
            ones = tmp("ones", [P, P])
            idxi = tmp("iota_i", [P, GRP], I32)

            made = sem("patterns_made")
            padded = sem("edges_padded")
            got = sem("edges_loaded")
            chain = sem("edge_steps")
            paired, laid = sem("edges_paired"), sem("edges_laid")
            turned = sem("turned")
            aimed, gathered = sem("windows_aimed"), sem("windows_gathered")
            picked, moved = sem("parts_made"), sem("group_moved")
            block = ctx.enter_context(nc.Block())

            @block.gpsimd
            def _(pool):
                pool.iota(idxi[:, :], pattern=[[1, GRP]], base=0, channel_multiplier=0).then_inc(made, 1)
                pool.iota(place[:, :], pattern=[[0, 1]], base=0, channel_multiplier=1).then_inc(made, 1)
                pool.iota(base_i[:, :], pattern=[[GRP, T]], base=0, channel_multiplier=0).then_inc(made, 1)
                pool.memset(ident[:, :], 0.0).then_inc(made, 1)
                pool.memset(below[:, :], 0.0).then_inc(made, 1)
                pool.wait_ge(made, 5)
                pool.affine_select(out=ident[:, :], in_=ident[:, :], compare_op=ALU.not_equal, fill=1.0,
                                   base=0, pattern=[[-1, P]], channel_multiplier=1).then_inc(made, 1)
                pool.affine_select(out=below[:, :], in_=below[:, :], compare_op=ALU.is_ge, fill=1.0,
                                   base=0, pattern=[[-1, P]], channel_multiplier=1).then_inc(made, 1)
                pool.wait_ge(laid, 32)
                pool.wait_ge(aimed, 1)
                for t in range(T):
                    pool.indirect_dma_start(
                        out=win[:, t, :, :].rearrange("p c f -> p (c f)"), out_offset=None, in_=edges_d,
                        in_offset=bass.IndirectOffsetOnAxis(ap=row[:, t:t + 1], axis=0),
                        bounds_check=EROWS - 1, oob_is_err=False).then_inc(gathered, 16)

            @block.sync
            def _(sp):
                sp.wait_ge(padded, 2)
                full = (P - 1) * EC
                for tile, e, off in ((si, src, 0), (di, dst, 0), (ni, dst, 1)):
                    sp.dma_start(tile[0:P - 1, :], e[off:off + full].rearrange("(p c) -> p c", p=P - 1))\
                      .then_inc(got, 16)
                    sp.dma_start(tile[P - 1:P, 0:TAIL - off],
                                 e[off + full:EDGES].rearrange("(o c) -> o c", o=1)).then_inc(got, 16)
                sp.wait_ge(paired, 1)
                flat = edges_d.rearrange("r f -> (r f)")
                sp.dma_start(flat[0:2 * P * EC].rearrange("(p f) -> p f", p=P),
                             pair[:, :, :].rearrange("p c f -> p (c f)")).then_inc(laid, 16)
                sp.dma_start(flat[2 * P * EC:2 * WIN * EROWS].rearrange("(p f) -> p f", p=2),
                             pads[:, :, :].rearrange("p c f -> p (c f)")).then_inc(laid, 16)
                sp.wait_ge(laid, 32)

            @block.tensor
            def _(pe):
                pe.wait_ge(turned, 1)
                for d in range(4):
                    last = pe.matmul(bank[0][:, 0:P], ones[:, :], spread[:, d, :], start=(d == 0), stop=(d == 3))
                last.then_inc(turned, 1)
                pe.sem_inc(moved, SEVEN)
                pe.wait_ge(made, 7)
                pe.wait_ge(turned, 3)
                pe.matmul(bank[1][:, 0:T], below[:, :], before[:, :, WIN - 1], start=True, stop=True)\
                  .then_inc(turned, 1)
                for half in range(2):
                    with pe.Fori(0, T // 2 // SEVEN) as j:
                        for o in range(SEVEN):
                            t = j * SEVEN + o
                            pe.wait_ge(picked, t + (half * (T // 2) + 1))
                            for k in range(WIN):
                                for f in range(2):
                                    last = pe.matmul(
                                        bank[2 + 3 * half + f][:, bass.ds(t * (2 * CH), 2 * CH)],
                                        parts[o][:, k, :],
                                        value[:, bass.ds(t * WIN + (half * (T // 2) * WIN + k), 1),
                                              2 * f:2 * f + 2, :].rearrange("p o f k -> p (o f k)"),
                                        start=(k == 0), stop=(k == WIN - 1), skip_group_check=True)
                            last.then_inc(moved, 1)
                pe.wait_ge(turned, 5)
                pe.matmul(bank[4][:, 0:4], ones[:, :], seen[:, :], start=True, stop=True)\
                  .then_inc(turned, 1)

            @block.vector
            def _(dve):
                steps = [0]

                def then(ins):
                    steps[0] += 1
                    ins.then_inc(chain, 1)
                    dve.wait_ge(chain, steps[0])

                dve.memset(si[:, :], 0).then_inc(padded, 1)
                dve.memset(di[:, :], PADV)
                dve.memset(ni[:, :], PADV).then_inc(padded, 1)
                dve.memset(pads[:, :, :], -float(PADV))
                dve.memset(start[:, 0:1], 0.0)
                dve.memset(row_f[:, :], 0.0)
                then(dve.memset(ones[:, :], 1.0))
                dve.wait_ge(made, 7)
                dve.tensor_copy(iota[:, :], idxi[:, :])
                dve.tensor_copy(base_f[:, :], base_i[:, :])
                dve.tensor_copy(place_f[:, :], place[:, :])
                dve.wait_ge(got, 96)
                dve.tensor_copy(df[:, :], di[:, :])
                dve.tensor_copy(nf[:, :], ni[:, :])
                dve.tensor_scalar(q1[:, :], di[:, :], 9, None, ALU.logical_shift_right)
                then(dve.tensor_copy(pair[:, :, 0], si[:, :]))
                then(dve.tensor_tensor(ends[:, :], df[:, :], nf[:, :], ALU.not_equal))
                dve.tensor_scalar(ni[:, :], di[:, :], 3, 7, ALU.bitwise_and, ALU.logical_shift_left)
                then(dve.tensor_scalar(q2[:, :], di[:, :], GRP - 1, 2, ALU.bitwise_and, ALU.logical_shift_right))
                then(dve.tensor_tensor(q2[:, :], q2[:, :], ni[:, :], ALU.bitwise_or))
                dve.tensor_copy(a[:, :], q1[:, :])
                then(dve.tensor_copy(b[:, :], q2[:, :]))
                then(dve.scalar_tensor_tensor(out=b[:, :], in0=a[:, :], scalar=float(GRP), in1=b[:, :],
                                              op0=ALU.mult, op1=ALU.add))
                dve.scalar_tensor_tensor(out=pair[:, :, 1], in0=ends[:, :], scalar=-2.0 * PADV,
                                         in1=b[:, :], op0=ALU.mult, op1=ALU.add).then_inc(paired, 1)
                dve.tensor_copy(first[:, 0:1], a[:, 0:1])
                then(dve.tensor_copy(first[:, 1:2], a[:, 0:1]))
                for d in range(1, 4):
                    then(dve.tensor_scalar(first[:, d:d + 1], first[:, 0:1], float(d), None, ALU.add))
                for d in range(4):
                    then(dve.tensor_scalar(b[:, :], a[:, :], first[:, d:d + 1], None, ALU.is_equal))
                    then(dve.tensor_reduce(held[:, d:d + 1], b[:, :], AX_X, ALU.add))
                for d in range(4):
                    last = dve.tensor_scalar(spread[:, d, :], iota[:, 0:P], first[:, d:d + 1],
                                             held[:, d:d + 1], ALU.is_equal, ALU.mult)
                last.then_inc(turned, 1)
                dve.wait_ge(turned, 2)
                then(dve.tensor_tensor_scan(start[:, 1:T + 1], bank[0][:, 0:T], row_f[:, :], 0.0,
                                            ALU.add, ALU.add))
                then(dve.tensor_scalar(row_f[:, :], start[:, 0:T], -(WIN // 2), 1.0 / WIN, ALU.add, ALU.mult))
                then(dve.tensor_scalar(row_f[:, :], row_f[:, :], 0.0, None, ALU.max))
                then(dve.tensor_copy(row[:, :], row_f[:, :]))
                then(dve.tensor_copy(row_f[:, :], row[:, :]))
                then(dve.tensor_scalar(row_f[:, :], row_f[:, :], place_f[:, 0:1], None, ALU.add))
                dve.tensor_copy(row[:, :], row_f[:, :]).then_inc(aimed, 1)
                dve.tensor_reduce(seen[:, 2:3], ends[:, :], AX_X, ALU.add)
                then(dve.tensor_tensor(b[:, :], pair[:, :, 0], df[:, :], ALU.not_equal))
                then(dve.tensor_tensor(b[:, :], b[:, :], ends[:, :], ALU.mult))
                dve.tensor_reduce(seen[:, 1:2], b[:, :], AX_X, ALU.add)
                then(dve.tensor_tensor(c[:, :], nf[:, :], df[:, :], ALU.is_lt))
                then(dve.tensor_reduce(seen[:, 0:1], c[:, :], AX_X, ALU.add))
                dve.wait_ge(gathered, 16 * T)
                for k in range(WIN):
                    last = dve.tensor_tensor(w[:, :, k], win[:, :, k, 1], base_f[:, :], ALU.subtract)
                then(last)
                then(dve.tensor_scalar(ok[:, :, :], w[:, :, :], 0.0, None, ALU.is_ge))
                then(dve.scalar_tensor_tensor(out=ok[:, :, :], in0=w[:, :, :], scalar=float(GRP),
                                              in1=ok[:, :, :], op0=ALU.is_lt, op1=ALU.mult))
                then(dve.tensor_copy(before[:, :, 0], ok[:, :, 0]))
                for k in range(1, WIN):
                    then(dve.tensor_tensor(before[:, :, k], before[:, :, k - 1], ok[:, :, k], ALU.add))
                dve.memset(row_f[:, :], 0.0).then_inc(turned, 1)
                dve.wait_ge(turned, 4)
                for k in range(WIN):
                    last = dve.tensor_tensor(before[:, :, k], before[:, :, k], bank[1][:, 0:T], ALU.add)
                then(last)
                then(dve.tensor_tensor(before[:, :, :], before[:, :, :], ok[:, :, :], ALU.mult))
                then(dve.tensor_scalar(before[:, :, :], before[:, :, :], 1.0, None, ALU.subtract))
                then(dve.tensor_copy(rank[:, :, :], before[:, :, :]))
                dve.tensor_scalar(rank_k[:, :, :], rank[:, :, :], 7, None, ALU.logical_shift_right)
                then(dve.tensor_scalar(rank_p[:, :, :], rank[:, :, :], P - 1, None, ALU.bitwise_and))
                dve.tensor_copy(of_k[:, :], rank_k[:, :, :].rearrange("p t c -> p (t c)"))
                dve.tensor_copy(of_p[:, :], rank_p[:, :, :].rearrange("p t c -> p (t c)"))
                for f, (what, bits) in enumerate(((win[:, :, :, 0], 8), (w[:, :, :], 7))):
                    then(dve.tensor_copy(rank[:, :, :], what))
                    dve.tensor_scalar(rank_k[:, :, :], rank[:, :, :], bits, None, ALU.logical_shift_right)
                    then(dve.tensor_scalar(rank_p[:, :, :], rank[:, :, :], (1 << bits) - 1, None, ALU.bitwise_and))
                    dve.tensor_copy(digit[2 * f][:, :], rank_k[:, :, :].rearrange("p t c -> p (t c)"))
                    then(dve.tensor_copy(digit[2 * f + 1][:, :], rank_p[:, :, :].rearrange("p t c -> p (t c)")))
                then(dve.tensor_scalar(digit[2][:, :], digit[2][:, :], 1.0, None, ALU.add))
                for f in range(4):
                    for k in range(CH):
                        last = dve.scalar_tensor_tensor(out=value[:, :, f, k], in0=of_k[:, :], scalar=float(k),
                                                        in1=digit[f][:, :], op0=ALU.is_equal, op1=ALU.mult)
                then(last)
                for half in range(2):
                    with dve.Fori(0, T // 2 // SEVEN) as j:
                        for o in range(SEVEN):
                            t = j * SEVEN + (half * (T // 2) + o)
                            dve.wait_ge(moved, t + 1)
                            for k in range(WIN):
                                last = dve.tensor_scalar(parts[o][:, k, :], iota[:, 0:P],
                                                         col(of_p, t * WIN + k), None, ALU.is_equal)
                            last.then_inc(picked, 1)
                dve.wait_ge(moved, SEVEN + T)
                for n in range(4):
                    last = dve.tensor_copy(sums[:, n, :, :, :].rearrange("p t f k -> p (t f k)"),
                                           bank[2 + 3 * (n // 2) + n % 2][:, 0:T * CH])
                then(last)
                for half in range(2):
                    g = slice(half * (T // 2), (half + 1) * (T // 2))
                    at = [tile[:, :].rearrange("p (t k) -> p t k", k=CH)[:, g, :] for tile in (filled, dcol)]
                    for n in range(2):
                        v = sums[:, 2 * half + n, :, :, :]
                        last = dve.scalar_tensor_tensor(out=at[n], in0=v[:, :, 0, :], scalar=(256.0, 128.0)[n],
                                                        in1=v[:, :, 1, :], op0=ALU.mult, op1=ALU.add)
                then(last)
                dve.tensor_copy(idx[:, :], filled[:, :])
                then(dve.tensor_scalar(dcol[:, :], dcol[:, :], float(P), None, ALU.subtract))
                then(dve.tensor_scalar(filled[:, :], dcol[:, :], 0.0, None, ALU.is_ge))
                dve.tensor_reduce(seen[:, 3:4], filled[:, :], AX_X, ALU.add).then_inc(turned, 1)
                then(dve.tensor_scalar(filled[:, :], filled[:, :], -float(NOWHERE), float(NOWHERE),
                                       ALU.mult, ALU.add))
                then(dve.tensor_tensor(filled[:, :], filled[:, :], idx[:, :], ALU.add))
                dve.tensor_copy(idx[:, :], filled[:, :])
                dve.wait_ge(turned, 6)
                then(dve.tensor_copy(total[:, :], bank[4][:, 0:4]))
                dve.tensor_tensor(total[:, 0:1], total[:, 0:1], total[:, 1:2], ALU.add)
                dve.tensor_scalar(total[:, 3:4], total[:, 3:4], float(EDGES - NODES), None, ALU.not_equal)
                then(dve.tensor_scalar(total[:, 2:3], total[:, 2:3], float(NODES), None, ALU.not_equal))
                then(dve.tensor_tensor(total[:, 2:3], total[:, 2:3], total[:, 3:4], ALU.add))
                then(dve.tensor_tensor(total[:, 0:1], total[:, 0:1], total[:, 2:3], ALU.add))
                then(dve.tensor_scalar(total[:, 0:1], total[:, 0:1], 0.0, None, ALU.is_gt))
                dve.tensor_copy(general[:, :], total[:, 0:1])
                then(dve.tensor_scalar(own[:, :], total[:, 0:1], -1.0, 1.0, ALU.mult, ALU.add))
                then(dve.tensor_scalar(own1[:, :], own[:, :], 1.0, None, ALU.add))
                dve.tensor_scalar(id_own1[:, :], ident[:, :], own1[:, 0:1], None, ALU.mult)
                dve.tensor_scalar(id_own[:, :], ident[:, :], own[:, 0:1], None, ALU.mult)

    class EdgeRows:

        def __init__(self, ph, table, width, parts, hots=2):
            self.table = table
            self.rows = ph.pair("rows", [P, CH, width], n=4)
            self.hi = ph.pair("hi", [P, parts, min(width, HID) if width != MW else D], F32R)
            self.lo = ph.pair("lo", [P, parts, min(width, HID) if width != MW else D], F32R)
            self.hots = hots
            self.onehot = ph.pair("onehot", [P, CH, GRP], F32R, n=hots)
            self.index = ph.pair("index", [P, CH], U32, n=4)
            self.cleared = ph.sem("rows_cleared")
            self.indexed = ph.sem("index_copied")
            self.gathered = ph.sems("rows_gathered", 4)
            self.split = ph.sem("rows_hi")
            self.ready = ph.sem("rows_ready")
            self.summed = ph.sem("rows_summed")

        def aim(self, pool, q, used=None):
            if is_first(q.t, 4):
                pool.memset(self.rows[q.r][:, :, :], 0.0).then_inc(self.cleared, 1)
            else:
                wait_for(pool, used or self.ready, q.t - 3)
            pool.tensor_copy(self.index[q.r][:, :], col(idx, q.t * CH, CH)).then_inc(self.indexed, 1)

        def gather(self, pool, q):
            if is_first(q.t, 4):
                pool.wait_ge(self.cleared, q.t + 1)
            wait_for(pool, self.indexed, q.t + 1)
            for k in range(CH):
                pool.indirect_dma_start(
                    out=self.rows[q.r][:, k, :], out_offset=None, in_=self.table[0:NPAD, :],
                    in_offset=bass.IndirectOffsetOnAxis(ap=self.index[q.r][:, k:k + 1], axis=0),
                    bounds_check=NPAD - 1, oob_is_err=False).then_inc(self.gathered[q.r], 16)

        def fetch(self, pool, used=None):
            over_groups(pool, [(0, lambda q: self.aim(pool, q, used)), (1, lambda q: self.gather(pool, q))])

        def arrived(self, eng, q):
            eng.wait_ge(self.gathered[q.r], (q.m + 1) * (16 * CH))

        def free(self, eng, q):
            if not is_first(q.t):
                eng.wait_ge(self.summed, q.t - 1)

        def take_hi(self, act, q):
            self.arrived(act, q)
            self.free(act, q)
            act.activation(self.hi[q.u][:, :, :], self.rows[q.r][:, :, :], ACT.Copy).then_inc(self.split, 1)

        def make_onehots(self, dve, q):
            if not is_first(q.t, self.hots):
                dve.wait_ge(self.summed, q.t - (self.hots - 1))
            for k in range(CH):
                last = dve.tensor_scalar(self.onehot[q.d % self.hots][:, k, :], iota[:, :],
                                         col(dcol, q.t * CH + k), None, ALU.is_equal)
            return last

        def take_lo(self, dve, q):
            dve.wait_ge(self.split, q.t + 1)
            dve.tensor_tensor(self.lo[q.u][:, :, :], self.rows[q.r][:, :, :],
                              self.hi[q.u][:, :, :].bitcast(F32), ALU.subtract).then_inc(self.ready, 1)

        def prepare(self, dve, q):
            self.make_onehots(dve, q)
            self.take_lo(dve, q)

        def sum_by_feature(self, pe, q, banks, close=True):
            for h, to in enumerate(banks):
                for k in range(CH):
                    for part in (self.hi, self.lo):
                        last = pe.matmul(to[:, :], part[q.u][:, k, h * P:(h + 1) * P],
                                         self.onehot[q.d % self.hots][:, k, :], start=(k == 0 and part is self.hi),
                                         stop=(close and k == CH - 1 and part is self.lo),
                                         skip_group_check=True)
            return last

        def sum_by_node(self, pe, q, to):
            for b in range(BLK):
                for k in range(CH):
                    for part in (self.hi, self.lo):
                        last = pe.matmul(to[:, b * P:(b + 1) * P],
                                         self.onehot[q.d % self.hots][:, k, b * P:(b + 1) * P], part[q.u][:, k, :],
                                         start=(k == 0 and part is self.hi),
                                         stop=(k == CH - 1 and part is self.lo), skip_group_check=True)
            return last

    class LayerNorm:

        def __init__(self, ph):
            self.stats = ph.pair("ln_stats", [P, BLK, 6])
            self.mv = ph.pair("ln_mv", [P, BLK, 2])
            self.var = ph.pair("ln_var", [P, BLK])
            self.std = ph.pair("ln_std", [P, BLK])
            self.rstd = ph.pair("ln_rstd", [P, BLK])
            self.shift = ph.pair("ln_shift", [P, BLK])
            self.link = ph.sem("ln_link")
            self.link2 = ph.sem("ln_link2")
            self.varied = ph.sem("ln_varied")
            self.rooted = ph.sem("ln_rooted")
            self.scaled = ph.sem("ln_scaled")
            self.applied = ph.sem("ln_applied")

        def take_stats(self, dve, q, z):
            for b in range(BLK):
                last = dve.bn_stats(self.stats[q.u][:, b, :], z[:, b * D:(b + 1) * D])
            last.then_inc(self.link, 1)
            wait_for(dve, self.link, q.t * 2 + 1)
            for b in range(BLK):
                last = dve.bn_aggr(self.mv[q.u][:, b, :], self.stats[q.u][:, b, :])
            last.then_inc(self.link, 1)
            dve.wait_ge(self.link, q.t * 2 + 2)
            dve.tensor_scalar(self.var[q.u][:, :], self.mv[q.u][:, :, 1], LN_EPS, None, ALU.add)\
               .then_inc(self.varied, 1)

        def root(self, act, q):
            act.wait_ge(self.varied, q.t + 1)
            act.activation(self.std[q.u][:, :], self.var[q.u][:, :], ACT.Sqrt).then_inc(self.rooted, 1)

        def invert(self, dve, q):
            dve.wait_ge(self.rooted, q.t + 1)
            dve.reciprocal(self.rstd[q.u][:, :], self.std[q.u][:, :]).then_inc(self.link2, 1)
            dve.wait_ge(self.link2, q.t + 1)
            dve.scalar_tensor_tensor(out=self.shift[q.u][:, :], in0=self.mv[q.u][:, :, 0], scalar=-1.0,
                                     in1=self.rstd[q.u][:, :], op0=ALU.mult, op1=ALU.mult)\
               .then_inc(self.scaled, 1)

        def normalise(self, act, q, to, z):
            act.wait_ge(self.scaled, q.t + 1)
            for b in range(BLK):
                last = act.activation(to[:, b * D:(b + 1) * D], z[:, b * D:(b + 1) * D], ACT.Identity,
                                      bias=self.shift[q.u][:, b:b + 1], scale=self.rstd[q.u][:, b:b + 1])
            last.then_inc(self.applied, 1)

    def load(sp, q, to, what, loaded, free=None, slots=2):
        if free is not None and not (isinstance(q.t, int) and q.t < slots):
            wait_for(sp, free, q.t - (slots - 1))
        sp.dma_start(to, what).then_inc(loaded, 16)

    def store(sp, q, to, what, made, stored):
        wait_for(sp, made, q.t + 1)
        sp.dma_start(to, what).then_inc(stored[q.d % len(stored)], 16)

    def all_stored(sp, *stored):
        for sems in stored:
            for u, sem in enumerate(sems):
                sp.wait_ge(sem, 16 * ((T + len(sems) - 1 - u) // len(sems)))

    def own_group(table, t):
        return group_of(table, t + way["rows"])

    def row_of(a, t):
        return a[bass.ds(t, 1), :].broadcast_to([P, GRP])

    def general_slots():
        with ExitStack() as ctx:
            ph = Phase(ctx, "gs")
            row = ph.tile("row", [P, T, BLK], I32)
            place = ph.tile("place", [P, BLK], I32)
            made, link = ph.sem("made"), ph.sem("link")
            block = ctx.enter_context(nc.Block())

            @block.gpsimd
            def _(pool):
                pool.iota(row[:, :, :], pattern=[[GRP, T], [1, BLK]], base=0, channel_multiplier=BLK)\
                    .then_inc(made, 1)
                pool.iota(place[:, :], pattern=[[P, BLK]], base=0, channel_multiplier=1).then_inc(made, 1)

            @block.vector
            def _(dve):
                dve.memset(idx[:, :], NOWHERE)
                dve.memset(dcol[:, :], -1.0).then_inc(link, 1)
                dve.wait_ge(link, 1)
                dve.wait_ge(made, 2)
                dve.tensor_copy(idx[:, :].rearrange("p (t k) -> p t k", k=CH)[:, :, 0:BLK], row[:, :, :])
                for k in range(BLK):
                    dve.tensor_scalar(dcol[:, :].rearrange("p (t k) -> p t k", k=CH)[:, :, k], row[:, :, 0],
                                      0.0, 0.0, ALU.mult, ALU.add).then_inc(link, 1)
                dve.tensor_copy(id_own1[:, 0:BLK], place[:, :]).then_inc(link, 1)
                dve.wait_ge(link, 2 + BLK)
                for k in range(BLK):
                    v = dcol[:, :].rearrange("p (t k) -> p t k", k=CH)[:, :, k]
                    dve.tensor_scalar(v, v, id_own1[:, k:k + 1], None, ALU.add).then_inc(link, 1)
                dve.wait_ge(link, 2 + 2 * BLK)
                dve.tensor_scalar(id_own1[:, :], ident[:, :], own1[:, 0:1], None, ALU.mult)

    summed_for = []

    def general_sums(table, width, kind="rows"):
        JUNK = NPAD + P
        sums = sums_by_width[width]
        with ExitStack() as ctx:
            ph = Phase(ctx, f"sums{len(summed_for)}")
            summed_for.append(table)
            si, di = ph.tile("src", [P, EC], I32), ph.tile("dst", [P, EC], I32)
            nowhere = ph.tile("nowhere", [P, EC], I32)
            jrow = ph.tile("jrow", [P, 1], I32)
            junk, before = ph.tile("junk", [P, 1]), ph.tile("before", [P, P])
            zero, ones = ph.tile("zero", [P, BLK * width]), ph.tile("ones", [P, P])
            s_now, d_now, to_now = (ph.tile(n, [P, 1], U32) for n in ("s_now", "d_now", "to_now"))
            d_f, d_all = ph.tile("d_f", [P, 1]), ph.tile("d_all", [P, P])
            same, scrap = ph.tile("same", [P, P]), ph.tile("scrap", [P, P])
            ahead, move = ph.tile("ahead", [P, 1]), ph.tile("move", [P, 1])
            rows, theirs = ph.tile("rows", [P, width]), ph.tile("theirs", [P, width])
            att = ph.tile("att", [P, 1])
            part = ph.tile("part", [P, width])
            degs = ph.tile("degs", [P, T, BLK])
            made, filled, got, link = ph.sem("made"), ph.sem("filled"), ph.sem("got"), ph.sem("link")
            spread, matched, gathered = ph.sem("spread"), ph.sem("matched"), ph.sem("gathered")
            aimed, weighed, summed = ph.sem("aimed"), ph.sem("weighed"), ph.sem("summed")
            parted, added, copied = ph.sem("parted"), ph.sem("added"), ph.sem("copied")
            asked = ph.sem("asked")
            gathers = 0 if kind == "ones" else 2 if kind == "messages" else 1
            block = ctx.enter_context(nc.Block())

            @block.sync
            def _(sp):
                sp.wait_ge(filled, 1)
                full = (P - 1) * EC
                for tile, a in ((si, src), (di, dst)):
                    sp.dma_start(tile[0:P - 1, :], a[0:full].rearrange("(p c) -> p c", p=P - 1)).then_inc(got, 16)
                    sp.dma_start(tile[P - 1:P, 0:TAIL], a[full:EDGES].rearrange("(o c) -> o c", o=1))\
                      .then_inc(got, 16)
                view = sums[0:NPAD, :].rearrange("(t p b) f -> t p (b f)", p=P, b=BLK)
                for t in range(T):
                    sp.dma_start(view[t], zero[:, :])\
                      .then_inc(copied, 16)
                sp.dma_start(sums[NPAD:NPAD + P, 0:width], zero[:, 0:width]).then_inc(copied, 16)
                sp.dma_start(sums[JUNK:JUNK + P, 0:width], zero[:, 0:width]).then_inc(copied, 16)
                moves = T + 2
                if kind != "ones":
                    sp.dma_start(table[NPAD:2 * NPAD, :], table[0:NPAD, :]).then_inc(copied, 16)
                    moves += 1
                sp.wait_ge(added, 16 * EC)
                if kind == "ones":
                    for k in range(BLK):
                        sp.dma_start(degs[:, :, k], sums[0:NPAD, :].rearrange("(t p b) f -> p t b f", p=P, b=BLK)
                                     [:, :, k, 0], allow_slow_non_contiguous=True).then_inc(got, 16)
                    sp.wait_ge(got, 16 * (4 + BLK))
                    for k in range(BLK):
                        sp.dma_start(deg_d[:, k * P:(k + 1) * P].rearrange("t p -> p t"), degs[:, :, k],
                                     allow_slow_non_contiguous=True).then_inc(copied, 16)
                    sp.wait_ge(copied, 16 * (moves + BLK))
                else:
                    sp.wait_ge(copied, 16 * moves)
                    sp.dma_start(table[0:NPAD, :], sums[0:NPAD, 0:width]).then_inc(copied, 16)
                    sp.wait_ge(copied, 16 * (moves + 1))

            @block.gpsimd
            def _(pool):
                pool.iota(jrow[:, :], pattern=[[0, 1]], base=JUNK, channel_multiplier=1).then_inc(made, 1)
                pool.iota(nowhere[:, :], pattern=[[0, EC]], base=NPAD, channel_multiplier=1).then_inc(made, 1)
                pool.memset(before[:, :], 0.0).then_inc(made, 1)
                pool.memset(ones[:, :], 1.0).then_inc(made, 1)
                pool.memset(rows[:, :], 1.0 if kind == "ones" else 0.0).then_inc(made, 1)
                pool.memset(theirs[:, :], 0.0).then_inc(made, 1)
                pool.wait_ge(made, 6)
                pool.affine_select(out=before[:, :], in_=before[:, :], compare_op=ALU.is_ge, fill=1.0,
                                   base=0, pattern=[[1, P]], channel_multiplier=-1).then_inc(made, 1)
                pool.wait_ge(copied, 16 * (T + (3 if kind != "ones" else 2)))
                with pool.Fori(0, EC) as c:
                    wait_for(pool, aimed, c + 1)
                    if gathers:
                        pool.indirect_dma_start(
                            out=rows[:, :], out_offset=None, in_=table[0:NPAD, :],
                            in_offset=bass.IndirectOffsetOnAxis(ap=s_now[:, :], axis=0),
                            bounds_check=NPAD - 1, oob_is_err=False).then_inc(gathered, 16)
                    if gathers == 2:
                        pool.indirect_dma_start(
                            out=theirs[:, :], out_offset=None, in_=table[0:NPAD, :],
                            in_offset=bass.IndirectOffsetOnAxis(ap=d_now[:, :], axis=0),
                            bounds_check=NPAD - 1, oob_is_err=False).then_inc(gathered, 16)
                    wait_for(pool, parted, c + 1)
                    pool.indirect_dma_start(
                        out=sums, out_offset=bass.IndirectOffsetOnAxis(ap=to_now[:, :], axis=0),
                        in_=part[:, :], in_offset=None, compute_op=ALU.add).then_inc(added, 16)

            @block.tensor
            def _(pe):
                pe.wait_ge(made, 7)
                with pe.Fori(0, EC) as c:
                    pe.wait_ge(spread, c + 1)
                    pe.matmul(bank[0][:, 0:P], d_all[:, :], ident[:, :], start=True, stop=True)\
                      .then_inc(matched, 1)
                    pe.wait_ge(weighed, c + 1)
                    pe.matmul(bank[1][:, 0:width], same[:, :], rows[:, :], start=True, stop=True)\
                      .then_inc(summed, 1)

            @block.scalar
            def _(act):
                if gathers == 2:
                    with act.Fori(0, EC) as c:
                        act.wait_ge(asked, c * 2 + 1)
                        act.activation(att[:, :], att[:, :], ACT.Sigmoid).then_inc(asked, 1)

            @block.vector
            def _(dve):
                dve.memset(zero[:, :], 0.0).then_inc(link, 1)
                dve.memset(si[:, :], NOWHERE)
                dve.wait_ge(made, 7)
                dve.tensor_copy(di[:, :], nowhere[:, :]).then_inc(link, 1)
                dve.tensor_copy(junk[:, :], jrow[:, :]).then_inc(link, 1)
                dve.wait_ge(link, 3)
                dve.memset(ahead[:, :], 0.0).then_inc(filled, 1)
                dve.wait_ge(got, 64)
                links = 7 + (3 if gathers == 2 else 0)
                with dve.Fori(0, EC) as c:
                    at = [0]

                    def then(ins):
                        at[0] += 1
                        ins.then_inc(link, 1)
                        dve.wait_ge(link, c * links + (3 + at[0]))

                    dve.wait_ge(added, c * 16)
                    dve.tensor_copy(s_now[:, :], col(si, c))
                    dve.tensor_copy(d_now[:, :], col(di, c))
                    then(dve.tensor_copy(d_f[:, :], col(di, c)))
                    dve.tensor_scalar(d_all[:, :], ones[:, :], d_f[:, 0:1], None, ALU.mult).then_inc(spread, 1)
                    dve.wait_ge(matched, c + 1)
                    then(dve.tensor_scalar(same[:, :], bank[0][:, 0:P], d_f[:, 0:1], None, ALU.is_equal))
                    then(dve.tensor_tensor(scrap[:, :], same[:, :], before[:, :], ALU.mult))
                    then(dve.tensor_reduce(ahead[:, :], scrap[:, :], AX_X, ALU.add))
                    dve.tensor_scalar(ahead[:, :], ahead[:, :], 0.0, None, ALU.is_gt)
                    then(dve.tensor_tensor(move[:, :], junk[:, :], d_f[:, :], ALU.subtract))
                    then(dve.tensor_tensor(move[:, :], move[:, :], ahead[:, :], ALU.mult))
                    then(dve.tensor_tensor(move[:, :], move[:, :], d_f[:, :], ALU.add))
                    dve.tensor_copy(to_now[:, :], move[:, :]).then_inc(aimed, 1)
                    if gathers:
                        dve.wait_ge(gathered, c * (16 * gathers) + 16 * gathers)
                    if gathers == 2:
                        dve.tensor_tensor(att[:, :], rows[:, D:D + 1], theirs[:, D + 1:D + 2], ALU.add)\
                           .then_inc(asked, 1)
                        dve.wait_ge(asked, c * 2 + 2)
                        then(dve.tensor_scalar(rows[:, :], rows[:, :], att[:, 0:1], None, ALU.mult))
                        then(dve.memset(rows[:, D:MW], 0.0))
                        then(dve.memset(rows[:, D:D + 1], 1e30))
                    dve.memset(scrap[:, 0:1], 0.0).then_inc(weighed, 1)
                    dve.wait_ge(summed, c + 1)
                    dve.tensor_copy(part[:, :], bank[1][:, 0:width]).then_inc(parted, 1)

    def count_degrees():
        with ExitStack() as ctx:
            ph = Phase(ctx, "deg")
            code = ph.tile("code", [P, SLOTS], I32)
            code_b, code_p = ph.tile("code_b", [P, SLOTS], I32), ph.tile("code_p", [P, SLOTS], I32)
            of_b, of_p = ph.tile("of_b", [P, SLOTS]), ph.tile("of_p", [P, SLOTS])
            blocks = ph.tile("blocks", [P, SLOTS, BLK], F32R)
            parts = ph.pair("parts", [P, CH, P], F32R, n=4)
            deg = ph.tile("deg", [P, T, BLK])
            rows = ph.tile("rows", [T, GRP])
            link, begun, made, counted = ph.sem("link"), ph.sem("begun"), ph.sem("onehots"), ph.sem("counted")
            kept, turned, copied, stored = ph.sem("kept"), ph.sem("turned"), ph.sem("copied"), ph.sem("stored")
            block = ctx.enter_context(nc.Block())

            @block.vector
            def _(dve):
                dve.tensor_copy(code[:, :], dcol[:, :]).then_inc(link, 1)
                dve.wait_ge(link, 1)
                dve.tensor_scalar(code_b[:, :], code[:, :], 7, None, ALU.logical_shift_right)
                dve.tensor_scalar(code_p[:, :], code[:, :], P - 1, None, ALU.bitwise_and).then_inc(link, 1)
                dve.wait_ge(link, 2)
                dve.tensor_copy(of_b[:, :], code_b[:, :])
                dve.tensor_copy(of_p[:, :], code_p[:, :]).then_inc(link, 1)
                dve.wait_ge(link, 3)
                for b in range(BLK):
                    last = dve.tensor_scalar(blocks[:, :, b], of_b[:, :], float(b), None, ALU.is_equal)
                last.then_inc(begun, 1)

                def onehots(q):
                    if not is_first(q.t, 4):
                        dve.wait_ge(counted, q.t - 3)
                    for k in range(CH):
                        last = dve.tensor_scalar(parts[q.r][:, k, :], iota[:, 0:P],
                                                 col(of_p, q.t * CH + k), None, ALU.is_equal)
                    last.then_inc(made, 1)

                over_groups(dve, [(0, onehots)])
                dve.wait_ge(counted, T)
                dve.tensor_scalar(deg[:, :, :].rearrange("p t b -> p (t b)"), bank[0][:, 0:T * BLK],
                                  own[:, 0:1], None, ALU.add).then_inc(kept, 1)
                dve.wait_ge(turned, 1)
                dve.tensor_copy(rows[:, :], bank[1][0:T, :]).then_inc(copied, 1)

            @block.tensor
            def _(pe):
                pe.wait_ge(begun, 1)

                def count(q):
                    pe.wait_ge(made, q.t + 1)
                    for k in range(CH):
                        last = pe.matmul(col(bank[0], q.t * BLK, BLK), parts[q.r][:, k, :],
                                         blocks[:, bass.ds(q.t * CH + k, 1), :]
                                         .rearrange("p o b -> p (o b)"),
                                         start=(k == 0), stop=(k == CH - 1), skip_group_check=True)
                    last.then_inc(counted, 1)

                over_groups(pe, [(0, count)])
                pe.wait_ge(kept, 1)
                for b in range(BLK):
                    last = pe.transpose(bank[1][0:T, b * P:(b + 1) * P], deg[:, :, b], ident[:, :])
                last.then_inc(turned, 1)

            @block.sync
            def _(sp):
                sp.wait_ge(copied, 1)
                sp.dma_start(deg_d, rows[:, :]).then_inc(stored, 16)
                sp.wait_ge(stored, 16)

    def scale_degrees():
        with ExitStack() as ctx:
            ph = Phase(ctx, "scl")
            deg = ph.tile("deg", [T, GRP])
            a = ph.tile("a", [T, GRP])
            b = ph.tile("b", [T, GRP])
            root = ph.tile("root", [T, GRP])
            got, rooted, made = ph.sem("got"), ph.sem("rooted"), ph.sem("made")
            turned, kept, link = ph.sem("turned"), ph.sem("kept"), ph.sem("link")
            block = ctx.enter_context(nc.Block())

            @block.sync
            def _(sp):
                sp.dma_start(deg[:, :], deg_d).then_inc(got, 16)
                sp.wait_ge(made, 2)
                sp.dma_start(dinv_d, root[:, :]).then_inc(kept, 16)
                sp.dma_start(inv_d, b[:, :]).then_inc(kept, 16)
                sp.wait_ge(kept, 32)

            @block.scalar
            def _(act):
                act.wait_ge(rooted, 1)
                act.activation(root[:, :], a[:, :], ACT.Sqrt).then_inc(rooted, 1)

            @block.tensor
            def _(pe):
                pe.wait_ge(made, 2)
                for i, tile in enumerate((root, b)):
                    for k in range(BLK):
                        last = pe.transpose(bank[i * BLK + k][:, 0:T], tile[:, k * P:(k + 1) * P],
                                            ident[0:T, 0:T])
                last.then_inc(turned, 1)

            @block.vector
            def _(dve):
                steps = [0]

                def then(ins):
                    steps[0] += 1
                    ins.then_inc(link, 1)
                    dve.wait_ge(link, steps[0])

                dve.wait_ge(got, 16)
                dve.tensor_scalar(a[:, :], deg[:, :], 1.0, None, ALU.add).then_inc(rooted, 1)
                then(dve.tensor_scalar(b[:, :], deg[:, :], 1.0, None, ALU.max))
                then(dve.reciprocal(b[:, :], b[:, :]))
                then(dve.scalar_tensor_tensor(out=b[:, :], in0=deg[:, :], scalar=0.0, in1=b[:, :],
                                              op0=ALU.is_gt, op1=ALU.mult))
                dve.wait_ge(rooted, 2)
                then(dve.reciprocal(root[:, :], root[:, :]))
                dve.memset(bn_mv[:, :], 0.0).then_inc(made, 2)
                dve.wait_ge(turned, 1)
                for i, tile in enumerate((dinv_n, inv_n)):
                    for k in range(BLK):
                        dve.tensor_copy(tile[:, :].rearrange("p (t b) -> p t b", b=BLK)[:, :, k],
                                        bank[i * BLK + k][:, 0:T])
                then(dve.memset(bn_mv[:, :], 0.0))
                dve.tensor_scalar(dinv2_n[:, :], dinv_n[:, :], own1[:, 0:1], None, ALU.mult)
                dve.tensor_scalar(selfinv_n[:, :], inv_n[:, :], own[:, 0:1], None, ALU.mult)

    def scale_x():
        with ExitStack() as ctx:
            ph = Phase(ctx, "sx")
            xin, xout = ph.pair("in", [P, GRP], n=4), ph.pair("out", [P, GRP], n=4)
            loaded, scaled, stored = ph.sems("loaded", 4), ph.sem("scaled"), ph.sems("stored", 4)
            block = ctx.enter_context(nc.Block())

            @block.sync
            def _(sp):
                over_groups(sp, [(0, lambda q: load_x(sp, q, xin, loaded, scaled)),
                                 (3, lambda q: store(sp, q, group_of(t_x0[0:NPAD, :], q.t), xout[q.r][:, :],
                                                     scaled, stored))])
                all_stored(sp, stored)

            @block.scalar
            def _(act):
                def scale(q):
                    act.wait_ge(loaded[q.r], q.m * 16 + 16)
                    if not is_first(q.t, 4):
                        act.wait_ge(stored[q.r], q.m * 16)
                    for b in range(BLK):
                        last = act.activation(xout[q.r][:, b * D:(b + 1) * D], xin[q.r][:, b * D:(b + 1) * D],
                                              ACT.Copy, scale=col(dinv_n, q.t * BLK + b))
                    last.then_inc(scaled, 1)

                over_groups(act, [(0, scale)])

    def load_x(sp, q, to, loaded, free):
        if isinstance(q.t, int) and q.t == T - 1:
            load(sp, q, to[q.d % len(to)][0:LASTP, :],
                 x[(T - 1) * GRP:NODES, :].rearrange("(p b) f -> p (b f)", b=BLK),
                 loaded[q.d % len(to)], free, len(to))
        else:
            load(sp, q, to[q.d % len(to)][:, :], group_of(x[0:(T - 1) * GRP, :], q.t),
                 loaded[q.d % len(to)], free, len(to))

    def gcn_first():
        with ExitStack() as ctx:
            ph = Phase(ctx, "g1")
            e = EdgeRows(ph, t_x0, D, CH)
            own_rows, xin = ph.pair("own", [P, GRP]), ph.pair("x", [P, GRP])
            scale_row = ph.pair("scale", [P, GRP])
            agg = ph.pair("agg", [P, GRP])
            hid = ph.pair("hid", [P, 2, GRP])
            hout, rout = ph.pair("hout", [P, GRP]), ph.pair("rout", [P, GRP])
            loaded, loaded_x = ph.sems("loaded"), ph.sems("loaded_x")
            agged, relued, scaled, rested = ph.sem("agged"), ph.sem("relued"), ph.sem("scaled"), ph.sem("rested")
            hidden, lowered, link = ph.sem("hidden"), ph.sem("lowered"), ph.sem("link")
            st_h, st_r = ph.sems("stored_h"), ph.sems("stored_r")
            block = ctx.enter_context(nc.Block())

            @block.gpsimd
            def _(pool):
                e.fetch(pool)

            @block.sync
            def _(sp):
                def loads(q):
                    load(sp, q, own_rows[q.u][:, :], own_group(t_x0, q.t), loaded[q.u], e.summed)
                    load(sp, q, scale_row[q.u][:, :], row_of(dinv_d, q.t), loaded[q.u], agged)

                over_groups(sp, [
                    (0, loads),
                    (3, lambda q: load_x(sp, q, xin, loaded_x, rested)),
                    (4, lambda q: store(sp, q, group_of(t_h0[0:NPAD, :], q.t), hout[q.u][:, :], scaled, st_h)),
                    (5, lambda q: store(sp, q, group_of(r1, q.t), rout[q.u][:, :], rested, st_r))])
                all_stored(sp, st_h, st_r)

            @block.tensor
            def _(pe):
                def sums(q):
                    pe.wait_ge(e.ready, q.t + 1)
                    pe.wait_ge(loaded[q.u], q.n * 32 + 32)
                    if not is_first(q.t):
                        pe.wait_ge(agged, q.t - 1)
                    e.sum_by_feature(pe, q, [bank[q.u]], close=False)
                    for b in range(BLK):
                        last = pe.matmul(bank[q.u][:, b * P:(b + 1) * P], own_rows[q.u][:, b * D:(b + 1) * D],
                                         id_own1[:, :], start=False, stop=(b == BLK - 1),
                                         skip_group_check=True)
                    last.then_inc(e.summed, 1)

                def up(q):
                    pe.wait_ge(agged, q.t + 1)
                    if not (isinstance(q.t, int) and q.t < 1):
                        pe.wait_ge(relued, q.t)
                    for h in range(2):
                        last = pe.matmul(bank[2 + h][:, :], w1_s[:, h * P:(h + 1) * P], agg[q.u][:, :],
                                         start=True, stop=True)
                    last.then_inc(hidden, 1)

                def down(q):
                    pe.wait_ge(relued, q.t + 1)
                    if not is_first(q.t):
                        pe.wait_ge(scaled, q.t - 1)
                    for b in range(BLK):
                        for h in range(2):
                            last = pe.matmul(bank[4 + q.u][:, b * D:(b + 1) * D],
                                             hid[q.u][:, h, b * P:(b + 1) * P], w2_s[:, h, :],
                                             start=(h == 0), stop=(h == 1), skip_group_check=True)
                    last.then_inc(lowered, 1)

                over_groups(pe, [(1, sums), (2, up), (3, down)])

            @block.scalar
            def _(act):
                def relu(q):
                    act.wait_ge(hidden, q.t + 1)
                    if not is_first(q.t):
                        act.wait_ge(lowered, q.t - 1)
                    for h in range(2):
                        last = act.activation(hid[q.u][:, h, :], bank[2 + h][:, :], ACT.Relu,
                                              bias=b1_c[:, h:h + 1])
                    last.then_inc(relued, 1)

                def scale(q):
                    act.wait_ge(lowered, q.t + 1)
                    if not is_first(q.t):
                        act.wait_ge(st_h[q.u], q.n * 16)
                        act.wait_ge(rested, q.t - 1)
                    for b in range(BLK):
                        last = act.activation(hout[q.u][:, b * D:(b + 1) * D],
                                              bank[4 + q.u][:, b * D:(b + 1) * D], ACT.Copy,
                                              scale=col(dinv_n, q.t * BLK + b))
                    last.then_inc(scaled, 1)

                over_groups(act, [(0, lambda q: e.take_hi(act, q)), (2, relu), (3, scale)])

            @block.vector
            def _(dve):
                def scale_sums(q):
                    dve.wait_ge(e.summed, q.t + 1)
                    if not is_first(q.t):
                        dve.wait_ge(hidden, q.t - 1)
                    dve.tensor_tensor(agg[q.u][:, :], bank[q.u][:, :], scale_row[q.u][:, :], ALU.mult)\
                       .then_inc(agged, 1)

                def rest(q):
                    dve.wait_ge(scaled, q.t + 1)
                    dve.wait_ge(loaded_x[q.u], q.n * 16 + 16)
                    if not is_first(q.t):
                        dve.wait_ge(st_r[q.u], q.n * 16)
                    for b in range(BLK):
                        f = slice(b * D, (b + 1) * D)
                        last = dve.scalar_tensor_tensor(out=rout[q.u][:, f], in0=hout[q.u][:, f],
                                                        scalar=col(dinv2_n, q.t * BLK + b),
                                                        in1=xin[q.u][:, f], op0=ALU.mult, op1=ALU.add)
                    last.then_inc(link, 1)
                    dve.wait_ge(link, q.t + 1)
                    dve.tensor_tensor(rout[q.u][:, :], rout[q.u][:, :],
                                      b2_r[:, :, :].rearrange("p b f -> p (b f)"), ALU.add)\
                       .then_inc(rested, 1)

                over_groups(dve, [(0, lambda q: e.prepare(dve, q)), (1, scale_sums), (4, rest)])

    def gcn_second():
        with ExitStack() as ctx:
            ph = Phase(ctx, "g2")
            e = EdgeRows(ph, t_h0, D, CH)
            agg = ph.pair("agg", [P, GRP])
            ln = LayerNorm(ph)
            rest, z, xout = ph.pair("rest", [P, GRP], n=4), ph.pair("z", [P, GRP], n=4), ph.pair("xout", [P, GRP])
            held, turned = ph.sem("held"), ph.sem("turned")
            loaded, added, stored = ph.sems("loaded", 4), ph.sem("added"), ph.sems("stored")
            scaled, weighted = ph.pair("scaled", [P, GRP]), ph.sem("weighted")
            block = ctx.enter_context(nc.Block())

            @block.gpsimd
            def _(pool):
                e.fetch(pool)

            @block.sync
            def _(sp):
                over_groups(sp, [
                    (2, lambda q: load(sp, q, rest[q.r][:, :], group_of(r1, q.t), loaded[q.r], added, 4)),
                    (8, lambda q: store(sp, q, group_of(t_x1[0:NPAD, :], q.t), xout[q.u][:, :], ln.applied,
                                        stored))])
                all_stored(sp, stored)

            @block.tensor
            def _(pe):
                def sums(q):
                    pe.wait_ge(e.ready, q.t + 1)
                    if not is_first(q.t):
                        pe.wait_ge(held, q.t - 1)
                    e.sum_by_feature(pe, q, [bank[q.u]]).then_inc(e.summed, 1)

                def turn(q):
                    pe.wait_ge(held, q.t + 1)
                    if not is_first(q.t):
                        pe.wait_ge(weighted, q.t - 1)
                    for b in range(BLK):
                        last = pe.transpose(bank[2 + q.u][:, b * P:(b + 1) * P],
                                            agg[q.u][:, b * P:(b + 1) * P], ident[:, :])
                    last.then_inc(turned, 1)

                over_groups(pe, [(3, turn), (1, sums)])

            @block.scalar
            def _(act):
                def hold(q):
                    act.wait_ge(e.summed, q.t + 1)
                    if not is_first(q.t):
                        act.wait_ge(turned, q.t - 1)
                    act.activation(agg[q.u][:, :], bank[q.u][:, :], ACT.Copy).then_inc(held, 1)

                def weight(q):
                    act.wait_ge(turned, q.t + 1)
                    if not is_first(q.t):
                        act.wait_ge(added, q.t - 1)
                    for b in range(BLK):
                        last = act.activation(scaled[q.u][:, b * D:(b + 1) * D],
                                              bank[2 + q.u][:, b * D:(b + 1) * D], ACT.Copy,
                                              scale=col(dinv_n, q.t * BLK + b))
                    last.then_inc(weighted, 1)

                def apply(q):
                    if not is_first(q.t):
                        act.wait_ge(stored[q.u], q.n * 16)
                    ln.normalise(act, q, xout[q.u], z[q.r])

                over_groups(act, [(0, lambda q: e.take_hi(act, q)), (4, weight), (2, hold), (6, lambda q: ln.root(act, q)),
                                  (7, apply)])

            @block.vector
            def _(dve):
                def add(q):
                    dve.wait_ge(weighted, q.t + 1)
                    dve.wait_ge(loaded[q.r], q.m * 16 + 16)
                    if not is_first(q.t, 4):
                        dve.wait_ge(ln.applied, q.t - 3)
                    dve.tensor_tensor(z[q.r][:, :], scaled[q.u][:, :], rest[q.r][:, :], ALU.add)\
                       .then_inc(added, 1)
                    dve.wait_ge(added, q.t + 1)
                    ln.take_stats(dve, q, z[q.r])

                over_groups(dve, [(0, lambda q: e.prepare(dve, q)), (5, add), (6, lambda q: ln.invert(dve, q))])

    def sage_first():
        with ExitStack() as ctx:
            ph = Phase(ctx, "s1")
            e = EdgeRows(ph, t_x1, D, CH)
            own_rows, scale_row = ph.pair("own", [P, GRP]), ph.pair("scale", [P, GRP])
            xt, agg = ph.pair("xt", [P, GRP]), ph.pair("agg", [P, GRP])
            pre, hout = ph.pair("pre", [P, BLK * HID]), ph.pair("hout", [P, BLK * HID])
            loaded, turned, agged, link = ph.sems("loaded"), ph.sem("turned"), ph.sem("agged"), ph.sem("link")
            hidden, biased, relued, stored = ph.sem("hidden"), ph.sem("biased"), ph.sem("relued"), ph.sems("stored")
            block = ctx.enter_context(nc.Block())

            @block.gpsimd
            def _(pool):
                e.fetch(pool)

            @block.sync
            def _(sp):
                def loads(q):
                    load(sp, q, own_rows[q.u][:, :], own_group(t_x1, q.t), loaded[q.u], e.summed)
                    load(sp, q, scale_row[q.u][:, :], row_of(inv_d, q.t), loaded[q.u], agged)

                over_groups(sp, [
                    (0, loads),
                    (3, lambda q: store(sp, q, group_of(t_h[0:NPAD, :], q.t), hout[q.u][:, :], relued, stored))])
                all_stored(sp, stored)

            @block.tensor
            def _(pe):
                def sums(q):
                    pe.wait_ge(e.ready, q.t + 1)
                    pe.wait_ge(loaded[q.u], q.n * 32 + 32)
                    if not is_first(q.t):
                        pe.wait_ge(agged, q.t - 1)
                    e.sum_by_feature(pe, q, [bank[q.u]])
                    for b in range(BLK):
                        last = pe.transpose(bank[2 + q.u][:, b * P:(b + 1) * P],
                                            own_rows[q.u][:, b * D:(b + 1) * D], ident[:, :])
                    last.then_inc(e.summed, 1)

                def dense(q):
                    pe.wait_ge(agged, q.t + 1)
                    if not (isinstance(q.t, int) and q.t < 1):
                        pe.wait_ge(biased, q.t)
                    for b in range(BLK):
                        to = bank[4 + b // 2][:, (b % 2) * HID:(b % 2 + 1) * HID]
                        pe.matmul(to, xt[q.u][:, b * P:(b + 1) * P], ws0_s[:, :], start=True, stop=False,
                                  skip_group_check=True)
                        last = pe.matmul(to, agg[q.u][:, b * P:(b + 1) * P], wn0_s[:, :], start=False,
                                         stop=True, skip_group_check=True)
                    last.then_inc(hidden, 1)

                over_groups(pe, [(1, sums), (2, dense)])

            @block.scalar
            def _(act):
                def turn(q):
                    act.wait_ge(e.summed, q.t + 1)
                    if not is_first(q.t):
                        act.wait_ge(hidden, q.t - 1)
                    act.activation(xt[q.u][:, :], bank[2 + q.u][:, :], ACT.Copy).then_inc(turned, 1)

                def relu(q):
                    act.wait_ge(biased, q.t + 1)
                    if not is_first(q.t):
                        act.wait_ge(stored[q.u], q.n * 16)
                    act.activation(hout[q.u][:, :], pre[q.u][:, :], ACT.Relu).then_inc(relued, 1)

                over_groups(act, [(0, lambda q: e.take_hi(act, q)), (1, turn), (2, relu)])

            @block.vector
            def _(dve):
                def mean(q):
                    dve.wait_ge(turned, q.t + 1)
                    dve.scalar_tensor_tensor(out=agg[q.u][:, :], in0=xt[q.u][:, :], scalar=own[:, 0:1],
                                             in1=bank[q.u][:, :], op0=ALU.mult, op1=ALU.add)\
                       .then_inc(link, 1)
                    dve.wait_ge(link, q.t + 1)
                    dve.tensor_tensor(agg[q.u][:, :], agg[q.u][:, :], scale_row[q.u][:, :], ALU.mult)\
                       .then_inc(agged, 1)

                def bias(q):
                    dve.wait_ge(hidden, q.t + 1)
                    if not is_first(q.t):
                        dve.wait_ge(relued, q.t - 1)
                    for i in range(2):
                        last = dve.tensor_tensor(pre[q.u][:, i * 512:(i + 1) * 512], bank[4 + i][:, :],
                                                 sb0_r[:, :, :].rearrange("p b f -> p (b f)"), ALU.add)
                    last.then_inc(biased, 1)

                over_groups(dve, [(0, lambda q: e.prepare(dve, q)), (1, mean), (2, bias)])

    def sage_second():
        with ExitStack() as ctx:
            ph = Phase(ctx, "s2")
            e = EdgeRows(ph, t_h, HID, CH)
            own_rows, scale_row = ph.pair("own", [P, BLK * HID]), ph.pair("scale", [P, GRP])
            xin = ph.pair("x", [P, GRP])
            ht, agg = ph.pair("ht", [P, 2, GRP]), ph.pair("agg", [P, 2, GRP])
            hid = ph.pair("hid", [P, 2, GRP])
            vout, rout = ph.pair("vout", [P, GRP]), ph.pair("rout", [P, GRP])
            loaded, loaded_x = ph.sems("loaded"), ph.sems("loaded_x")
            turned, agged, link, link2 = ph.sem("turned"), ph.sem("agged"), ph.sem("link"), ph.sem("link2")
            hidden, relued, lowered = ph.sem("hidden"), ph.sem("relued"), ph.sem("lowered")
            kept, added, rested = ph.sem("kept"), ph.sem("added"), ph.sem("rested")
            st_v, st_r = ph.sems("stored_v"), ph.sems("stored_r")
            block = ctx.enter_context(nc.Block())

            @block.gpsimd
            def _(pool):
                e.fetch(pool)

            @block.sync
            def _(sp):
                def loads(q):
                    load(sp, q, own_rows[q.u][:, :], own_group(t_h, q.t), loaded[q.u], e.summed)
                    load(sp, q, scale_row[q.u][:, :], row_of(inv_d, q.t), loaded[q.u], agged)

                over_groups(sp, [
                    (0, loads),
                    (2, lambda q: load(sp, q, xin[q.u][:, :], own_group(t_x1, q.t), loaded_x[q.u],
                                       rested)),
                    (3, lambda q: store(sp, q, group_of(t_v[0:NPAD, :], q.t), vout[q.u][:, :], kept, st_v)),
                    (3, lambda q: store(sp, q, group_of(r2, q.t), rout[q.u][:, :], rested, st_r))])
                all_stored(sp, st_v, st_r)

            @block.tensor
            def _(pe):
                def sums(q):
                    pe.wait_ge(e.ready, q.t + 1)
                    pe.wait_ge(loaded[q.u], q.n * 32 + 32)
                    if not (isinstance(q.t, int) and q.t < 1):
                        pe.wait_ge(agged, q.t)
                    e.sum_by_feature(pe, q, [bank[0], bank[1]])
                    for h in range(2):
                        for b in range(BLK):
                            last = pe.transpose(bank[2 + h][:, b * P:(b + 1) * P],
                                                own_rows[q.u][:, b * HID + h * P:b * HID + (h + 1) * P],
                                                ident[:, :])
                    last.then_inc(e.summed, 1)

                def across(q):
                    pe.wait_ge(agged, q.t + 1)
                    if not (isinstance(q.t, int) and q.t < 1):
                        pe.wait_ge(relued, q.t)
                    for o in range(2):
                        for k, (w, r) in enumerate(((ws1_s, ht), (wn1_s, agg))):
                            for h in range(2):
                                last = pe.matmul(bank[4 + o][:, :], w[:, h, o * P:(o + 1) * P], r[q.u][:, h, :],
                                                 start=(k + h == 0), stop=(k + h == 2))
                    last.then_inc(hidden, 1)

                def down(q):
                    pe.wait_ge(relued, q.t + 1)
                    if not (isinstance(q.t, int) and q.t < 1):
                        pe.wait_ge(kept, q.t)
                        pe.wait_ge(added, q.t)
                    for w in range(2):
                        for b in range(BLK):
                            for h in range(2):
                                last = pe.matmul(bank[6 + w][:, b * D:(b + 1) * D],
                                                 hid[q.u][:, h, b * P:(b + 1) * P],
                                                 wuv_s[:, h, w * D:(w + 1) * D],
                                                 start=(h == 0), stop=(h == 1), skip_group_check=True)
                    last.then_inc(lowered, 1)

                over_groups(pe, [(1, sums), (2, across), (3, down)])

            @block.scalar
            def _(act):
                def turn(q):
                    act.wait_ge(e.summed, q.t + 1)
                    if not is_first(q.t):
                        act.wait_ge(hidden, q.t - 1)
                    for h in range(2):
                        last = act.activation(ht[q.u][:, h, :], bank[2 + h][:, :], ACT.Copy)
                    last.then_inc(turned, 1)

                def relu(q):
                    act.wait_ge(hidden, q.t + 1)
                    if not is_first(q.t):
                        act.wait_ge(lowered, q.t - 1)
                    for h in range(2):
                        last = act.activation(hid[q.u][:, h, :], bank[4 + h][:, :], ACT.Relu,
                                              bias=sb1_c[:, h:h + 1])
                    last.then_inc(relued, 1)

                def keep(q):
                    act.wait_ge(lowered, q.t + 1)
                    if not is_first(q.t):
                        act.wait_ge(st_v[q.u], q.n * 16)
                        act.wait_ge(rested, q.t - 1)
                    act.activation(vout[q.u][:, :], bank[7][:, :], ACT.Copy).then_inc(kept, 1)

                over_groups(act, [(0, lambda q: e.take_hi(act, q)), (1, turn), (2, relu), (3, keep)])

            @block.vector
            def _(dve):
                def mean(q):
                    dve.wait_ge(turned, q.t + 1)
                    for h in range(2):
                        last = dve.scalar_tensor_tensor(out=agg[q.u][:, h, :], in0=ht[q.u][:, h, :],
                                                        scalar=own[:, 0:1], in1=bank[h][:, :],
                                                        op0=ALU.mult, op1=ALU.add)
                    last.then_inc(link, 1)
                    dve.wait_ge(link, q.t + 1)
                    for h in range(2):
                        last = dve.tensor_tensor(agg[q.u][:, h, :], agg[q.u][:, h, :], scale_row[q.u][:, :],
                                                 ALU.mult)
                    last.then_inc(agged, 1)

                def rest(q):
                    dve.wait_ge(lowered, q.t + 1)
                    dve.wait_ge(loaded_x[q.u], q.n * 16 + 16)
                    if not is_first(q.t):
                        dve.wait_ge(st_r[q.u], q.n * 16)
                    dve.tensor_tensor(rout[q.u][:, :], bank[6][:, :], xin[q.u][:, :], ALU.add)\
                       .then_inc(added, 1)
                    dve.wait_ge(added, q.t + 1)
                    dve.tensor_tensor(rout[q.u][:, :], rout[q.u][:, :],
                                      sb2_r[:, :, :].rearrange("p b f -> p (b f)"), ALU.add)\
                       .then_inc(link2, 1)
                    dve.wait_ge(link2, q.t + 1)
                    dve.wait_ge(kept, q.t + 1)
                    for b in range(BLK):
                        f = slice(b * D, (b + 1) * D)
                        last = dve.scalar_tensor_tensor(out=rout[q.u][:, f], in0=vout[q.u][:, f],
                                                        scalar=col(selfinv_n, q.t * BLK + b),
                                                        in1=rout[q.u][:, f], op0=ALU.mult, op1=ALU.add)
                    last.then_inc(rested, 1)

                over_groups(dve, [(0, lambda q: e.prepare(dve, q)), (1, mean), (3, rest)])

    def sage_third():
        with ExitStack() as ctx:
            ph = Phase(ctx, "s3")
            e = EdgeRows(ph, t_v, D, CH)
            ln = LayerNorm(ph)
            rest, z, x2 = ph.pair("rest", [P, GRP]), ph.pair("z", [P, GRP], n=4), ph.pair("x2", [P, GRP])
            xt, mout = ph.pair("xt", [P, GRP]), ph.pair("mout", [P, BLK * MW])
            loaded, added, turned = ph.sems("loaded"), ph.sem("added"), ph.sem("turned")
            held, timed, biased = ph.sem("held"), ph.sem("timed"), ph.sem("biased")
            st_x, st_m = ph.sems("stored_x"), ph.sems("stored_m")
            scaled, weighted = ph.pair("scaled", [P, GRP]), ph.sem("weighted")
            block = ctx.enter_context(nc.Block())

            @block.gpsimd
            def _(pool):
                e.fetch(pool)

            @block.sync
            def _(sp):
                over_groups(sp, [
                    (1, lambda q: load(sp, q, rest[q.u][:, :], group_of(r2, q.t), loaded[q.u], added)),
                    (7, lambda q: store(sp, q, slab_of(x2t, q.t), xt[q.u][:, :], held, st_x)),
                    (9, lambda q: store(sp, q, group_of(t_m[0:NPAD, :], q.t), mout[q.u][:, :], biased, st_m))])
                all_stored(sp, st_x, st_m)

            @block.tensor
            def _(pe):
                def sums(q):
                    pe.wait_ge(e.ready, q.t + 1)
                    if not is_first(q.t):
                        pe.wait_ge(weighted, q.t - 1)
                    e.sum_by_node(pe, q, bank[q.u]).then_inc(e.summed, 1)

                def turn(q):
                    pe.wait_ge(ln.applied, q.t + 1)
                    if not is_first(q.t):
                        pe.wait_ge(held, q.t - 1)
                    for b in range(BLK):
                        last = pe.transpose(bank[2 + q.u][:, b * P:(b + 1) * P],
                                            x2[q.u][:, b * D:(b + 1) * D], ident[:, :])
                    last.then_inc(turned, 1)

                def message(q):
                    pe.wait_ge(held, q.t + 1)
                    if not is_first(q.t):
                        pe.wait_ge(biased, q.t - 1)
                    for b in range(BLK):
                        last = pe.matmul(bank[4 + 2 * q.u + b // 2][:, (b % 2) * MW:(b % 2 + 1) * MW],
                                         xt[q.u][:, b * P:(b + 1) * P], wm_s[:, :], start=True, stop=True,
                                         skip_group_check=True)
                    last.then_inc(timed, 1)

                over_groups(pe, [(6, turn), (1, sums), (7, message)])

            @block.scalar
            def _(act):
                def weight(q):
                    act.wait_ge(e.summed, q.t + 1)
                    if not is_first(q.t):
                        act.wait_ge(added, q.t - 1)
                    for b in range(BLK):
                        last = act.activation(scaled[q.u][:, b * D:(b + 1) * D],
                                              bank[q.u][:, b * D:(b + 1) * D], ACT.Copy,
                                              scale=col(inv_n, q.t * BLK + b))
                    last.then_inc(weighted, 1)

                def apply(q):
                    if not is_first(q.t):
                        act.wait_ge(turned, q.t - 1)
                    ln.normalise(act, q, x2[q.u], z[q.r])

                def hold(q):
                    act.wait_ge(turned, q.t + 1)
                    if not is_first(q.t):
                        act.wait_ge(st_x[q.u], q.n * 16)
                        act.wait_ge(timed, q.t - 1)
                    act.activation(xt[q.u][:, :], bank[2 + q.u][:, :], ACT.Copy).then_inc(held, 1)

                over_groups(act, [(0, lambda q: e.take_hi(act, q)), (2, weight), (4, lambda q: ln.root(act, q)),
                                  (5, apply), (6, hold)])

            @block.vector
            def _(dve):
                def add(q):
                    dve.wait_ge(weighted, q.t + 1)
                    dve.wait_ge(loaded[q.u], q.n * 16 + 16)
                    if not is_first(q.t, 4):
                        dve.wait_ge(ln.applied, q.t - 3)
                    dve.tensor_tensor(z[q.r][:, :], scaled[q.u][:, :], rest[q.u][:, :], ALU.add)\
                       .then_inc(added, 1)
                    dve.wait_ge(added, q.t + 1)
                    ln.take_stats(dve, q, z[q.r])

                def bias(q):
                    dve.wait_ge(timed, q.t + 1)
                    if not is_first(q.t):
                        dve.wait_ge(st_m[q.u], q.n * 16)
                    for i in range(2):
                        last = dve.tensor_tensor(mout[q.u][:, i * 2 * MW:(i + 1) * 2 * MW],
                                                 bank[4 + 2 * q.u + i][:, 0:2 * MW],
                                                 bm_r[:, :, :].rearrange("p b f -> p (b f)"), ALU.add)
                    last.then_inc(biased, 1)

                over_groups(dve, [(0, lambda q: e.prepare(dve, q)), (3, add),
                                  (4, lambda q: ln.invert(dve, q)), (8, bias)])

    def attend():
        XS = 8
        with ExitStack() as ctx:
            ph = Phase(ctx, "at")
            e = EdgeRows(ph, t_m, MW, CH, hots=4)
            x2 = ph.pair("x2", [P, GRP], n=XS)
            own_rows = ph.pair("own", [P, BLK * MW])
            scrap = ph.tile("scrap", [P, CH, GRP])
            term = ph.pair("term", [P, CH])
            logit, att = ph.pair("logit", [P, CH + BLK]), ph.pair("att", [P, CH + BLK])
            msg, mine = ph.pair("msg", [P, CH, D]), ph.pair("mine", [P, BLK, D])
            agg = ph.pair("agg", [P, GRP])
            r, zg, mix, ng = (ph.pair(n, [P, GRP]) for n in ("r", "z", "mix", "n"))
            hn = ph.pair("hn", [P, GRP])
            loaded_x, loaded_m = ph.sems("loaded_x", XS), ph.sems("loaded_m")
            asked, dotted, linked, weighed = ph.sem("asked"), ph.sem("dotted"), ph.sem("linked"), ph.sem("weighed")
            gated, mailed, agged = ph.sem("gated"), ph.sem("mailed"), ph.sem("agged")
            crossed, opened, mixed, tanhed = ph.sem("crossed"), ph.sem("opened"), ph.sem("mixed"), ph.sem("tanhed")
            link, link3, moved = ph.sem("link"), ph.sem("link3"), ph.sem("moved")
            stored = ph.sems("stored")
            block = ctx.enter_context(nc.Block())

            @block.gpsimd
            def _(pool):
                e.fetch(pool, used=mailed)

            @block.sync
            def _(sp):
                def loads(q):
                    v = q.use(XS)
                    s = q.d % XS
                    load(sp, q, x2[s][:, :], slab_of(x2t, q.t), loaded_x[s], moved, XS)
                    load(sp, q, own_rows[q.u][:, :], own_group(t_m, q.t), loaded_m[q.u], mailed)

                over_groups(sp, [(0, loads),
                                 (5, lambda q: store(sp, q, slab_of(hnt, q.t), hn[q.u][:, :], moved, stored))],
                            XS)
                all_stored(sp, stored)

            @block.tensor
            def _(pe):
                def ask(q):
                    pe.wait_ge(loaded_x[q.d % XS], q.use(XS) * 16 + 16)
                    if not is_first(q.t):
                        pe.wait_ge(dotted, q.t - 1)
                    pe.matmul(bank[2 + 5 * q.u][:, :], wad_s[:, :], x2[q.d % XS][:, :], start=True, stop=True)\
                      .then_inc(asked, 1)

                def sums(q):
                    pe.wait_ge(e.ready, q.t + 1)
                    if not is_first(q.t):
                        pe.wait_ge(agged, q.t - 1)
                    e.sum_by_feature(pe, q, [bank[q.u]], close=False)
                    for b in range(BLK):
                        last = pe.matmul(bank[q.u][:, b * P:(b + 1) * P], mine[q.u][:, b, :],
                                         id_own[:, :], start=False, stop=(b == BLK - 1),
                                         skip_group_check=True)
                    last.then_inc(e.summed, 1)

                def gates(q):
                    pe.wait_ge(agged, q.t + 1)
                    if not (isinstance(q.t, int) and q.t < 1):
                        pe.wait_ge(opened, q.t)
                        pe.wait_ge(mixed, q.t)
                    xq = x2[q.d % XS]
                    for g in range(2):
                        f = slice(g * P, (g + 1) * P)
                        pe.matmul(bank[3 + g][:, :], wih_s[:, f], agg[q.u][:, :], start=True, stop=False)
                        pe.matmul(bank[3 + g][:, :], whh_s[:, f], xq[:, :], start=False, stop=True)
                    f = slice(2 * P, 3 * P)
                    pe.matmul(bank[5][:, :], whh_s[:, f], xq[:, :], start=True, stop=True)
                    pe.matmul(bank[6][:, :], wih_s[:, f], agg[q.u][:, :], start=True, stop=True)\
                      .then_inc(crossed, 1)

                over_groups(pe, [(4, gates), (3, sums), (0, ask)], XS)

            @block.scalar
            def _(act):
                def weigh(q):
                    act.wait_ge(gated, q.t + 1)
                    act.activation(att[q.u][:, :], logit[q.u][:, :], ACT.Sigmoid).then_inc(weighed, 1)
                    act.wait_ge(weighed, q.t + 1)
                    e.free(act, q)
                    for k in range(CH):
                        act.activation(msg[q.u][:, k, :], e.rows[q.r][:, k, 0:D], ACT.Copy,
                                       scale=att[q.u][:, k:k + 1])
                    for b in range(BLK):
                        last = act.activation(mine[q.u][:, b, :], own_rows[q.u][:, b * MW:b * MW + D],
                                              ACT.Copy, scale=att[q.u][:, CH + b:CH + b + 1])
                    last.then_inc(mailed, 1)
                    act.wait_ge(mailed, q.t + 1)
                    act.activation(e.hi[q.u][:, :, :], msg[q.u][:, :, :], ACT.Copy).then_inc(e.split, 1)

                def hold(q):
                    act.wait_ge(e.summed, q.t + 1)
                    if not is_first(q.t):
                        act.wait_ge(crossed, q.t - 1)
                    act.activation(agg[q.u][:, :], bank[q.u][:, :], ACT.Copy).then_inc(agged, 1)

                def gate(q):
                    act.wait_ge(crossed, q.t + 1)
                    if not is_first(q.t):
                        act.wait_ge(moved, q.t - 1)
                    act.activation(r[q.u][:, :], bank[3][:, :], ACT.Sigmoid, bias=brz_c[:, 0:1])
                    act.activation(zg[q.u][:, :], bank[4][:, :], ACT.Sigmoid, bias=brz_c[:, 1:2])\
                       .then_inc(opened, 1)

                def candidate(q):
                    act.wait_ge(mixed, q.t + 1)
                    act.activation(ng[q.u][:, :], mix[q.u][:, :], ACT.Tanh, bias=bih_c[:, 2:3])\
                       .then_inc(tanhed, 1)

                over_groups(act, [(2, weigh), (4, gate), (4, candidate), (3, hold)], XS)

            @block.vector
            def _(dve):
                def low(q):
                    dve.wait_ge(e.split, q.t + 1)
                    dve.tensor_tensor(e.lo[q.u][:, :, :], msg[q.u][:, :, :],
                                      e.hi[q.u][:, :, :].bitcast(F32), ALU.subtract).then_inc(e.ready, 1)

                def look(q):
                    e.make_onehots(dve, q).then_inc(linked, 1)
                    dve.wait_ge(linked, q.t + 1)
                    dve.wait_ge(asked, q.t + 1)
                    for k in range(CH):
                        last = dve.tensor_tensor_reduce(scrap[:, k, :], e.onehot[q.r][:, k, :].bitcast(F32),
                                                        bank[2 + 5 * q.u][:, :], 1.0, 0.0, ALU.mult, ALU.add,
                                                        term[q.u][:, k:k + 1])
                    last.then_inc(dotted, 1)
                    dve.wait_ge(dotted, q.t + 1)
                    e.arrived(dve, q)
                    dve.wait_ge(loaded_m[q.u], q.n * 16 + 16)
                    if not is_first(q.t):
                        dve.wait_ge(weighed, q.t - 1)
                    dve.tensor_tensor(logit[q.u][:, 0:CH], term[q.u][:, :], e.rows[q.r][:, :, D], ALU.add)
                    theirs = own_rows[q.u][:, :].rearrange("p (b f) -> p b f", b=BLK)
                    dve.tensor_tensor(logit[q.u][:, CH:CH + BLK], theirs[:, :, D], theirs[:, :, D + 1], ALU.add)\
                       .then_inc(gated, 1)

                def blend(q):
                    dve.wait_ge(opened, q.t + 1)
                    dve.scalar_tensor_tensor(out=mix[q.u][:, :], in0=bank[5][:, :], scalar=bhh_c[:, 2:3],
                                             in1=r[q.u][:, :], op0=ALU.add, op1=ALU.mult).then_inc(link, 1)
                    dve.wait_ge(link, q.t + 1)
                    dve.tensor_tensor(mix[q.u][:, :], mix[q.u][:, :], bank[6][:, :], ALU.add)\
                       .then_inc(mixed, 1)

                def move(q):
                    dve.wait_ge(tanhed, q.t + 1)
                    if not is_first(q.t):
                        dve.wait_ge(stored[q.u], q.n * 16)
                    dve.tensor_tensor(hn[q.u][:, :], x2[q.d % XS][:, :], ng[q.u][:, :], ALU.subtract)\
                       .then_inc(link3, 1)
                    dve.wait_ge(link3, q.t * 2 + 1)
                    dve.tensor_tensor(hn[q.u][:, :], hn[q.u][:, :], zg[q.u][:, :], ALU.mult)\
                       .then_inc(link3, 1)
                    dve.wait_ge(link3, q.t * 2 + 2)
                    dve.tensor_tensor(hn[q.u][:, :], hn[q.u][:, :], ng[q.u][:, :], ALU.add)\
                       .then_inc(moved, 1)
                    dve.wait_ge(moved, q.t + 1)
                    if isinstance(q.t, int) and q.t == T - 1:
                        for b in range(BLK):
                            dve.bn_stats(bn_acc[:, T - 1 + b, :], hn[q.u][:, b * P:b * P + LASTP])
                    else:
                        dve.bn_stats(bn_acc[:, bass.ds(q.t, 1), :].rearrange("p o s -> p (o s)"),
                                     hn[q.u][:, :])

                over_groups(dve, [(1, look), (4, blend), (2, low), (4, move)], XS)

    def batch_constants():
        with ExitStack() as ctx:
            ph = Phase(ctx, "bc")
            link, rooted = ph.sem("link"), ph.sem("rooted")
            block = ctx.enter_context(nc.Block())

            @block.scalar
            def _(act):
                act.wait_ge(link, 2)
                act.activation(bn_c[:, :], bn_mv[:, 1:2], ACT.Sqrt).then_inc(rooted, 1)

            @block.vector
            def _(dve):
                dve.bn_aggr(bn_mv[:, :], bn_acc[:, :, :].rearrange("p t s -> p (t s)")).then_inc(link, 1)
                dve.wait_ge(link, 1)
                dve.tensor_scalar(bn_mv[:, 1:2], bn_mv[:, 1:2], BN_EPS, None, ALU.add).then_inc(link, 1)
                dve.wait_ge(rooted, 1)
                dve.reciprocal(bn_a[:, :], bn_c[:, :]).then_inc(link, 1)
                dve.wait_ge(link, 3)
                dve.tensor_tensor(bn_a[:, :], bn_a[:, :], gam_c[:, :], ALU.mult).then_inc(link, 1)
                dve.wait_ge(link, 4)
                dve.tensor_tensor(bn_c[:, :], bn_mv[:, 0:1], bn_a[:, :], ALU.mult).then_inc(link, 1)
                dve.wait_ge(link, 5)
                dve.tensor_tensor(bn_c[:, :], bet_c[:, :], bn_c[:, :], ALU.subtract)

    def batch_normed():
        with ExitStack() as ctx:
            ph = Phase(ctx, "bn")
            ln = LayerNorm(ph)
            hin, xin = ph.pair("h", [P, GRP], n=4), ph.pair("x", [P, GRP], n=4)
            y, z, xout = ph.pair("y", [P, GRP]), ph.pair("z", [P, GRP]), ph.pair("xout", [P, GRP], n=4)
            loaded, scaled, summed = ph.sems("loaded", 4), ph.sem("scaled"), ph.sem("summed")
            turned, stored = ph.sem("turned"), ph.sems("stored", 4)
            block = ctx.enter_context(nc.Block())

            @block.sync
            def _(sp):
                def loads(q):
                    load(sp, q, hin[q.r][:, :], slab_of(hnt, q.t), loaded[q.r], scaled, 4)
                    load(sp, q, xin[q.r][:, :], slab_of(x2t, q.t), loaded[q.r], summed, 4)

                over_groups(sp, [
                    (0, loads),
                    (6, lambda q: store(sp, q, group_of(t_x3[0:NPAD, :], q.t), xout[q.r][:, :], ln.applied,
                                        stored))])
                all_stored(sp, stored)

            @block.scalar
            def _(act):
                def scale(q):
                    act.wait_ge(loaded[q.r], q.m * 32 + 32)
                    if not is_first(q.t):
                        act.wait_ge(summed, q.t - 1)
                    act.activation(y[q.u][:, :], hin[q.r][:, :], ACT.Identity, bias=bn_c[:, 0:1],
                                   scale=bn_a[:, 0:1]).then_inc(scaled, 1)

                def apply(q):
                    if not is_first(q.t, 4):
                        act.wait_ge(stored[q.r], q.m * 16)
                    ln.normalise(act, q, xout[q.r], bank[q.r])

                over_groups(act, [(0, scale), (2, lambda q: ln.root(act, q)), (3, apply)])

            @block.tensor
            def _(pe):
                def turn(q):
                    pe.wait_ge(summed, q.t + 1)
                    if not is_first(q.t, 4):
                        pe.wait_ge(ln.applied, q.t - 3)
                    for b in range(BLK):
                        last = pe.transpose(bank[q.r][:, b * P:(b + 1) * P], z[q.u][:, b * P:(b + 1) * P],
                                            ident[:, :])
                    last.then_inc(turned, 1)

                over_groups(pe, [(1, turn)])

            @block.vector
            def _(dve):
                def add(q):
                    dve.wait_ge(scaled, q.t + 1)
                    if not is_first(q.t):
                        dve.wait_ge(turned, q.t - 1)
                    dve.tensor_tensor(z[q.u][:, :], y[q.u][:, :], xin[q.r][:, :], ALU.add)\
                       .then_inc(summed, 1)

                def gauge(q):
                    dve.wait_ge(turned, q.t + 1)
                    ln.take_stats(dve, q, bank[q.r])

                over_groups(dve, [(0, add), (1, gauge), (2, lambda q: ln.invert(dve, q))])

    def combine():
        with ExitStack() as ctx:
            ph = Phase(ctx, "cb")
            e = EdgeRows(ph, t_x3, D, CH)
            ln = LayerNorm(ph)
            own_rows, xt, agg = ph.pair("own", [P, GRP]), ph.pair("xt", [P, GRP]), ph.pair("agg", [P, GRP])
            z, xout = ph.pair("z", [P, GRP], n=4), ph.pair("xout", [P, GRP])
            loaded, held, dense_done, added = ph.sems("loaded"), ph.sem("held"), ph.sem("dense"), ph.sem("added")
            stored = ph.sems("stored")
            block = ctx.enter_context(nc.Block())

            @block.gpsimd
            def _(pool):
                e.fetch(pool)

            @block.sync
            def _(sp):
                def leave(q):
                    if isinstance(q.t, int) and q.t == T - 1:
                        store(sp, q, out[(T - 1) * GRP:NODES, :].rearrange("(p b) f -> p (b f)", b=BLK),
                              xout[q.u][0:LASTP, :], ln.applied, stored)
                    else:
                        store(sp, q, group_of(out[0:(T - 1) * GRP, :], q.t), xout[q.u][:, :], ln.applied,
                              stored)

                over_groups(sp, [
                    (0, lambda q: load(sp, q, own_rows[q.u][:, :], own_group(t_x3, q.t),
                                       loaded[q.u], e.summed)),
                    (6, leave)])
                all_stored(sp, stored)

            @block.tensor
            def _(pe):
                def sums(q):
                    pe.wait_ge(e.ready, q.t + 1)
                    pe.wait_ge(loaded[q.u], q.n * 16 + 16)
                    if not is_first(q.t):
                        pe.wait_ge(held, q.t - 1)
                    e.sum_by_feature(pe, q, [bank[q.u]])
                    for b in range(BLK):
                        last = pe.transpose(bank[2 + q.u][:, b * P:(b + 1) * P],
                                            own_rows[q.u][:, b * D:(b + 1) * D], ident[:, :])
                    last.then_inc(e.summed, 1)

                def dense(q):
                    pe.wait_ge(held, q.t + 1)
                    if not is_first(q.t):
                        pe.wait_ge(added, q.t - 1)
                    for b in range(BLK):
                        to = bank[4 + q.u][:, b * D:(b + 1) * D]
                        pe.matmul(to, agg[q.u][:, b * P:(b + 1) * P], wn_s[:, :], start=True, stop=False,
                                  skip_group_check=True)
                        last = pe.matmul(to, xt[q.u][:, b * P:(b + 1) * P], wsx_s[:, :], start=False,
                                         stop=True, skip_group_check=True)
                    last.then_inc(dense_done, 1)

                over_groups(pe, [(1, sums), (2, dense)])

            @block.scalar
            def _(act):
                def hold(q):
                    act.wait_ge(e.summed, q.t + 1)
                    if not is_first(q.t):
                        act.wait_ge(dense_done, q.t - 1)
                    act.activation(agg[q.u][:, :], bank[q.u][:, :], ACT.Copy)
                    act.activation(xt[q.u][:, :], bank[2 + q.u][:, :], ACT.Copy).then_inc(held, 1)

                def apply(q):
                    if not is_first(q.t):
                        act.wait_ge(stored[q.u], q.n * 16)
                    ln.normalise(act, q, xout[q.u], z[q.r])

                over_groups(act, [(0, lambda q: e.take_hi(act, q)), (1, hold),
                                  (4, lambda q: ln.root(act, q)), (5, apply)])

            @block.vector
            def _(dve):
                def add(q):
                    dve.wait_ge(dense_done, q.t + 1)
                    if not is_first(q.t, 4):
                        dve.wait_ge(ln.applied, q.t - 3)
                    dve.tensor_tensor(z[q.r][:, :], bank[4 + q.u][:, :],
                                      b3_r[:, :, :].rearrange("p b f -> p (b f)"), ALU.add)\
                       .then_inc(added, 1)
                    dve.wait_ge(added, q.t + 1)
                    ln.take_stats(dve, q, z[q.r])

                over_groups(dve, [(0, lambda q: e.prepare(dve, q)), (3, add),
                                  (4, lambda q: ln.invert(dve, q))])

    def fold_weights():
        with ExitStack() as ctx:
            ph = Phase(ctx, "fw")
            link = ph.sem("link")
            block = ctx.enter_context(nc.Block())

            @block.vector
            def _(dve):
                dve.tensor_tensor(brz_c[:, :], bih_c[:, 0:2], bhh_c[:, 0:2], ALU.add)
                dve.tensor_tensor(b3_r[:, :, :], b3_r[:, :, :], b3b_r[:, :, :], ALU.add)
                dve.tensor_scalar(wad_s[:, :], iota[:, 0:P], 0.0, wm_s[:, D + 1:D + 2], ALU.mult, ALU.add)
                dve.scalar_tensor_tensor(out=wsx_s[:, :], in0=wn_s[:, :], scalar=own[:, 0:1],
                                         in1=wsx_s[:, :], op0=ALU.mult, op1=ALU.add).then_inc(link, 1)
                dve.wait_ge(link, 1)
                dve.tensor_tensor(wsx_s[:, :], wsx_s[:, :], ident[:, :], ALU.add)

    def if_general(*parts):
        with nc.If(way["general"] == 1):
            for part, *args in parts:
                part(*args)

    way = {}
    with top:
        load_weights()
        sort_edges()
        way["general"] = nc.values_load(general[0:1, 0:1], min_val=0, max_val=1)
        way["rows"] = way["general"] * T
        fold_weights()
        count_degrees()
        if_general((general_sums, None, D, "ones"), (general_slots,))
        scale_degrees()
        scale_x()
        if_general((general_sums, t_x0, D))
        gcn_first()
        if_general((general_sums, t_h0, D))
        gcn_second()
        if_general((general_sums, t_x1, D))
        sage_first()
        if_general((general_sums, t_h, HID))
        sage_second()
        if_general((general_sums, t_v, D))
        sage_third()
        if_general((general_sums, t_m, MW, "messages"))
        attend()
        batch_constants()
        batch_normed()
        if_general((general_sums, t_x3, D))
        combine()


_INS = ["x", "src", "dst", "L0_gnn_W1", "L0_gnn_b1", "L0_gnn_W2", "L0_gnn_b2", "L1_gnn_ws0",
        "L1_gnn_wn0", "L1_gnn_b0", "L1_gnn_ws1", "L1_gnn_wn1", "L1_gnn_b1", "L1_gnn_ws2", "L1_gnn_wn2",
        "L1_gnn_b2", "L2_gnn_W_msg", "L2_gnn_b_msg", "L2_gnn_W_att", "L2_gnn_b_att", "L2_gnn_W_ih",
        "L2_gnn_b_ih", "L2_gnn_W_hh", "L2_gnn_b_hh", "L2_gnn_gamma", "L2_gnn_beta", "L3_gnn_W_neigh",
        "L3_gnn_b_neigh", "L3_gnn_W_self", "L3_gnn_b_self"]
_TURNED = {"L2_gnn_W_ih", "L2_gnn_W_hh", "L3_gnn_W_neigh", "L3_gnn_W_self"}


def kernel(**inputs):
    import numpy as _np
    import concourse.bacc as _bacc
    from concourse import mybir as _mybir
    from concourse.bass_utils import run_bass_kernel_spmd as _run

    nc = _bacc.Bacc("TRN2", target_bir_lowering=False, num_devices=1)
    arrays, args = {}, []
    for name in _INS:
        a = _np.asarray(inputs[name])
        a = _np.ascontiguousarray(a.T if name in _TURNED else a)
        arrays[f"in_{name}_dram"] = a
        args.append(nc.dram_tensor(f"in_{name}_dram", a.shape, _mybir.dt.from_np(a.dtype),
                                   kind="ExternalInput").ap())
    out = nc.dram_tensor("out_0_dram", (NODES, D), F32, kind="ExternalOutput").ap()
    build_program(nc, *args, out)
    r = _run(nc, [arrays], core_ids=[0])
    return r.results[0]["out_0_dram"]
```
